# Optimizing a Trainium2 kernel written in Bass

```python
import numpy as np
import jax
import jax.numpy as jnp

def _softmax(x, axis=-1):
    return jax.nn.softmax(x, axis=axis)
def _gelu(x):
    return jax.nn.gelu(x, approximate=True)
def _silu(x):
    return jax.nn.silu(x)
def _sigmoid(x):
    return jax.nn.sigmoid(x)
def _layernorm(x, axis=-1, eps=1e-5):
    m = jnp.mean(x, axis=axis, keepdims=True)
    v = jnp.var(x, axis=axis, keepdims=True)
    return (x - m) / jnp.sqrt(v + eps)
def _scatter_add(tgt, idx, src, axis=0):
    return tgt.at[idx].add(src)
def _segment_sum(src, seg, n):
    return jax.ops.segment_sum(src, seg, n)

kernel_name = 'mk_adj_ffn_d1_adj_256_b664ec'

def setup_inputs(seed: int = 0):
    np.random.seed(seed)
    _w = jnp.asarray
    def _rec_inputs():
        import jax
        import jax.numpy as jnp
        _gk = jax.random.key(seed)
        x = -0.000929 + 1 * jax.random.normal(jax.random.fold_in(_gk, 1), (3327, 256), jnp.float32)
        _a = jax.random.bernoulli(jax.random.fold_in(_gk, 2), 0.00120228, (3327, 3327))
        _a = jnp.logical_or(_a, jnp.eye(3327, dtype=bool))
        _af = _a.astype(jnp.float32)
        _af = _af * jax.random.uniform(jax.random.fold_in(_gk, 3), (3327, 3327), jnp.float32, 0.05, 1)
        adj = _af
        return x, adj
    x, adj = _rec_inputs()
    def _L0_gnn_setup():
        import jax, jax.numpy as jnp
        import numpy as np
        N = 4096
        IN = 256
        H = 8
        D = 32
        ALPHA = 0.2
        key = jax.random.key(seed)
        ks = jax.random.split(key, 9)
        xav = lambda k, sh: jax.random.normal(k, sh, jnp.float32) * np.float32(np.sqrt(2.0 / (sh[0] + sh[-1])))
        return {'x': jax.random.normal(ks[0], (N, IN), jnp.float32), 'adj_matrix': jax.random.uniform(ks[1], (N, N), jnp.float32), 'W': xav(ks[2], (H * D, IN)), 'We': xav(ks[3], (H, 1)), 'be': jnp.zeros((H,), jnp.float32), 'a_src': xav(ks[4], (H, D)), 'a_dst': xav(ks[5], (H, D)), 'Wr': xav(ks[6], (H * D, IN)), 'br': jnp.zeros((H * D,), jnp.float32)}
    _L0_gnn_all = _L0_gnn_setup()
    _L0_gnn_in = {k: v for k, v in _L0_gnn_all.items() if k in ('W', 'We', 'be', 'a_src', 'a_dst', 'Wr', 'br', )}
    del _L0_gnn_all

    def _L0_ffn_setup():
        import jax, jax.numpy as jnp
        import numpy as np
        B, T, C = (64, 384, 256)
        NH, NKV = (4, 2)
        HD = C // NH
        NREP = NH // NKV
        NE, TOPK = (8, 2)
        HID = int(8 / 3 * C)
        EPS_RMS = 1e-06

        def _rope_tables(t_len):
            inv_freq = 1.0 / 10000.0 ** (np.arange(0, HD, 2, dtype=np.float32) / HD)
            t = np.arange(t_len, dtype=np.float32)
            freqs = np.outer(t, inv_freq)
            emb = np.concatenate([freqs, freqs], axis=-1)
            return (jnp.asarray(np.cos(emb)), jnp.asarray(np.sin(emb)))

        def _rotate_half(x):
            h = x.shape[-1] // 2
            return jnp.concatenate([-x[..., h:], x[..., :h]], axis=-1)

        def _rmsnorm(v, w):
            return v * jax.lax.rsqrt(jnp.mean(v * v, axis=-1, keepdims=True) + EPS_RMS) * w
        key = jax.random.key(seed)
        ks = jax.random.split(key, 10)
        s = lambda k, shape: jax.random.normal(k, shape, jnp.float32) * 0.02
        return {'x': jax.random.normal(ks[0], (B, T, C), jnp.float32), 'ln1_w': jnp.ones((C,), jnp.float32), 'ln2_w': jnp.ones((C,), jnp.float32), 'wq': s(ks[1], (NH * HD, C)), 'wk': s(ks[2], (NKV * HD, C)), 'wv': s(ks[3], (NKV * HD, C)), 'wo': s(ks[4], (C, C)), 'router_w': s(ks[5], (NE, C)), 'w1': s(ks[6], (NE, HID, C)), 'w2': s(ks[7], (NE, C, HID)), 'w3': s(ks[8], (NE, HID, C))}
    _L0_ffn_all = _L0_ffn_setup()
    _L0_ffn_in = {k: v for k, v in _L0_ffn_all.items() if k in ('ln1_w', 'ln2_w', 'wq', 'wk', 'wv', 'wo', 'router_w', 'w1', 'w2', 'w3', )}
    del _L0_ffn_all

    return {
        "x": x,
        "adj": adj,
        "L0_gnn_W": _L0_gnn_in["W"],
        "L0_gnn_We": _L0_gnn_in["We"],
        "L0_gnn_be": _L0_gnn_in["be"],
        "L0_gnn_a_src": _L0_gnn_in["a_src"],
        "L0_gnn_a_dst": _L0_gnn_in["a_dst"],
        "L0_gnn_Wr": _L0_gnn_in["Wr"],
        "L0_gnn_br": _L0_gnn_in["br"],
        "L0_ffn_ln1_w": _L0_ffn_in["ln1_w"],
        "L0_ffn_ln2_w": _L0_ffn_in["ln2_w"],
        "L0_ffn_wq": _L0_ffn_in["wq"],
        "L0_ffn_wk": _L0_ffn_in["wk"],
        "L0_ffn_wv": _L0_ffn_in["wv"],
        "L0_ffn_wo": _L0_ffn_in["wo"],
        "L0_ffn_router_w": _L0_ffn_in["router_w"],
        "L0_ffn_w1": _L0_ffn_in["w1"],
        "L0_ffn_w2": _L0_ffn_in["w2"],
        "L0_ffn_w3": _L0_ffn_in["w3"],
    }

def reference(x, adj, L0_gnn_W, L0_gnn_We, L0_gnn_be, L0_gnn_a_src, L0_gnn_a_dst, L0_gnn_Wr, L0_gnn_br, L0_ffn_ln1_w, L0_ffn_ln2_w, L0_ffn_wq, L0_ffn_wk, L0_ffn_wv, L0_ffn_wo, L0_ffn_router_w, L0_ffn_w1, L0_ffn_w2, L0_ffn_w3):
    import jax
    import jax.numpy as jnp
    def _L0_gnn_ref(x, adj_matrix, W, We, be, a_src, a_dst, Wr, br):
        import jax, jax.numpy as jnp
        import numpy as np
        N = 4096
        IN = 256
        H = 8
        D = 32
        ALPHA = 0.2
        n = x.shape[0]
        h = (x @ W.T).reshape(n, H, D)
        s_src = jnp.einsum('nhd,hd->nh', h, a_src)
        s_dst = jnp.einsum('nhd,hd->nh', h, a_dst)
        attn = s_src[:, None, :] + s_dst[None, :, :]
        attn = attn + adj_matrix[:, :, None] * We[:, 0] + be
        mask = (adj_matrix > 0)[:, :, None]
        attn = jnp.where(mask, attn, -jnp.inf)
        attn = jax.nn.leaky_relu(attn, ALPHA)
        attn = jax.nn.softmax(attn, axis=1)
        h_out = jnp.einsum('ijh,jhd->ihd', attn, h).reshape(n, H * D)
        return h_out + x @ Wr.T + br

    def _L0_ffn_ref(x, ln1_w, ln2_w, wq, wk, wv, wo, router_w, w1, w2, w3):
        import jax, jax.numpy as jnp
        import numpy as np
        B, T, C = (64, 384, 256)
        NH, NKV = (4, 2)
        HD = C // NH
        NREP = NH // NKV
        NE, TOPK = (8, 2)
        HID = int(8 / 3 * C)
        EPS_RMS = 1e-06

        def _rope_tables(t_len):
            inv_freq = 1.0 / 10000.0 ** (np.arange(0, HD, 2, dtype=np.float32) / HD)
            t = np.arange(t_len, dtype=np.float32)
            freqs = np.outer(t, inv_freq)
            emb = np.concatenate([freqs, freqs], axis=-1)
            return (jnp.asarray(np.cos(emb)), jnp.asarray(np.sin(emb)))

        def _rotate_half(x):
            h = x.shape[-1] // 2
            return jnp.concatenate([-x[..., h:], x[..., :h]], axis=-1)

        def _rmsnorm(v, w):
            return v * jax.lax.rsqrt(jnp.mean(v * v, axis=-1, keepdims=True) + EPS_RMS) * w
        Bx, Tx, Cx = x.shape
        h = _rmsnorm(x, ln1_w)
        q = (h @ wq.T).reshape(Bx, Tx, NH, HD).transpose(0, 2, 1, 3)
        k = (h @ wk.T).reshape(Bx, Tx, NKV, HD).transpose(0, 2, 1, 3)
        v = (h @ wv.T).reshape(Bx, Tx, NKV, HD).transpose(0, 2, 1, 3)
        cos, sin = _rope_tables(Tx)
        cos, sin = (cos[None, None], sin[None, None])
        q = q * cos + _rotate_half(q) * sin
        k = k * cos + _rotate_half(k) * sin
        k = jnp.repeat(k, NREP, axis=1)
        v = jnp.repeat(v, NREP, axis=1)
        scores = jnp.einsum('bhtd,bhsd->bhts', q, k) / jnp.sqrt(jnp.float32(HD))
        causal = jnp.tril(jnp.ones((Tx, Tx), dtype=bool))
        scores = jnp.where(causal[None, None], scores, jnp.float32(-1e+30))
        att = jax.nn.softmax(scores, axis=-1)
        y = jnp.einsum('bhts,bhsd->bhtd', att, v).transpose(0, 2, 1, 3).reshape(Bx, Tx, Cx)
        x = x + y @ wo.T
        flat = _rmsnorm(x, ln2_w).reshape(-1, Cx)
        probs = jax.nn.softmax(flat @ router_w.T, axis=-1)
        tp, ti = jax.lax.top_k(probs, TOPK)
        tp = tp / (jnp.sum(tp, axis=-1, keepdims=True) + 1e-09)
        weights = jnp.sum(tp[..., None] * jax.nn.one_hot(ti, NE, dtype=flat.dtype), axis=1)
        out = jnp.zeros_like(flat)
        for e in range(NE):
            hh = jax.nn.silu(flat @ w1[e].T) * (flat @ w3[e].T)
            out = out + weights[:, e:e + 1] * (hh @ w2[e].T)
        return x + out.reshape(Bx, Tx, Cx)

    x = x + _L0_gnn_ref(_layernorm(x, axis=-1), adj, L0_gnn_W, L0_gnn_We, L0_gnn_be, L0_gnn_a_src, L0_gnn_a_dst, L0_gnn_Wr, L0_gnn_br)
    x = x + _L0_ffn_ref((_layernorm(x, axis=-1))[None], L0_ffn_ln1_w, L0_ffn_ln2_w, L0_ffn_wq, L0_ffn_wk, L0_ffn_wv, L0_ffn_wo, L0_ffn_router_w, L0_ffn_w1, L0_ffn_w2, L0_ffn_w3)[0]
    return x


_drawn_inputs = setup_inputs


def setup_inputs(seed=0):
    import zlib

    import numpy as np

    out = dict(_drawn_inputs(seed))
    spreads = {'L0_gnn_be': (0.0, 0.8),
     'L0_gnn_br': (0.0, 0.1),
     'L0_ffn_ln1_w': (1.0, 0.6),
     'L0_ffn_ln2_w': (1.0, 0.6)}
    factors = {'L0_ffn_wq': 8.0,
     'L0_ffn_wk': 8.0,
     'L0_ffn_wv': 8.0,
     'L0_ffn_wo': 8.0,
     'L0_ffn_router_w': 7.317,
     'L0_ffn_w1': 6.578,
     'L0_ffn_w2': 6.497,
     'L0_ffn_w3': 6.47}
    for name, (base, spread) in spreads.items():
        noise = np.random.default_rng([zlib.crc32(name.encode()), seed]).standard_normal(out[name].shape)
        drawn = base * np.exp(spread * noise) if base else spread * noise
        out[name] = jnp.asarray(drawn.astype(out[name].dtype))
    for name, factor in factors.items():
        out[name] = (out[name] * factor).astype(out[name].dtype)
    return out
```

```python
from contextlib import ExitStack

import numpy as np

import concourse.bass as bass
from concourse import mybir

F32 = mybir.dt.float32
U32 = mybir.dt.uint32
I32 = mybir.dt.int32
ALU = mybir.AluOpType
ACT = mybir.ActivationFunctionType
AX_X = mybir.AxisListType.X

P = 128
N = 3327
NT = -(-N // P)
NP = NT * P
C = 256
KC = C // P
GH, GD = 8, 32
ROW = C + GH
Q4 = 4
QW = NP // Q4
SLOTS = 16
CAND = Q4 * 8
EPS = 1e-5
ROUNDS = NP // 8
FAR = float(2 ** 20)
LOW = -1e30
HD = 64
NQK = 6
QKV = (NQK + 2) * HD
SCALE = HD ** -0.5
EPS_RMS = 1e-6
NE = 8
HID = 682
HH = HID // 2
KH = -(-HID // P)
LIST = (2 * NP + NE * (P - 1)) // P + (2 * NP + NE * (P - 1)) // P % 2
ZW = LIST * C // 16


def spread(nc, link, stats, mean, diff, var, done):
    m0, v0, m1, v1 = (stats[:, :, k] for k in (1, 2, 4, 5))
    link(nc.vector.tensor_tensor(mean, m0, m1, ALU.add))
    link(nc.vector.tensor_scalar(mean, mean, 0.5, None, ALU.mult))
    link(nc.vector.tensor_tensor(diff, m0, m1, ALU.subtract))
    link(nc.vector.scalar_tensor_tensor(diff, diff, 0.25, diff, ALU.mult, ALU.mult))
    link(nc.vector.tensor_tensor(var, v0, v1, ALU.add))
    link(nc.vector.scalar_tensor_tensor(var, var, 1.0 / C, diff, ALU.mult, ALU.add))
    nc.vector.tensor_scalar(var, var, EPS, None, ALU.add).then_inc(done, 1)


def prepare(nc, d, s):
    with ExitStack() as ctx:
        sb = lambda name, shape, dt=F32: ctx.enter_context(nc.sbuf_tensor(name, shape, dt))
        pb = lambda name, shape: ctx.enter_context(nc.psum_tensor(name, shape, F32))
        sem = lambda name: ctx.enter_context(nc.semaphore(name))

        wcat = sb("wcat", [P, KC, C + 2 * GH])
        wnat = sb("wnat", [P, KC, C])
        ablk = sb("ablk", [P, KC, 2 * GH])
        wrT = sb("wrT", [P, KC, C])
        brow = sb("brow", [1, C])
        ones = sb("ones", [1, P])
        be = sb("be", [P, GH])
        iota = sb("iota", [P, CAND])
        qoff = sb("qoff", [P, CAND])
        adj = [sb(f"adj{b}", [P, NP]) for b in range(2)]
        xn = [sb(f"xn{b}", [P, C]) for b in range(2)]
        xnT = sb("xnT", [P, KC, P])
        hs = [sb(f"hs{b}", [P, ROW]) for b in range(2)]
        stats = sb("stats", [P, NT, 6])
        mean = sb("mean", [P, NT])
        diff = sb("diff", [P, NT])
        var = sb("var", [P, NT])
        rstd = sb("rstd", [P, NT])
        cval = sb("cval", [P, CAND])
        cval2 = sb("cval2", [P, CAND])
        best = sb("best", [P, SLOTS])
        cidx = sb("cidx", [P, CAND], U32)
        cidf = sb("cidf", [P, CAND])
        pos = sb("pos", [P, SLOTS], U32)
        posf = sb("posf", [P, SLOTS])
        pick = sb("pick", [P, SLOTS, CAND])
        idf = sb("idf", [P, SLOTS])
        gone = sb("gone", [P, SLOTS])
        over = sb("over", [P, NT, Q4 + 1])
        overm = sb("overm", [P, 1])
        overall = sb("overall", [P, 1])
        psT, psH, psR, psW = (pb(n, [P, 512]) for n in ("psT", "psH", "psR", "psW"))
        psT, psH, psR = psT[:, 0:C], psH[:, 0:C + 2 * GH], psR[:, 0:C]
        psW = psW[:, 0:KC * 2 * GH].rearrange("p (k n) -> p k n", k=KC)

        weights_in = sem("weights_in")
        small_in = sem("small_in")
        x_in = sem("x_in")
        adj_in = [sem(f"adj_in{b}") for b in range(2)]
        table_out = [sem(f"table_out{b}") for b in range(2)]
        fold_ps = sem("fold_ps")
        fold_sb = sem("fold_sb")
        varred = sem("varred")
        rooted = sem("rooted")
        xn_ready = sem("xn_ready")
        xnT_ps = sem("xnT_ps")
        xnT_ready = sem("xnT_ready")
        proj = sem("proj")
        hs_ready = sem("hs_ready")
        resid = sem("resid")
        scanned = sem("scanned")
        step = sem("step")
        set_ones = sem("set_ones")
        xdone = sem("xdone")
        over_one = sem("over_one")
        over_all = sem("over_all")
        block = ctx.enter_context(nc.Block())

        @block.sync
        def _(sp):
            sp.dma_start(s.x1[:, 0:2, :], d.x[0:2 * P, :].rearrange("(t p) c -> p t c", p=P)).then_inc(x_in, 16)
            sp.dma_start(s.x1[:, 2:NT, :], d.x[2 * P:NP, :].rearrange("(t p) c -> p t c", p=P)).then_inc(x_in, 16)
            for b in range(2):
                sp.dma_start(adj[b][:, :], d.adj[b * P:(b + 1) * P, :]).then_inc(adj_in[b], 16)
            with sp.Fori(1, NT // 2) as i:
                for b in range(2):
                    sp.wait_ge(scanned, 2 * i + b - 1)
                    sp.dma_start(adj[b][:, :], d.adj[bass.ds(i * (2 * P) + b * P, P), :]).then_inc(adj_in[b], 16)

        @block.gpsimd
        def _(pool):
            pool.wait_ge(over_one, 1)
            nc.gpsimd.partition_all_reduce(overall[:, :], overm[:, :], P, bass.bass_isa.ReduceOp.max).then_inc(over_all, 1)

        @block.scalar
        def _(act):
            for dst, src in ((wnat, d.w), (wcat[:, :, 0:C], d.wT), (wrT, d.wrT)):
                act.dma_start(dst[:, :, :], src[:, :].rearrange("(k p) n -> p k n", p=P)).then_inc(weights_in, 16)
            act.dma_start(ablk[:, :, :], d.ablk[:, :].rearrange("(k p) n -> p k n", p=P)).then_inc(weights_in, 16)
            act.dma_start(s.ident[:, :], d.ident[:, :]).then_inc(weights_in, 16)
            act.dma_start(brow[:, :], d.br[:, :]).then_inc(weights_in, 16)
            act.dma_start(be[:, :], d.be[:, :]).then_inc(small_in, 16)
            act.dma_start(s.we[:, :], d.we[:, :]).then_inc(small_in, 16)
            act.dma_start(iota[:, :], d.iota[:, :]).then_inc(small_in, 16)
            act.dma_start(qoff[:, :], d.qoff[:, :]).then_inc(small_in, 16)
            act.wait_ge(fold_ps, 1)
            act.wait_ge(weights_in, 96)
            nc.scalar.activation(wcat[:, :, C:C + 2 * GH], psW[:, :, :], ACT.Copy).then_inc(fold_sb, 1)
            act.wait_ge(varred, 1)
            nc.scalar.activation(var[:, :], var[:, :], ACT.Sqrt).then_inc(rooted, 1)

            def tile(i, b):
                t = 2 * i + b
                act.wait_ge(xnT_ps, t + 1)
                nc.scalar.activation(xnT[:, :, :].rearrange("p k n -> p (k n)"), psT[:, :], ACT.Copy).then_inc(xnT_ready, 1)
                act.wait_ge(proj, t + 1)
                if not isinstance(i, int) or i >= 1:
                    act.wait_ge(table_out[b], 16 * i)
                nc.scalar.activation(hs[b][:, :], psH[:, 0:ROW], ACT.Copy).then_inc(hs_ready, 1)
                act.wait_ge(hs_ready, t + 1)
                act.dma_start(d.table[bass.ds(i * (2 * P) + b * P, P), :], hs[b][:, :]).then_inc(table_out[b], 16)

            for b in range(2):
                tile(0, b)
            with act.Fori(1, NT // 2) as i:
                for b in range(2):
                    tile(i, b)
            for b in range(2):
                act.wait_ge(table_out[b], 16 * (NT // 2))

        @block.tensor
        def _(pe):
            pe.wait_ge(weights_in, 96)
            for k in range(KC):
                for o in range(KC):
                    last = nc.tensor.matmul(psW[:, k, :], wnat[:, o, k * P:(k + 1) * P], ablk[:, o, :],
                                            start=(o == 0), stop=(o == KC - 1), skip_group_check=True)
            last.then_inc(fold_ps, 1)
            pe.wait_ge(fold_sb, 1)
            pe.wait_ge(set_ones, 1)

            def body(i, b):
                t = 2 * i + b
                pe.wait_ge(xn_ready, t + 1)
                if not (isinstance(t, int) and t == 0):
                    pe.wait_ge(xnT_ready, t)
                for k in range(KC):
                    last = nc.tensor.transpose(psT[:, k * P:(k + 1) * P], xn[b][:, k * P:(k + 1) * P], s.ident[:, :])
                last.then_inc(xnT_ps, 1)
                pe.wait_ge(xnT_ready, t + 1)
                if not (isinstance(t, int) and t == 0):
                    pe.wait_ge(hs_ready, t)
                    pe.wait_ge(resid, t)
                for k in range(KC):
                    nc.tensor.matmul(psH[:, :], xnT[:, k, :], wcat[:, k, :], start=(k == 0), stop=(k == KC - 1))
                for k in range(KC):
                    nc.tensor.matmul(psR[:, :], xnT[:, k, :], wrT[:, k, :], start=(k == 0), stop=False)
                nc.tensor.matmul(psR[:, :], ones[:, :], brow[:, :], start=False, stop=True).then_inc(proj, 1)

            for b in range(2):
                body(0, b)
            with pe.Fori(1, NT // 2) as i:
                for b in range(2):
                    body(i, b)

        @block.vector
        def _(dve):
            nc.vector.memset(ones[:, :], 1.0).then_inc(set_ones, 1)
            at = [0]

            def link(ins):
                at[0] += 1
                ins.then_inc(step, 1)
                dve.wait_ge(step, at[0])

            dve.wait_ge(x_in, 32)
            with dve.Fori(0, NT) as t:
                nc.vector.bn_stats(stats[:, t, :], s.x1[:, t, :]).then_inc(step, 1)
            at[0] += NT
            dve.wait_ge(step, at[0])
            spread(nc, link, stats, mean[:, :], diff[:, :], var[:, :], varred)
            dve.wait_ge(rooted, 1)
            link(nc.vector.reciprocal(rstd[:, :], var[:, :]))
            dve.wait_ge(small_in, 64)
            base = at[0]
            PER = 17

            def body(i, b):
                t = 2 * i + b
                now = [0]
                if not (isinstance(t, int) and t == 0):
                    dve.wait_ge(resid, t)

                def chain(ins, wait=True):
                    now[0] += 1
                    ins.then_inc(step, 1)
                    if wait:
                        dve.wait_ge(step, base + PER * t + now[0])

                if not (isinstance(i, int) and i == 0):
                    dve.wait_ge(xnT_ps, t - 1)
                dve.wait_ge(adj_in[b], 16 * (i + 1))
                nc.vector.tensor_scalar(xn[b][:, :], s.x1[:, t, :], mean[:, bass.ds(t, 1)], rstd[:, bass.ds(t, 1)],
                                        ALU.subtract, ALU.mult).then_inc(xn_ready, 1)
                for q in range(Q4):
                    chain(nc.vector.max(cval[:, 8 * q:8 * q + 8], adj[b][:, q * QW:(q + 1) * QW]), False)
                dve.wait_ge(step, base + PER * t + now[0])
                nc.vector.tensor_copy(over[:, t, 0:Q4], cval[:, :].rearrange("p (q e) -> p q e", e=8)[:, :, 7])
                for q in range(Q4):
                    ins = nc.vector.max_index(cidx[:, 8 * q:8 * q + 8], cval[:, 8 * q:8 * q + 8], adj[b][:, q * QW:(q + 1) * QW])
                ins.then_inc(scanned, 1)
                chain(nc.vector.max(best[:, 0:8], cval[:, :]))
                chain(nc.vector.tensor_copy(s.vals[:, t, 0:8], best[:, 0:8]), False)
                chain(nc.vector.match_replace(cval2[:, :], best[:, 0:8], cval[:, :], -3e38), False)
                chain(nc.vector.max_index(pos[:, 0:8], best[:, 0:8], cval[:, :]))
                chain(nc.vector.tensor_copy(posf[:, 0:8], pos[:, 0:8]), False)
                chain(nc.vector.max(best[:, 8:16], cval2[:, :]))
                chain(nc.vector.tensor_copy(s.vals[:, t, 8:16], best[:, 8:16]), False)
                chain(nc.vector.max_index(pos[:, 8:16], best[:, 8:16], cval2[:, :]))
                chain(nc.vector.tensor_copy(posf[:, 8:16], pos[:, 8:16]), False)
                chain(nc.vector.tensor_tensor(cidf[:, :], cidx[:, :], qoff[:, :], ALU.add))
                chain(nc.vector.tensor_tensor(pick[:, :, :], iota[:, :].unsqueeze(1).to_broadcast([P, SLOTS, CAND]),
                                              posf[:, :].unsqueeze(2).to_broadcast([P, SLOTS, CAND]), ALU.is_equal))
                chain(nc.vector.tensor_tensor(pick[:, :, :], pick[:, :, :],
                                              cidf[:, :].unsqueeze(1).to_broadcast([P, SLOTS, CAND]), ALU.mult))
                chain(nc.vector.tensor_reduce(idf[:, :], pick[:, :, :], AX_X, ALU.add))
                nc.vector.tensor_scalar(gone[:, :], s.vals[:, t, :], 0.0, FAR, ALU.is_le, ALU.mult).then_inc(xdone, 1)
                dve.wait_ge(xdone, t + 1)
                nc.vector.tensor_tensor(s.cols[:, t, :], idf[:, :], gone[:, :], ALU.add)
                nc.vector.tensor_copy(over[:, t, Q4:Q4 + 1], best[:, SLOTS - 1:SLOTS])
                dve.wait_ge(proj, t + 1)
                nc.vector.tensor_tensor(s.x1[:, t, :], s.x1[:, t, :], psR[:, :], ALU.add)
                dve.wait_ge(hs_ready, t + 1)
                nc.vector.tensor_tensor(s.ssrc[:, t, :], psH[:, ROW:ROW + GH], be[:, :], ALU.add).then_inc(resid, 1)
                assert now[0] == PER, now

            for b in range(2):
                body(0, b)
            with dve.Fori(1, NT // 2) as i:
                for b in range(2):
                    body(i, b)
            dve.wait_ge(resid, NT)
            nc.vector.tensor_reduce(overm[:, :], over[:, :, :].rearrange("p t q -> p (t q)"), AX_X, ALU.max).then_inc(over_one, 1)
            dve.wait_ge(over_all, 1)
            nc.vector.tensor_scalar(s.crowded[:, :], overall[:, :], 0.0, None, ALU.is_gt)


def build_crowded(s):
    def crowded(eng):
        return eng.value_load(s.crowded[0:1, 0:1], min_val=0, max_val=1)
    return crowded


def graph(nc, d, s):
    with ExitStack() as ctx:
        sb = lambda name, shape, dt=F32: ctx.enter_context(nc.sbuf_tensor(name, shape, dt))
        sem = lambda name: ctx.enter_context(nc.semaphore(name))
        rows = [sb(f"rows{b}", [P, SLOTS, ROW]) for b in range(2)]
        cols = [sb(f"cols{b}", [P, SLOTS], U32) for b in range(2)]
        z = [sb(f"z{b}", [P, SLOTS, GH]) for b in range(2)]
        vw = sb("vw", [P, SLOTS, GH])
        there = sb("there", [P, SLOTS])
        low = sb("low", [P, SLOTS])
        top = sb("top", [P, GH])
        total = sb("total", [P, GH])
        acc = sb("acc", [P, C])
        crowded = build_crowded(s)
        cleared = sem("cleared")
        turn = sem("turn")
        named = sem("named")
        gathered = [sem(f"gathered{b}") for b in range(2)]
        scored = sem("scored")
        raised = sem("raised")
        summed = sem("summed")
        step = sem("gstep")
        block = ctx.enter_context(nc.Block())

        @block.gpsimd
        def _(pool):
            with pool.If(crowded(pool) < 1):
                pool.wait_ge(cleared, 2)

                def body(i, b):
                    t = 2 * i + b
                    if not (isinstance(i, int) and i == 0):
                        pool.wait_ge(summed, t - 1)
                        pool.sem_inc(turn, 1)
                    nc.gpsimd.tensor_copy(cols[b][:, :], s.cols[:, t, :]).then_inc(named, 1)
                    pool.wait_ge(named, t + 1)
                    pool.sem_inc(turn, 1)
                    for k in range(SLOTS):
                        pool.indirect_dma_start(rows[b][:, k, :], None, d.table[:, :],
                                                bass.IndirectOffsetOnAxis(cols[b][:, k:k + 1], 0),
                                                bounds_check=NP - 1, oob_is_err=False).then_inc(gathered[b], 16)

                for b in range(2):
                    body(0, b)
                with pool.Fori(1, NT // 2) as i:
                    for b in range(2):
                        body(i, b)

        @block.scalar
        def _(act):
            with act.If(crowded(act) < 1):
                with act.Fori(0, NT // 2) as i:
                    for b in range(2):
                        act.wait_ge(scored, 2 * i + b + 1)
                        nc.scalar.activation(z[b][:, :, :], z[b][:, :, :], ACT.Exp).then_inc(raised, 1)

        @block.vector
        def _(dve):
            with dve.If(crowded(dve) < 1):
                for b in range(2):
                    nc.vector.memset(rows[b][:, :, :], 0.0).then_inc(cleared, 1)
                PER = 14
                with dve.Fori(0, NT // 2) as i:
                    for b in range(2):
                        t = 2 * i + b
                        now = [0]

                        def chain(ins):
                            now[0] += 1
                            ins.then_inc(step, 1)
                            dve.wait_ge(step, PER * t + now[0])

                        h = rows[b][:, :, 0:C]
                        zh = z[b][:, :, :].rearrange("p s h -> p h s")
                        each = lambda a: a.unsqueeze(1).to_broadcast([P, SLOTS, GH])
                        slot = lambda a: a.unsqueeze(2).to_broadcast([P, SLOTS, GH])
                        chain(nc.vector.tensor_tensor(vw[:, :, :], slot(s.vals[:, t, :]), each(s.we[:, :]), ALU.mult))
                        chain(nc.vector.tensor_scalar(low[:, :], s.vals[:, t, :], 0.0, LOW, ALU.is_le, ALU.mult))
                        chain(nc.vector.tensor_scalar(there[:, :], s.vals[:, t, :], 0.0, None, ALU.is_gt))
                        dve.wait_ge(gathered[b], 16 * SLOTS * (i + 1))
                        chain(nc.vector.tensor_tensor(z[b][:, :, :], rows[b][:, :, C:ROW], each(s.ssrc[:, t, :]), ALU.add))
                        chain(nc.vector.tensor_tensor(z[b][:, :, :], z[b][:, :, :], vw[:, :, :], ALU.add))
                        chain(nc.vector.scalar_tensor_tensor(z[b][:, :, :], z[b][:, :, :], 0.2, z[b][:, :, :], ALU.mult, ALU.max))
                        chain(nc.vector.tensor_tensor(z[b][:, :, :], z[b][:, :, :], slot(low[:, :]), ALU.add))
                        chain(nc.vector.tensor_reduce(top[:, :], zh, AX_X, ALU.max))
                        nc.vector.tensor_tensor(z[b][:, :, :], z[b][:, :, :], each(top[:, :]), ALU.subtract).then_inc(scored, 1)
                        dve.wait_ge(raised, t + 1)
                        chain(nc.vector.tensor_tensor(z[b][:, :, :], z[b][:, :, :], slot(there[:, :]), ALU.mult))
                        chain(nc.vector.tensor_reduce(total[:, :], zh, AX_X, ALU.add))
                        chain(nc.vector.reciprocal(total[:, :], total[:, :]))
                        chain(nc.vector.tensor_tensor(z[b][:, :, :], z[b][:, :, :], each(total[:, :]), ALU.mult))
                        chain(nc.vector.tensor_tensor(h.rearrange("p s (h d) -> p s h d", d=GD), h.rearrange("p s (h d) -> p s h d", d=GD),
                                                      z[b][:, :, :].unsqueeze(3).to_broadcast([P, SLOTS, GH, GD]), ALU.mult))
                        chain(nc.vector.tensor_reduce(acc[:, :], h.rearrange("p s c -> p c s"), AX_X, ALU.add))
                        nc.vector.tensor_tensor(s.x1[:, t, :], s.x1[:, t, :], acc[:, :], ALU.add).then_inc(summed, 1)
                        assert now[0] == PER, now


def general(nc, d, s):
    with ExitStack() as ctx:
        sb = lambda name, shape, dt=F32: ctx.enter_context(nc.sbuf_tensor(name, shape, dt))
        sem = lambda name: ctx.enter_context(nc.semaphore(name))
        row = sb("grow", [P, NP])
        rows = sb("grows", [P, 8, ROW])
        best = sb("gbest", [P, 8])
        found = sb("gfound", [P, 8], U32)
        foundf = sb("gfoundf", [P, 8])
        cols = sb("gcols", [P, 8], U32)
        low, there = sb("glow", [P, 8]), sb("gthere", [P, 8])
        z = sb("gz", [P, 9, GH])
        peak, newpeak, total, part = (sb(n, [P, GH]) for n in ("gpeak", "gnewpeak", "gtotal", "gpart"))
        acc, add = sb("gacc", [P, C]), sb("gadd", [P, C])
        row_in = sem("grow_in")
        crowded = build_crowded(s)
        found_ready = sem("gfound_ready")
        tick = sem("gtick")
        ptick = sem("gptick")
        gathered = sem("ggathered")
        scored = sem("gscored")
        raised = sem("graised")
        tiled = sem("gtiled")
        step = sem("ggstep")
        block = ctx.enter_context(nc.Block())

        @block.sync
        def _(sp):
            with sp.If(crowded(sp) > 0):
                with sp.Fori(0, NT) as t:
                    sp.wait_ge(tiled, t + 1)
                    sp.dma_start(row[:, :], d.adj[bass.ds(t * P, P), :]).then_inc(row_in, 16)

        @block.gpsimd
        def _(pool):
            with pool.If(crowded(pool) > 0):
                with pool.Fori(0, NT * ROUNDS) as n:
                    pool.wait_ge(found_ready, n + 1)
                    pool.sem_inc(ptick, 1)
                    for k in range(8):
                        pool.indirect_dma_start(rows[:, k, :], None, d.table[:, :],
                                                bass.IndirectOffsetOnAxis(cols[:, k:k + 1], 0),
                                                bounds_check=NP - 1, oob_is_err=False).then_inc(gathered, 16)

        @block.scalar
        def _(act):
            with act.If(crowded(act) > 0):
                with act.Fori(0, NT * ROUNDS) as n:
                    act.wait_ge(scored, n + 1)
                    nc.scalar.activation(z[:, :, :], z[:, :, :], ACT.Exp).then_inc(raised, 1)

        @block.vector
        def _(dve):
            with dve.If(crowded(dve) > 0):
                nc.vector.memset(rows[:, :, :], 0.0).then_inc(tiled, 1)
                PER, TILE = 24, 5
                with dve.Fori(0, NT) as t:
                    def link(k, ins):
                        ins.then_inc(step, 1)
                        dve.wait_ge(step, t * (PER * ROUNDS + TILE) + (PER * ROUNDS if k > 3 else 0) + k)

                    dve.wait_ge(tiled, t + 1)
                    link(1, nc.vector.memset(peak[:, :], LOW))
                    link(2, nc.vector.memset(total[:, :], 0.0))
                    link(3, nc.vector.memset(acc[:, :], 0.0))
                    dve.wait_ge(row_in, 16 * (t + 1))
                    dve.sem_inc(tick, 1)
                    with dve.Fori(0, ROUNDS) as r:
                        now = [0]

                        def chain(ins):
                            now[0] += 1
                            ins.then_inc(step, 1)
                            dve.wait_ge(step, t * (PER * ROUNDS + TILE) + 3 + PER * r + now[0])
                            dve.sem_inc(tick, 1)

                        n = t * ROUNDS + r
                        zs = z[:, 0:8, :]
                        zh = zs.rearrange("p s h -> p h s")
                        h = rows[:, :, 0:C]
                        each = lambda a: a.unsqueeze(1).to_broadcast([P, 8, GH])
                        slot = lambda a: a.unsqueeze(2).to_broadcast([P, 8, GH])
                        chain(nc.vector.max(best[:, :], row[:, :]))
                        chain(nc.vector.max_index(found[:, :], best[:, :], row[:, :]))
                        chain(nc.vector.match_replace(row[:, :], best[:, :], row[:, :], -3e38))
                        chain(nc.vector.tensor_scalar(low[:, :], best[:, :], 0.0, FAR, ALU.is_le, ALU.mult))
                        chain(nc.vector.tensor_copy(foundf[:, :], found[:, :]))
                        nc.vector.tensor_tensor(cols[:, :], foundf[:, :], low[:, :], ALU.add).then_inc(found_ready, 1)
                        dve.wait_ge(found_ready, n + 1)
                        chain(nc.vector.tensor_scalar(low[:, :], best[:, :], 0.0, LOW, ALU.is_le, ALU.mult))
                        chain(nc.vector.tensor_scalar(there[:, :], best[:, :], 0.0, None, ALU.is_gt))
                        chain(nc.vector.tensor_tensor(zs, slot(best[:, :]), each(s.we[:, :]), ALU.mult))
                        dve.wait_ge(gathered, 128 * (n + 1))
                        chain(nc.vector.tensor_tensor(rows[:, :, C:ROW], rows[:, :, C:ROW], each(s.ssrc[:, t, :]), ALU.add))
                        chain(nc.vector.tensor_tensor(zs, zs, rows[:, :, C:ROW], ALU.add))
                        chain(nc.vector.scalar_tensor_tensor(zs, zs, 0.2, zs, ALU.mult, ALU.max))
                        chain(nc.vector.tensor_tensor(zs, zs, slot(low[:, :]), ALU.add))
                        chain(nc.vector.tensor_reduce(newpeak[:, :], zh, AX_X, ALU.max))
                        chain(nc.vector.tensor_tensor(newpeak[:, :], newpeak[:, :], peak[:, :], ALU.max))
                        chain(nc.vector.tensor_tensor(zs, zs, each(newpeak[:, :]), ALU.subtract))
                        nc.vector.tensor_tensor(z[:, 8, :], peak[:, :], newpeak[:, :], ALU.subtract).then_inc(scored, 1)
                        dve.wait_ge(raised, n + 1)
                        chain(nc.vector.tensor_copy(peak[:, :], newpeak[:, :]))
                        chain(nc.vector.tensor_tensor(zs, zs, slot(there[:, :]), ALU.mult))
                        chain(nc.vector.tensor_reduce(part[:, :], zh, AX_X, ALU.add))
                        chain(nc.vector.tensor_tensor(total[:, :], total[:, :], z[:, 8, :], ALU.mult))
                        chain(nc.vector.tensor_tensor(total[:, :], total[:, :], part[:, :], ALU.add))
                        chain(nc.vector.tensor_tensor(h.rearrange("p s (h d) -> p s h d", d=GD), h.rearrange("p s (h d) -> p s h d", d=GD),
                                                      zs.unsqueeze(3).to_broadcast([P, 8, GH, GD]), ALU.mult))
                        ac = acc[:, :].rearrange("p (h d) -> p h d", d=GD)
                        chain(nc.vector.tensor_tensor(ac, ac, z[:, 8, :].unsqueeze(2).to_broadcast([P, GH, GD]), ALU.mult))
                        chain(nc.vector.tensor_reduce(add[:, :], h.rearrange("p s c -> p c s"), AX_X, ALU.add))
                        chain(nc.vector.tensor_tensor(acc[:, :], acc[:, :], add[:, :], ALU.add))
                        assert now[0] == PER, now
                    link(4, nc.vector.reciprocal(total[:, :], total[:, :]))
                    ac = acc[:, :].rearrange("p (h d) -> p h d", d=GD)
                    link(5, nc.vector.tensor_tensor(ac, ac, total[:, :].unsqueeze(2).to_broadcast([P, GH, GD]), ALU.mult))
                    nc.vector.tensor_tensor(s.x1[:, t, :], s.x1[:, t, :], acc[:, :], ALU.add).then_inc(tiled, 1)


def qkv(nc, d, s):
    with ExitStack() as ctx:
        sb = lambda name, shape, dt=F32: ctx.enter_context(nc.sbuf_tensor(name, shape, dt))
        pb = lambda name: ctx.enter_context(nc.psum_tensor(name, [P, 512], F32))
        sem = lambda name: ctx.enter_context(nc.semaphore(name))
        wqkvT = sb("wqkvT", [P, KC, QKV])
        ln1 = sb("ln1", [P, C])
        cos = sb("cos", [P, NT, HD])
        sin = sb("sin", [P, NT, HD])
        stats = sb("qstats", [P, NT, 6])
        mean, diff, var, rstd, rrms = (sb(n, [P, NT]) for n in ("qmean", "qdiff", "qvar", "qrstd", "qrrms"))
        square = sb("square", [P, C])
        hn = [sb(f"hn{b}", [P, C]) for b in range(2)]
        hT = sb("hT", [P, KC, P])
        qk = [sb(f"qk{b}", [P, QKV]) for b in range(2)]
        rot = [sb(f"rot{b}", [P, NQK, HD]) for b in range(2)]
        cross = sb("cross", [P, NQK, HD])
        psT, psQ, psK = pb("qpsT"), pb("qpsQ"), pb("qpsK")
        consts_in = sem("consts_in")
        varred = sem("qvarred")
        rooted = sem("qrooted")
        normed = sem("normed")
        squared = sem("squared")
        meaned = sem("meaned")
        step = sem("qstep")
        hn_ready = sem("hn_ready")
        hT_ps = sem("hT_ps")
        hT_ready = sem("hT_ready")
        qkv_ps = sem("qkv_ps")
        qk_ready = sem("qk_ready")
        turned = sem("turned")
        qkT_ps = sem("qkT_ps")
        stored = sem("stored")
        block = ctx.enter_context(nc.Block())

        @block.sync
        def _(sp):
            sp.dma_start(wqkvT[:, :, :], d.wqkvT[:, :].rearrange("(k p) n -> p k n", p=P)).then_inc(consts_in, 16)
            sp.dma_start(ln1[:, :], d.ln1[:, :]).then_inc(consts_in, 16)
            sp.dma_start(cos[:, :, :], d.cos[:, :].rearrange("(t p) n -> p t n", p=P)).then_inc(consts_in, 16)
            sp.dma_start(sin[:, :, :], d.sin[:, :].rearrange("(t p) n -> p t n", p=P)).then_inc(consts_in, 16)

        @block.scalar
        def _(act):
            act.wait_ge(varred, 1)
            nc.scalar.activation(var[:, :], var[:, :], ACT.Sqrt).then_inc(rooted, 1)
            with act.Fori(0, NT) as t:
                act.wait_ge(normed, t + 1)
                nc.scalar.activation(square[:, :], s.x2[:, t, :], ACT.Square, accum_out=rrms[:, bass.ds(t, 1)]).then_inc(squared, 1)
                act.wait_ge(squared, t + 1)
            act.wait_ge(meaned, 1)
            nc.scalar.activation(rrms[:, :], rrms[:, :], ACT.Sqrt).then_inc(rooted, 1)

            def store(b, t):
                act.wait_ge(qkT_ps, t + 1)
                nc.scalar.activation(s.qT[:, :, bass.ds(t * P, P)], psK[:, 0:2 * P].rearrange("p (a n) -> p a n", a=2), ACT.Copy)
                nc.scalar.activation(s.kT[:, bass.ds(t * P, P)], psK[:, 2 * P:3 * P], ACT.Copy).then_inc(stored, 1)

            def body(i, b):
                t = 2 * i + b
                act.wait_ge(hT_ps, t + 1)
                nc.scalar.activation(hT[:, :, :].rearrange("p k n -> p (k n)"), psT[:, 0:C], ACT.Copy).then_inc(hT_ready, 1)
                if not (isinstance(t, int) and t == 0):
                    store(1 - b, t - 1)
                if not (isinstance(i, int) and i == 0):
                    act.wait_ge(turned, t - 1)
                act.wait_ge(qkv_ps, t + 1)
                nc.scalar.activation(qk[b][:, :], psQ[:, :], ACT.Copy).then_inc(qk_ready, 1)

            for b in range(2):
                body(0, b)
            with act.Fori(1, NT // 2) as i:
                for b in range(2):
                    body(i, b)
            store(1, NT - 1)

        @block.tensor
        def _(pe):
            pe.wait_ge(consts_in, 64)

            def turn(b, t):
                pe.wait_ge(turned, t + 1)
                if not (isinstance(t, int) and t == 0):
                    pe.wait_ge(stored, t)
                for k in range(3):
                    last = nc.tensor.transpose(psK[:, k * P:(k + 1) * P],
                                               rot[b][:, 2 * k:2 * k + 2, :].rearrange("p a n -> p (a n)"), s.ident[:, :])
                last.then_inc(qkT_ps, 1)

            def body(i, b):
                t = 2 * i + b
                first = isinstance(t, int) and t == 0
                pe.wait_ge(hn_ready, t + 1)
                for k in range(KC):
                    last = nc.tensor.transpose(psT[:, k * P:(k + 1) * P], hn[b][:, k * P:(k + 1) * P], s.ident[:, :])
                last.then_inc(hT_ps, 1)
                if not first:
                    turn(1 - b, t - 1)
                pe.wait_ge(hT_ready, t + 1)
                if not first:
                    pe.wait_ge(qk_ready, t)
                for k in range(KC):
                    last = nc.tensor.matmul(psQ[:, :], hT[:, k, :], wqkvT[:, k, :], start=(k == 0), stop=(k == KC - 1))
                last.then_inc(qkv_ps, 1)

            for b in range(2):
                body(0, b)
            with pe.Fori(1, NT // 2) as i:
                for b in range(2):
                    body(i, b)
            turn(1, NT - 1)

        @block.vector
        def _(dve):
            at = [0]

            def link(ins):
                at[0] += 1
                ins.then_inc(step, 1)
                dve.wait_ge(step, at[0])

            nc.vector.memset(s.v[:, :, :, HD:HD + 1], 1.0)
            with dve.Fori(0, NT) as t:
                nc.vector.bn_stats(stats[:, t, :], s.x1[:, t, :]).then_inc(step, 1)
            at[0] += NT
            dve.wait_ge(step, at[0])
            spread(nc, link, stats, mean[:, :], diff[:, :], var[:, :], varred)
            dve.wait_ge(rooted, 1)
            link(nc.vector.reciprocal(rstd[:, :], var[:, :]))
            with dve.Fori(0, NT) as t:
                nc.vector.tensor_scalar(s.x2[:, t, :], s.x1[:, t, :], mean[:, bass.ds(t, 1)], rstd[:, bass.ds(t, 1)],
                                        ALU.subtract, ALU.mult).then_inc(normed, 1)
            dve.wait_ge(squared, NT)
            nc.vector.tensor_scalar(rrms[:, :], rrms[:, :], 1.0 / C, EPS_RMS, ALU.mult, ALU.add).then_inc(meaned, 1)
            dve.wait_ge(rooted, 2)
            link(nc.vector.reciprocal(rrms[:, :], rrms[:, :]))
            dve.wait_ge(consts_in, 64)
            base = at[0]
            PER = 3

            def scale(i, b):
                t = 2 * i + b
                if not (isinstance(i, int) and i == 0):
                    dve.wait_ge(hT_ps, t - 1)
                nc.vector.scalar_tensor_tensor(hn[b][:, :], s.x2[:, t, :], rrms[:, bass.ds(t, 1)], ln1[:, :],
                                               ALU.mult, ALU.mult).then_inc(hn_ready, 1)

            def rope(i, b):
                t = 2 * i + b
                now = [0]

                def chain(ins, wait=True):
                    now[0] += 1
                    ins.then_inc(step, 1)
                    if wait:
                        dve.wait_ge(step, base + PER * t + now[0])

                dve.wait_ge(qk_ready, t + 1)
                if not (isinstance(i, int) and i == 0):
                    dve.wait_ge(qkT_ps, t - 1)
                src = qk[b][:, 0:NQK * HD].rearrange("p (a n) -> p a n", n=HD)
                half = HD // 2
                wide = lambda a, n: a.unsqueeze(1).to_broadcast([P, NQK, n])
                nc.vector.tensor_copy(s.v[:, t, :, 0:HD], qk[b][:, NQK * HD:QKV].rearrange("p (a n) -> p a n", n=HD))
                chain(nc.vector.tensor_tensor(rot[b][:, :, :], src, wide(cos[:, t, :], HD), ALU.mult), False)
                chain(nc.vector.tensor_tensor(cross[:, :, 0:half], src[:, :, half:HD], wide(sin[:, t, 0:half], half), ALU.mult), False)
                chain(nc.vector.tensor_tensor(cross[:, :, half:HD], src[:, :, 0:half], wide(sin[:, t, half:HD], half), ALU.mult))
                nc.vector.tensor_tensor(rot[b][:, :, :], rot[b][:, :, :], cross[:, :, :], ALU.add).then_inc(turned, 1)
                dve.wait_ge(turned, t + 1)
                assert now[0] == PER

            scale(0, 0)
            scale(0, 1)
            rope(0, 0)
            with dve.Fori(1, NT // 2) as i:
                scale(i, 0)
                rope(i - 1, 1)
                scale(i, 1)
                rope(i, 0)
            rope(NT // 2 - 1, 1)


def attend(nc, d, s):
    with ExitStack() as ctx:
        sb = lambda name, shape, dt=F32: ctx.enter_context(nc.sbuf_tensor(name, shape, dt))
        pb = lambda name: ctx.enter_context(nc.psum_tensor(name, [P, 512], F32))
        sem = lambda name: ctx.enter_context(nc.semaphore(name))
        FULL = (NT - 1) // 4
        mask = sb("mask", [P, P])
        woT = sb("woT", [P, KC, C])
        q = [[sb(f"q{j}{x}", [P, P]) for x in range(2)] for j in range(2)]
        own = [[sb(f"own{j}{x}", [P, 512]) for x in range(2)] for j in range(2)]
        past = [[sb(f"past{j}{x}", [P, FULL * 512]) for x in range(2)] for j in range(2)]
        high = [[sb(f"high{j}{x}", [P, 1]) for x in range(2)] for j in range(2)]
        bias = [[sb(f"bias{j}{x}", [P, 1]) for x in range(2)] for j in range(2)]
        p = [sb(f"p{x}", [P, 512]) for x in range(2)]
        pT = [sb(f"pT{x}", [P, 512]) for x in range(2)]
        part = [sb(f"part{x}", [P, 1]) for x in range(2)]
        y = [sb(f"y{j}", [P, C]) for j in range(2)]
        yT = sb("yT", [P, C])
        psS, psT, psO = ([pb(f"ps{n}{x}") for x in range(2)] for n in "STO")
        psY, psZ = pb("psY"), pb("psZ")
        consts_in = sem("aconsts_in")
        q_ready = sem("q_ready")
        s_ps = [sem(f"s_ps{x}") for x in range(2)]
        s_out = [sem(f"s_out{x}") for x in range(2)]
        high_ready = sem("high_ready")
        p_ready = [sem(f"p_ready{x}") for x in range(2)]
        t_ps = [sem(f"t_ps{x}") for x in range(2)]
        pT_ready = [sem(f"pT_ready{x}") for x in range(2)]
        pv = [sem(f"pv{x}") for x in range(2)]
        o_out = sem("o_out")
        yT_ps = sem("yT_ps")
        yT_ready = sem("yT_ready")
        z_ps = sem("z_ps")
        z_out = sem("z_out")
        step = sem("astep")
        own_step = sem("own_step")
        turn = sem("aturn")
        block = ctx.enter_context(nc.Block())
        BLOCKS = 4

        def upto(g, k):
            return 4 * g * (g + 1) + k * (g + 1)

        def groups(eng, body):
            body(0, 4)
            with eng.Fori(1, NT // 4) as g:
                body(g, 4)
            body(NT // 4, NT % 4)

        def chunks(eng, g, body):
            if not (isinstance(g, int) and g == 0):
                with eng.Fori(0, g) as c:
                    body(c)

        zero = lambda v: isinstance(v, int) and v == 0

        @block.sync
        def _(sp):
            sp.dma_start(mask[:, :], d.mask[:, :]).then_inc(consts_in, 16)
            sp.dma_start(woT[:, :, :], d.woT[:, :].rearrange("(k p) n -> p k n", p=P)).then_inc(consts_in, 16)

        @block.gpsimd
        def _(pool):
            for j in range(2):
                for x in range(2):
                    nc.gpsimd.memset(q[j][x][64 - 64 * x:128 - 64 * x, :], 0.0)
            def group(g, tiles):
                for k in range(2 * tiles):
                    if not (isinstance(g, int) and g == 0 and k < 2):
                        for x in range(2):
                            pool.wait_ge(s_ps[x], upto(g, max(k - 1, 0)))
                        pool.sem_inc(turn, 1)
                    for x in range(2):
                        r = slice(64 * x, 64 * x + 64)
                        nc.gpsimd.tensor_copy(q[k % 2][x][r, :], s.qT[r, k % 2, bass.ds(g * 512 + (k // 2) * P, P)]).then_inc(q_ready, 1)
            groups(pool, group)

        @block.tensor
        def _(pe):
            pe.wait_ge(consts_in, 32)

            def scores_own(g, k):
                pe.wait_ge(q_ready, 2 * (8 * g + k + 1))
                at = upto(g, k)
                w = (k // 2 + 1) * P
                for x in range(2):
                    if not zero(at):
                        pe.wait_ge(s_out[x], at)
                    nc.tensor.matmul(psS[x][:, 0:w], q[k % 2][x][:, :], s.kT[:, bass.ds(g * 512, w)],
                                     start=True, stop=True).then_inc(s_ps[x], 1)

            def score_full(g, k, c, x):
                pe.wait_ge(s_out[x], upto(g, k) + 1 + c)
                nc.tensor.matmul(psS[x][:, :], q[k % 2][x][:, :], s.kT[:, bass.ds(c * 512, 512)],
                                 start=True, stop=True).then_inc(s_ps[x], 1)

            def turn_p(x, n, blocks):
                pe.wait_ge(p_ready[x], n + 1)
                if not zero(n):
                    pe.wait_ge(pT_ready[x], n)
                for j in range(blocks):
                    last = nc.tensor.transpose(psT[x][:, j * P:(j + 1) * P], p[x][:, j * P:(j + 1) * P], s.ident[:, :])
                last.then_inc(t_ps[x], 1)

            def times_v(x, n, g, k, chunk, blocks, first):
                pe.wait_ge(pT_ready[x], n + 1)
                if first and not zero(8 * g + k):
                    pe.wait_ge(o_out, 8 * g + k)
                for j in range(blocks):
                    last = nc.tensor.matmul(psO[x][:, 0:HD + 1], pT[x][:, j * P:(j + 1) * P],
                                            s.v[:, bass.ds(chunk * 4 + j, 1), x, :].rearrange("p a n -> p (a n)"),
                                            start=(first and j == 0), stop=(first and j == blocks - 1), skip_group_check=True)
                last.then_inc(pv[x], 1)

            def turn_y(tile, j):
                pe.wait_ge(o_out, 2 * tile + 2)
                if not zero(tile):
                    pe.wait_ge(yT_ready, tile)
                for k in range(KC):
                    last = nc.tensor.transpose(psY[:, k * P:(k + 1) * P], y[j][:, k * P:(k + 1) * P], s.ident[:, :])
                last.then_inc(yT_ps, 1)

            def times_wo(tile):
                pe.wait_ge(yT_ready, tile + 1)
                if not zero(tile):
                    pe.wait_ge(z_out, tile)
                for k in range(KC):
                    last = nc.tensor.matmul(psZ[:, 0:C], yT[:, k * P:(k + 1) * P], woT[:, k, :], start=(k == 0), stop=(k == KC - 1))
                last.then_inc(z_ps, 1)

            def group(g, tiles):
                U = 2 * tiles
                scores_own(g, 0)
                def alone(c):
                    for x in range(2):
                        score_full(g, 0, c, x)
                chunks(pe, g, alone)
                for k in range(U):
                    n = upto(g, k)
                    blocks = k // 2 + 1
                    more = k + 1 < U
                    if more:
                        scores_own(g, k + 1)
                    done = k >= 2 and k % 2 == 0
                    if done:
                        turn_y(4 * g + k // 2 - 1, (k // 2 - 1) % 2)
                    for x in range(2):
                        turn_p(x, n, blocks)
                    for x in range(2):
                        times_v(x, n, g, k, g, blocks, True)
                    if done:
                        times_wo(4 * g + k // 2 - 1)

                    def full(c):
                        turn_p(0, n + 1 + c, BLOCKS)
                        if more:
                            score_full(g, k + 1, c, 0)
                        turn_p(1, n + 1 + c, BLOCKS)
                        times_v(0, n + 1 + c, g, k, c, BLOCKS, False)
                        if more:
                            score_full(g, k + 1, c, 1)
                        times_v(1, n + 1 + c, g, k, c, BLOCKS, False)
                    chunks(pe, g, full)
                turn_y(4 * g + tiles - 1, (tiles - 1) % 2)
                times_wo(4 * g + tiles - 1)

            groups(pe, group)

        @block.scalar
        def _(act):
            def raise_(x, j, n, src, dst):
                if not zero(n):
                    act.wait_ge(t_ps[x], n)
                nc.scalar.activation(dst, src, ACT.Exp, bias=bias[j][x][:, :], scale=SCALE).then_inc(p_ready[x], 1)

            def copy_t(n, width):
                act.wait_ge(t_ps[1], n + 1)
                if not zero(n):
                    act.wait_ge(pv[1], n)
                nc.scalar.activation(pT[1][:, 0:width], psT[1][:, 0:width], ACT.Copy).then_inc(pT_ready[1], 1)

            def copy_y(tile):
                act.wait_ge(yT_ps, tile + 1)
                if not zero(tile):
                    act.wait_ge(z_ps, tile)
                nc.scalar.activation(yT[:, :], psY[:, 0:C], ACT.Copy).then_inc(yT_ready, 1)

            def group(g, tiles):
                for k in range(2 * tiles):
                    n = upto(g, k)
                    j = k % 2
                    w = (k // 2 + 1) * P
                    act.wait_ge(high_ready, 8 * g + k + 1)
                    if k >= 2 and k % 2 == 0:
                        copy_y(4 * g + k // 2 - 1)
                    for x in range(2):
                        raise_(x, j, n, own[j][x][:, 0:w], p[x][:, 0:w])
                    copy_t(n, w)

                    def full(c):
                        for x in range(2):
                            raise_(x, j, n + 1 + c, past[j][x][:, bass.ds(c * 512, 512)], p[x][:, :])
                        copy_t(n + 1 + c, 512)
                    chunks(act, g, full)
                copy_y(4 * g + tiles - 1)

            groups(act, group)

        @block.vector
        def _(dve):
            def take_own(g, k, x):
                j, n, w = k % 2, upto(g, k), (k // 2) * P
                dve.wait_ge(s_ps[x], n + 1)
                nc.vector.tensor_tensor(own[j][x][:, w:w + P], psS[x][:, w:w + P], mask[:, :], ALU.add).then_inc(own_step, 1)
                if w:
                    nc.vector.tensor_scalar(own[j][x][:, 0:w], psS[x][:, 0:w], 1.0, None, ALU.mult).then_inc(own_step, 1)
                dve.wait_ge(own_step, owned(g, k, x))
                nc.vector.tensor_reduce(high[j][x][:, :], own[j][x][:, 0:w + P], AX_X, ALU.max).then_inc(s_out[x], 1)

            def owned(g, k, x):
                per = 2 * 2 * 2 * 4 - 4
                before = sum((2 if kk >= 2 else 1) * 2 for kk in range(k))
                return per * g + before + (2 if k >= 2 else 1) * (x + 1)

            def take_full(g, k, c, x):
                j, n = k % 2, upto(g, k) + 1 + c
                dve.wait_ge(s_out[x], n)
                dve.wait_ge(s_ps[x], n + 1)
                nc.vector.tensor_scalar(past[j][x][:, bass.ds(c * 512, 512)], psS[x][:, :], 1.0, high[j][x][:, :],
                                        ALU.mult, ALU.max, accum_out=high[j][x][:, :]).then_inc(s_out[x], 1)

            def settle(g, k):
                j = k % 2
                for x in range(2):
                    dve.wait_ge(s_out[x], upto(g, k + 1))
                    ins = nc.vector.tensor_scalar(bias[j][x][:, :], high[j][x][:, :], -SCALE, None, ALU.mult)
                ins.then_inc(high_ready, 1)

            def copy_t(n, width):
                dve.wait_ge(t_ps[0], n + 1)
                if not zero(n):
                    dve.wait_ge(pv[0], n)
                nc.vector.tensor_copy(pT[0][:, 0:width], psT[0][:, 0:width]).then_inc(pT_ready[0], 1)

            def finish(g, k):
                tile = k // 2
                for x in range(2):
                    dve.wait_ge(pv[x], upto(g, k + 1))
                    nc.vector.reciprocal(part[x][:, :], psO[x][:, HD:HD + 1]).then_inc(step, 1)
                if k % 2 == 0 and not (zero(g) and k < 4):
                    dve.wait_ge(yT_ps, 4 * g + tile - 1)
                dve.wait_ge(step, 2 * (8 * g + k) + 2)
                for x in range(2):
                    h = (2 * (k % 2) + x) * HD
                    ins = nc.vector.tensor_scalar(y[tile % 2][:, h:h + HD], psO[x][:, 0:HD], part[x][:, :], None, ALU.mult)
                ins.then_inc(o_out, 1)

            def add_z(g, k):
                t = 4 * g + k
                dve.wait_ge(z_ps, t + 1)
                nc.vector.tensor_tensor(s.x2[:, t, :], s.x2[:, t, :], psZ[:, 0:C], ALU.add).then_inc(z_out, 1)

            def group(g, tiles):
                U = 2 * tiles
                if not zero(g):
                    for x in range(2):
                        dve.wait_ge(p_ready[x], upto(g, 0))
                for x in range(2):
                    take_own(g, 0, x)
                def alone(c):
                    for x in range(2):
                        take_full(g, 0, c, x)
                chunks(dve, g, alone)
                settle(g, 0)
                for k in range(U):
                    n = upto(g, k)
                    more = k + 1 < U
                    w = (k // 2 + 1) * P
                    if more:
                        for x in range(2):
                            if k >= 1:
                                dve.wait_ge(p_ready[x], upto(g, k))
                            take_own(g, k + 1, x)
                    copy_t(n, w)
                    if k >= 2 and k % 2 == 0:
                        add_z(g, k // 2 - 1)

                    def full(c):
                        copy_t(n + 1 + c, 512)
                        if more:
                            for x in range(2):
                                take_full(g, k + 1, c, x)
                    chunks(dve, g, full)
                    if more:
                        settle(g, k + 1)
                    finish(g, k)
                add_z(g, tiles - 1)

            dve.wait_ge(consts_in, 32)
            groups(dve, group)


def route(nc, d, s):
    with ExitStack() as ctx:
        sb = lambda name, shape, dt=F32: ctx.enter_context(nc.sbuf_tensor(name, shape, dt))
        pb = lambda name: ctx.enter_context(nc.psum_tensor(name, [P, 512], F32))
        sem = lambda name: ctx.enter_context(nc.semaphore(name))
        ln2 = sb("ln2", [P, C])
        routerT = sb("routerT", [P, KC, NE])
        before = sb("before", [P, P])
        all1 = sb("all1", [P, P])
        iota = sb("riota", [P, LIST])
        zeros = sb("zeros", [P, ZW])
        rrms = sb("rrms", [P, NT])
        square = sb("rsquare", [P, C])
        flat = [sb(f"flat{b}", [P, C]) for b in range(2)]
        flatT = sb("flatT", [P, C])
        grid = lambda name: sb(name, [P, NT, NE])
        logit, key, one1, one2, both, run, place = (grid(n) for n in ("logit", "key", "one1", "one2", "both", "run", "place"))
        lift = sb("lift", [P, NT, NE + 1])
        m1, m2, i12, den, psum1 = (sb(n, [P, NT]) for n in ("m1", "m2", "i12", "den", "psum1"))
        filled = sb("filled", [P, NE, NT])
        tiles, end, start = (sb(n, [P, NE]) for n in ("tiles", "end", "start"))
        owner = sb("owner", [P, LIST, NE])
        ownerf = sb("ownerf", [P, LIST])
        where = [sb(f"where{b}", [P, 2], U32) for b in range(2)]
        psT, psL, psR, psC = (pb("r" + n) for n in ("psT", "psL", "psR", "psC"))
        consts_in = sem("rconsts_in")
        zeroed = sem("zeroed")
        blank = sem("blank")
        squared = sem("rsquared")
        meaned = sem("rmeaned")
        rooted = sem("rrooted")
        flat_ready = sem("flat_ready")
        flatT_ps = sem("flatT_ps")
        flatT_ready = sem("flatT_ready")
        logit_ps = sem("logit_ps")
        logit_ready = sem("logit_ready")
        lifted = sem("lifted")
        raised = sem("rraised")
        chosen = sem("chosen")
        counted = sem("counted")
        placed = sem("placed")
        again = sem("again")
        named = sem("rnamed")
        turn = sem("rturn")
        sent = [sem(f"sent{b}") for b in range(2)]
        step = sem("rstep")
        block = ctx.enter_context(nc.Block())

        @block.sync
        def _(sp):
            for dst, src in ((ln2[:, :], d.ln2[:, :]), (routerT[:, :, :], d.routerT[:, :].rearrange("(k p) n -> p k n", p=P)),
                             (before[:, :], d.before[:, :]), (iota[:, :], d.list[:, :])):
                sp.dma_start(dst, src).then_inc(consts_in, 16)
            sp.wait_ge(zeroed, 1)
            flatlist = d.list_x[:, :].rearrange("(p a) c -> p (a c)", p=P)
            for k in range(LIST * C // ZW):
                sp.dma_start(flatlist[:, k * ZW:(k + 1) * ZW], zeros[:, :]).then_inc(blank, 16)
            for e in range(NE):
                sp.dma_start(s.w13[:, e, :, :], d.w13[e, :, :].rearrange("(k p) n -> p k n", p=P)).then_inc(s.weights_in, 16)
                sp.dma_start(s.w2[:, e, :, :], d.w2[e, :, :].rearrange("(k p) n -> p k n", p=P)).then_inc(s.weights_in, 16)

        @block.gpsimd
        def _(pool):
            nc.gpsimd.memset(zeros[:, :], 0.0).then_inc(zeroed, 1)
            pool.wait_ge(blank, 16 * (LIST * C // ZW))
            pool.wait_ge(placed, 1)

            def body(i, b):
                t = 2 * i + b
                if not (isinstance(i, int) and i == 0):
                    pool.wait_ge(sent[b], 32 * i)
                    pool.sem_inc(turn, 1)
                nc.gpsimd.tensor_copy(where[b][:, :], s.where[:, t, :]).then_inc(named, 1)
                pool.wait_ge(named, t + 1)
                pool.wait_ge(again, t + 1)
                pool.sem_inc(turn, 1)
                for k in range(2):
                    pool.indirect_dma_start(d.list_x[:, :], bass.IndirectOffsetOnAxis(where[b][:, k:k + 1], 0),
                                            flat[b][:, :], None, bounds_check=LIST * P - 1, oob_is_err=False).then_inc(sent[b], 16)

            for b in range(2):
                body(0, b)
            with pool.Fori(1, NT // 2) as i:
                for b in range(2):
                    body(i, b)
            for b in range(2):
                pool.wait_ge(sent[b], 32 * (NT // 2))

        @block.scalar
        def _(act):
            with act.Fori(0, NT) as t:
                nc.scalar.activation(square[:, :], s.x2[:, t, :], ACT.Square, accum_out=rrms[:, bass.ds(t, 1)]).then_inc(squared, 1)
                act.wait_ge(squared, t + 1)
            act.wait_ge(meaned, 1)
            nc.scalar.activation(rrms[:, :], rrms[:, :], ACT.Sqrt).then_inc(rooted, 1)
            with act.Fori(0, NT) as t:
                act.wait_ge(flatT_ps, t + 1)
                nc.scalar.activation(flatT[:, :], psT[:, 0:C], ACT.Copy).then_inc(flatT_ready, 1)
                act.wait_ge(logit_ps, t + 1)
                nc.scalar.activation(logit[:, t, :], psL[:, 0:NE], ACT.Copy).then_inc(logit_ready, 1)
            act.wait_ge(lifted, 1)
            nc.scalar.activation(lift[:, :, :], lift[:, :, :], ACT.Exp).then_inc(raised, 1)

        @block.tensor
        def _(pe):
            pe.wait_ge(consts_in, 64)

            def body(i, b):
                t = 2 * i + b
                pe.wait_ge(flat_ready, t + 1)
                for k in range(KC):
                    last = nc.tensor.transpose(psT[:, k * P:(k + 1) * P], flat[b][:, k * P:(k + 1) * P], s.ident[:, :])
                last.then_inc(flatT_ps, 1)
                pe.wait_ge(flatT_ready, t + 1)
                if not (isinstance(t, int) and t == 0):
                    pe.wait_ge(logit_ready, t)
                for k in range(KC):
                    last = nc.tensor.matmul(psL[:, 0:NE], flatT[:, k * P:(k + 1) * P], routerT[:, k, :], start=(k == 0), stop=(k == KC - 1))
                last.then_inc(logit_ps, 1)

            for b in range(2):
                body(0, b)
            with pe.Fori(1, NT // 2) as i:
                for b in range(2):
                    body(i, b)
            pe.wait_ge(chosen, 1)
            m = both[:, :, :].rearrange("p t e -> p (t e)")
            nc.tensor.matmul(psR[:, 0:NT * NE], before[:, :], m, start=True, stop=True)
            nc.tensor.matmul(psC[:, 0:NT * NE], all1[:, :], m, start=True, stop=True).then_inc(counted, 1)

        @block.vector
        def _(dve):
            at = [0]

            def link(ins):
                at[0] += 1
                ins.then_inc(step, 1)
                dve.wait_ge(step, at[0])

            tt = lambda out, a, b, op: link(nc.vector.tensor_tensor(out, a, b, op))
            nc.vector.memset(all1[:, :], 1.0)
            dve.wait_ge(squared, NT)
            nc.vector.tensor_scalar(rrms[:, :], rrms[:, :], 1.0 / C, EPS_RMS, ALU.mult, ALU.add).then_inc(meaned, 1)
            dve.wait_ge(rooted, 1)
            link(nc.vector.reciprocal(rrms[:, :], rrms[:, :]))
            dve.wait_ge(consts_in, 64)

            def normal(t, b, done):
                nc.vector.scalar_tensor_tensor(flat[b][:, :], s.x2[:, t, :], rrms[:, bass.ds(t, 1)], ln2[:, :],
                                               ALU.mult, ALU.mult).then_inc(done, 1)

            for b in range(2):
                normal(b, b, flat_ready)
            with dve.Fori(1, NT // 2) as i:
                for b in range(2):
                    dve.wait_ge(flatT_ps, 2 * i + b - 1)
                    normal(2 * i + b, b, flat_ready)
            dve.wait_ge(logit_ready, NT)

            each = lambda a: a.unsqueeze(2).to_broadcast([P, NT, NE])
            number = iota[:, 0:NE].unsqueeze(1).to_broadcast([P, NT, NE])

            def choose(one, m, logits):
                link(nc.vector.tensor_reduce(m[:, :], logits, AX_X, ALU.max))
                tt(key[:, :, :], logits, each(m[:, :]), ALU.is_lt)
                link(nc.vector.scalar_tensor_tensor(key[:, :, :], key[:, :, :], float(NE), number, ALU.mult, ALU.add))
                link(nc.vector.tensor_reduce(i12[:, :], key[:, :, :], AX_X, ALU.min))
                tt(one, number, each(i12[:, :]), ALU.is_equal)

            choose(one1[:, :, :], m1, logit[:, :, :])
            link(nc.vector.scalar_tensor_tensor(run[:, :, :], one1[:, :, :], LOW, logit[:, :, :], ALU.mult, ALU.add))
            choose(one2[:, :, :], m2, run[:, :, :])
            tt(lift[:, :, 0:NE], logit[:, :, :], each(m1[:, :]), ALU.subtract)
            nc.vector.tensor_tensor(lift[:, :, NE], m2[:, :], m1[:, :], ALU.subtract).then_inc(lifted, 1)
            nc.vector.tensor_tensor(both[:, :, :], one1[:, :, :], one2[:, :, :], ALU.add).then_inc(chosen, 1)
            dve.wait_ge(raised, 1)
            link(nc.vector.tensor_reduce(psum1[:, :], lift[:, :, 0:NE], AX_X, ALU.add))
            link(nc.vector.reciprocal(psum1[:, :], psum1[:, :]))
            tt(m2[:, :], lift[:, :, NE], psum1[:, :], ALU.mult)
            tt(den[:, :], psum1[:, :], m2[:, :], ALU.add)
            link(nc.vector.tensor_scalar(den[:, :], den[:, :], 1e-9, None, ALU.add))
            link(nc.vector.reciprocal(den[:, :], den[:, :]))
            tt(s.share[:, :, 0], psum1[:, :], den[:, :], ALU.mult)
            tt(s.share[:, :, 1], m2[:, :], den[:, :], ALU.mult)
            dve.wait_ge(counted, 1)
            count = psC[:, 0:NT * NE].rearrange("p (t e) -> p t e", e=NE)
            link(nc.vector.tensor_copy(key[:, :, :], count))
            for e in range(NE):
                link(nc.vector.tensor_tensor_scan(run[:, :, e], key[:, :, e], key[:, :, e], 0.0, ALU.add, ALU.max))
            link(nc.vector.tensor_scalar(m1[:, :], iota[:, 0:NT], float(P), None, ALU.mult))
            tt(filled[:, :, :], run[:, NT - 1, :].unsqueeze(2).to_broadcast([P, NE, NT]),
               m1[:, :].unsqueeze(1).to_broadcast([P, NE, NT]), ALU.is_gt)
            link(nc.vector.tensor_reduce(tiles[:, :], filled[:, :, :], AX_X, ALU.add))
            link(nc.vector.tensor_tensor_scan(end[:, :], tiles[:, :], tiles[:, :], 0.0, ALU.add, ALU.max))
            tt(start[:, :], end[:, :], tiles[:, :], ALU.subtract)
            link(nc.vector.tensor_scalar(start[:, :], start[:, :], float(P), None, ALU.mult))
            tt(place[:, :, :], run[:, :, :], key[:, :, :], ALU.subtract)
            tt(place[:, :, :], place[:, :, :], start[:, :].unsqueeze(1).to_broadcast([P, NT, NE]), ALU.add)
            tt(place[:, :, :], place[:, :, :], psR[:, 0:NT * NE].rearrange("p (t e) -> p t e", e=NE), ALU.add)
            for n, one in enumerate((one1, one2)):
                tt(one[:, :, :], one[:, :, :], place[:, :, :], ALU.mult)
                link(nc.vector.tensor_reduce(i12[:, :], one[:, :, :], AX_X, ALU.add))
                link(nc.vector.tensor_copy(s.where[:, :, n], i12[:, :]))
            dve.sem_inc(placed, 1)
            tt(owner[:, :, :], iota[:, :].unsqueeze(2).to_broadcast([P, LIST, NE]),
               end[:, :].unsqueeze(1).to_broadcast([P, LIST, NE]), ALU.is_ge)
            link(nc.vector.tensor_reduce(ownerf[:, :], owner[:, :, :], AX_X, ALU.add))
            link(nc.vector.tensor_scalar(s.owner[:, :], ownerf[:, :], float(NE - 1), None, ALU.min))
            for b in range(2):
                normal(b, b, again)
            with dve.Fori(1, NT // 2) as i:
                for b in range(2):
                    dve.wait_ge(sent[b], 32 * i)
                    normal(2 * i + b, b, again)
            dve.wait_ge(again, NT)
            with dve.Fori(0, NT) as t:
                nc.vector.tensor_tensor(s.x1[:, t, :], s.x1[:, t, :], s.x2[:, t, :], ALU.add)


def experts(nc, d, s):
    with ExitStack() as ctx:
        sb = lambda name, shape, dt=F32: ctx.enter_context(nc.sbuf_tensor(name, shape, dt))
        pb = lambda name: ctx.enter_context(nc.psum_tensor(name, [P, 512], F32))
        sem = lambda name: ctx.enter_context(nc.semaphore(name))
        xs = [sb(f"xs{b}", [P, C]) for b in range(2)]
        xT = sb("exT", [P, C])
        gate = [sb(f"gate{z}", [P, HH]) for z in range(2)]
        h = sb("h", [P, KH * P])
        hT = sb("hidT", [P, KH * P])
        ys = [sb(f"ys{b}", [P, C]) for b in range(2)]
        psA = [pb(f"epsA{z}") for z in range(2)]
        psB = [pb(f"epsB{z}") for z in range(2)]
        psT, psY = pb("epsT"), pb("epsY")
        psH = [pb(f"epsH{z}") for z in range(2)]
        x_in = [sem(f"ex_in{b}") for b in range(2)]
        x_ps = sem("ex_ps")
        x_ready = sem("ex_ready")
        up = [sem(f"up{z}") for z in range(2)]
        gated = [sem(f"gated{z}") for z in range(2)]
        h_ready = [sem(f"h_ready{z}") for z in range(2)]
        h_ps = [sem(f"h_ps{z}") for z in range(2)]
        hT_ready = [sem(f"ehT{z}") for z in range(2)]
        y_ps = sem("ey_ps")
        y_ready = sem("ey_ready")
        y_out = [sem(f"ey_out{b}") for b in range(2)]
        block = ctx.enter_context(nc.Block())
        zero = lambda v: isinstance(v, int) and v == 0
        T3 = KH // 2 * P

        def pairs(eng, body):
            for b in range(2):
                body(b, b)
            with eng.Fori(1, LIST // 2) as i:
                for b in range(2):
                    body(2 * i + b, b)

        @block.sync
        def _(sp):
            for b in range(2):
                sp.dma_start(xs[b][:, :], d.list_x[b * P:(b + 1) * P, :]).then_inc(x_in[b], 16)
            with sp.Fori(1, LIST // 2) as i:
                for b in range(2):
                    sp.wait_ge(x_ps, 2 * i + b - 1)
                    sp.dma_start(xs[b][:, :], d.list_x[bass.ds(i * (2 * P) + b * P, P), :]).then_inc(x_in[b], 16)

        @block.gpsimd
        def _(pool):
            def body(n, b):
                pool.wait_ge(y_ready, n + 1)
                pool.sem_inc(s.turn, 1)
                pool.dma_start(d.list_y[bass.ds(n * P, P), :], ys[b][:, :]).then_inc(y_out[b], 16)
            pairs(pool, body)
            for b in range(2):
                pool.wait_ge(y_out[b], 16 * (LIST // 2))

        @block.tensor
        def _(pe):
            pe.wait_ge(s.weights_in, 32 * NE)

            def turn_x(n, b, i):
                pe.wait_ge(x_in[b], 16 * (i + 1))
                for k in range(KC):
                    last = nc.tensor.transpose(psT[:, k * P:(k + 1) * P], xs[b][:, k * P:(k + 1) * P], s.ident[:, :])
                last.then_inc(x_ps, 1)

            def turn_h(n):
                for z in range(2):
                    for w in range(2):
                        pe.wait_ge(h_ready[w], n + 1)
                    if not zero(n):
                        pe.wait_ge(hT_ready[z], n)
                    for k in range(KH // 2):
                        o = z * T3 + k * P
                        last = nc.tensor.transpose(psH[z][:, k * P:(k + 1) * P], h[:, o:o + P], s.ident[:, :])
                    last.then_inc(h_ps[z], 1)

            def ups(n, e):
                pe.wait_ge(x_ready, n + 1)
                for z in range(2):
                    if not zero(n):
                        pe.wait_ge(h_ready[z], n)
                    for ps, off in ((psA[z], 0), (psB[z], HID)):
                        for k in range(KC):
                            last = nc.tensor.matmul(ps[:, 0:HH], xT[:, k * P:(k + 1) * P],
                                                    s.w13[:, bass.ds(e, 1), k, off + z * HH:off + (z + 1) * HH].rearrange("p a n -> p (a n)"),
                                                    start=(k == 0), stop=(k == KC - 1))
                    last.then_inc(up[z], 1)

            def down(n, e):
                if not zero(n):
                    pe.wait_ge(y_ready, n)
                for k in range(KH):
                    if k % (KH // 2) == 0:
                        pe.wait_ge(hT_ready[k // (KH // 2)], n + 1)
                    last = nc.tensor.matmul(psY[:, 0:C], hT[:, k * P:(k + 1) * P],
                                            s.w2[:, bass.ds(e, 1), k, :].rearrange("p a n -> p (a n)"),
                                            start=(k == 0), stop=(k == KH - 1))
                last.then_inc(y_ps, 1)

            def expert(n):
                return pe.value_load(s.owner[0:1, bass.ds(n, 1)], min_val=0, max_val=NE - 1)

            turn_x(0, 0, 0)
            ups(0, expert(0))
            turn_x(1, 1, 0)
            turn_h(0)
            ups(1, expert(1))
            down(0, expert(0))
            with pe.Fori(1, LIST // 2) as i:
                for b in range(2):
                    n = 2 * i + b
                    turn_x(n, b, i)
                    turn_h(n - 1)
                    ups(n, expert(n))
                    down(n - 1, expert(n - 1))
            turn_h(LIST - 1)
            down(LIST - 1, expert(LIST - 1))

        @block.scalar
        def _(act):
            def body(n, b):
                act.wait_ge(x_ps, n + 1)
                if not zero(n):
                    act.wait_ge(up[1], n)
                nc.scalar.activation(xT[:, :], psT[:, 0:C], ACT.Copy).then_inc(x_ready, 1)
                if not zero(n):
                    copy_h(n - 1)
                for z in range(2):
                    act.wait_ge(up[z], n + 1)
                    if not zero(n):
                        act.wait_ge(h_ready[z], n)
                    nc.scalar.activation(gate[z][:, :], psA[z][:, 0:HH], ACT.Silu).then_inc(gated[z], 1)

            def copy_h(n):
                act.wait_ge(h_ps[0], n + 1)
                if not zero(n):
                    act.wait_ge(y_ps, n)
                nc.scalar.activation(hT[:, 0:T3], psH[0][:, 0:T3], ACT.Copy).then_inc(hT_ready[0], 1)

            pairs(act, body)
            copy_h(LIST - 1)

        @block.vector
        def _(dve):
            nc.vector.memset(h[:, HID:KH * P], 0.0)

            def copy_h(n):
                dve.wait_ge(h_ps[1], n + 1)
                if not zero(n):
                    dve.wait_ge(y_ps, n)
                nc.vector.tensor_copy(hT[:, T3:2 * T3], psH[1][:, 0:T3]).then_inc(hT_ready[1], 1)

            def copy_y(n, b, i):
                dve.wait_ge(y_ps, n + 1)
                if not zero(i):
                    dve.wait_ge(y_out[b], 16 * i)
                nc.vector.tensor_copy(ys[b][:, :], psY[:, 0:C]).then_inc(y_ready, 1)

            def hidden(n):
                for z in range(2):
                    dve.wait_ge(gated[z], n + 1)
                    if not zero(n):
                        dve.wait_ge(h_ps[1], n)
                    nc.vector.tensor_tensor(h[:, z * HH:(z + 1) * HH], gate[z][:, :], psB[z][:, 0:HH], ALU.mult).then_inc(h_ready[z], 1)

            hidden(0)
            copy_h(0)
            hidden(1)
            copy_y(0, 0, 0)
            with dve.Fori(1, LIST // 2) as i:
                copy_h(2 * i - 1)
                hidden(2 * i)
                copy_y(2 * i - 1, 1, i - 1)
                copy_h(2 * i)
                hidden(2 * i + 1)
                copy_y(2 * i, 0, i)
            copy_h(LIST - 1)
            copy_y(LIST - 1, 1, LIST // 2 - 1)


def finish(nc, d, s):
    with ExitStack() as ctx:
        sb = lambda name, shape, dt=F32: ctx.enter_context(nc.sbuf_tensor(name, shape, dt))
        sem = lambda name: ctx.enter_context(nc.semaphore(name))
        got = [[sb(f"got{b}{k}", [P, C]) for k in range(2)] for b in range(2)]
        where = [sb(f"fwhere{b}", [P, 2], U32) for b in range(2)]
        out = [sb(f"out{b}", [P, C]) for b in range(2)]
        named = sem("fnamed")
        turn = sem("fturn")
        fetched = [sem(f"fetched{b}") for b in range(2)]
        added = sem("added")
        ready = sem("fready")
        out_sent = [sem(f"out_sent{b}") for b in range(2)]
        block = ctx.enter_context(nc.Block())
        zero = lambda v: isinstance(v, int) and v == 0

        def tiles(eng, body):
            for b in range(2):
                body(0, b)
            with eng.Fori(1, NT // 2) as i:
                for b in range(2):
                    body(i, b)

        @block.gpsimd
        def _(pool):
            def body(i, b):
                t = 2 * i + b
                if not zero(i):
                    pool.wait_ge(ready, t - 1)
                    pool.sem_inc(turn, 1)
                nc.gpsimd.tensor_copy(where[b][:, :], s.where[:, t, :]).then_inc(named, 1)
                pool.wait_ge(named, t + 1)
                pool.sem_inc(turn, 1)
                for k in range(2):
                    pool.indirect_dma_start(got[b][k][:, :], None, d.list_y[:, :],
                                            bass.IndirectOffsetOnAxis(where[b][:, k:k + 1], 0),
                                            bounds_check=LIST * P - 1, oob_is_err=False).then_inc(fetched[b], 16)
            tiles(pool, body)

        @block.vector
        def _(dve):
            def body(i, b):
                t = 2 * i + b
                dve.wait_ge(fetched[b], 32 * (i + 1))
                if not zero(i):
                    dve.wait_ge(out_sent[b], 16 * i)
                nc.vector.scalar_tensor_tensor(got[b][0][:, :], got[b][0][:, :], s.share[:, t, 0:1], s.x1[:, t, :],
                                               ALU.mult, ALU.add).then_inc(added, 1)
                dve.wait_ge(added, t + 1)
                nc.vector.scalar_tensor_tensor(out[b][:, :], got[b][1][:, :], s.share[:, t, 1:2], got[b][0][:, :],
                                               ALU.mult, ALU.add).then_inc(ready, 1)
            tiles(dve, body)

        @block.sync
        def _(sp):
            def body(i, b):
                t = 2 * i + b
                sp.wait_ge(ready, t + 1)
                sp.dma_start(d.out[bass.ds(i * (2 * P) + b * P, P), :], out[b][:, :]).then_inc(out_sent[b], 16)
            tiles(sp, body)
            for b in range(2):
                sp.wait_ge(out_sent[b], 16 * (NT // 2))


class Named:
    pass


def build(nc, d):
    with ExitStack() as ctx:
        sb = lambda name, shape, dt=F32: ctx.enter_context(nc.sbuf_tensor(name, shape, dt))
        s = Named()
        s.ident = sb("ident", [P, P])
        s.x1 = sb("x1", [P, NT, C])
        s.where = sb("where", [P, NT, 2], U32)
        s.share = sb("share", [P, NT, 2])
        s.owner = sb("owners", [P, LIST], I32)
        s.weights_in = ctx.enter_context(nc.semaphore("expert_weights_in"))
        s.turn = ctx.enter_context(nc.semaphore("store_turn"))
        s.crowded = sb("crowded", [P, 1], I32)
        with ExitStack() as inner:
            sbi = lambda name, shape, dt=F32: inner.enter_context(nc.sbuf_tensor(name, shape, dt))
            s.vals = sbi("vals", [P, NT, SLOTS])
            s.cols = sbi("cols", [P, NT, SLOTS], U32)
            s.ssrc = sbi("ssrc", [P, NT, GH])
            s.we = sbi("we", [P, GH])
            prepare(nc, d, s)
            graph(nc, d, s)
            general(nc, d, s)
        s.x2 = sb("x2", [P, NT, C])
        with ExitStack() as inner:
            sbi = lambda name, shape, dt=F32: inner.enter_context(nc.sbuf_tensor(name, shape, dt))
            s.qT = sbi("qT", [P, 2, NP])
            s.kT = sbi("kT", [P, NP])
            s.v = sbi("v", [P, NT, 2, HD + 1])
            qkv(nc, d, s)
            attend(nc, d, s)
        s.w13 = sb("w13", [P, NE, KC, 2 * HID])
        s.w2 = sb("w2", [P, NE, KH, C])
        route(nc, d, s)
        experts(nc, d, s)
        finish(nc, d, s)


def kernel(x, adj, **w):
    import concourse.bacc as bacc
    from concourse.bass_utils import run_bass_kernel_spmd

    w = {k[3:]: np.asarray(v) for k, v in w.items()}
    x, adj = np.asarray(x), np.asarray(adj)

    xp = np.zeros((NP, C), np.float32)
    xp[:N] = x
    ap = np.zeros((NP, NP), np.float32)
    ap[:N, :N] = adj
    ap[np.arange(N, NP), np.arange(N, NP)] = 1.0
    ablk = np.zeros((C, 2 * GH), np.float32)
    for h in range(GH):
        ablk[h * GD:(h + 1) * GD, h] = w["gnn_a_dst"][h]
        ablk[h * GD:(h + 1) * GD, GH + h] = w["gnn_a_src"][h]
    wide = lambda v: np.ascontiguousarray(np.broadcast_to(v.reshape(1, -1), (P, v.size)))
    arrays = {
        "x": xp, "adj": ap, "w": w["gnn_W"], "wT": w["gnn_W"].T, "wrT": w["gnn_Wr"].T, "ablk": ablk,
        "br": w["gnn_br"].reshape(1, C), "be": wide(w["gnn_be"]), "we": wide(w["gnn_We"]),
        "ident": np.eye(P, dtype=np.float32),
        "iota": wide(np.arange(CAND, dtype=np.float32)),
        "qoff": wide((np.arange(CAND) // 8 * QW).astype(np.float32)),
    }
    order = (0, 2, 1, 3)
    wq = w["ffn_wq"].reshape(4, HD, C)[list(order)].reshape(C, C)
    arrays["wqkvT"] = np.concatenate([wq, w["ffn_wk"], w["ffn_wv"]]).T
    arrays["woT"] = w["ffn_wo"].reshape(C, 4, HD)[:, list(order)].reshape(C, C).T
    arrays["ln1"] = wide(w["ffn_ln1_w"])
    freq = np.outer(np.arange(NP, dtype=np.float32), 1.0 / 10000.0 ** (np.arange(0, HD, 2, dtype=np.float32) / HD))
    emb = np.concatenate([freq, freq], axis=-1)
    arrays["cos"] = np.cos(emb).astype(np.float32)
    arrays["sin"] = (np.sin(emb) * np.where(np.arange(HD) < HD // 2, -1, 1)).astype(np.float32)
    arrays["mask"] = np.where(np.arange(P)[None, :] <= np.arange(P)[:, None], 0.0, LOW).astype(np.float32)
    arrays["ln2"] = wide(w["ffn_ln2_w"])
    arrays["routerT"] = w["ffn_router_w"].T
    arrays["before"] = np.triu(np.ones((P, P), np.float32), 1)
    arrays["list"] = wide(np.arange(LIST, dtype=np.float32))
    arrays["w13"] = np.concatenate([w["ffn_w1"], w["ffn_w3"]], axis=1).transpose(0, 2, 1)
    arrays["w2"] = np.zeros((NE, KH * P, C), np.float32)
    arrays["w2"][:, :HID] = w["ffn_w2"].transpose(0, 2, 1)
    arrays = {k: np.ascontiguousarray(v) for k, v in arrays.items()}
    nc = bacc.Bacc("TRN2", target_bir_lowering=False, num_devices=1)
    d = Named()
    for name, a in arrays.items():
        setattr(d, name, nc.dram_tensor(f"in_{name}", a.shape, mybir.dt.from_np(a.dtype), kind="ExternalInput").ap())
    d.table = nc.dram_tensor("table", (NP, ROW), F32, kind="Internal").ap()
    d.list_x = nc.dram_tensor("list_x", (LIST * P, C), F32, kind="Internal").ap()
    d.list_y = nc.dram_tensor("list_y", (LIST * P, C), F32, kind="Internal").ap()
    d.out = nc.dram_tensor("out", (NP, C), F32, kind="ExternalOutput").ap()
    build(nc, d)
    r = run_bass_kernel_spmd(nc, [{f"in_{k}": v for k, v in arrays.items()}], core_ids=[0])
    return r.results[0]["out"][:N]
```

```python
from contextlib import ExitStack

import numpy as np

import concourse.bass as bass
from concourse import mybir

F32 = mybir.dt.float32
F32R = mybir.dt.float32r
U32 = mybir.dt.uint32
I32 = mybir.dt.int32
ALU = mybir.AluOpType
ACT = mybir.ActivationFunctionType
AX_X = mybir.AxisListType.X

P = 128
N = 3327
NT = -(-N // P)
NP = NT * P
C = 256
KC = C // P
GH, GD = 8, 32
ROW = C + GH
Q4 = 4
QW = NP // Q4
SLOTS = 16
CAND = Q4 * 8
EPS = 1e-5
ROUNDS = NP // 8
FAR = float(2 ** 20)
LOW = -1e30
HD = 64
NQK = 6
QKV = (NQK + 2) * HD
SCALE = HD ** -0.5
EPS_RMS = 1e-6
NE = 8
HID = 682
HH = HID // 2
KH = -(-HID // P)
LIST = (2 * NP + NE * (P - 1)) // P + (2 * NP + NE * (P - 1)) // P % 2
ZW = LIST * C // 16


def zero(v):
    return isinstance(v, int) and v == 0


def tiles(eng, body):
    for b in range(2):
        body(0, b)
    with eng.Fori(1, NT // 2) as i:
        for b in range(2):
            body(i, b)


def rounds(eng, body, last=NT // 2):
    body(1)
    with eng.Fori(2, last) as i:
        body(i)


def spread(nc, link, stats, mean, diff, raw, var, done):
    m0, v0, m1, v1 = (stats[:, :, k] for k in (1, 2, 4, 5))
    link(nc.vector.tensor_tensor(mean, m0, m1, ALU.add))
    link(nc.vector.tensor_scalar(mean, mean, 0.5, None, ALU.mult))
    link(nc.vector.tensor_tensor(diff, m0, m1, ALU.subtract))
    link(nc.vector.scalar_tensor_tensor(diff, diff, 0.25, diff, ALU.mult, ALU.mult))
    link(nc.vector.tensor_tensor(raw, v0, v1, ALU.add))
    link(nc.vector.scalar_tensor_tensor(raw, raw, 1.0 / C, diff, ALU.mult, ALU.add))
    nc.vector.tensor_scalar(var, raw, EPS, None, ALU.add).then_inc(done, 1)


def table(nc, d, s):
    with ExitStack() as ctx:
        sb = lambda name, shape, dt=F32: ctx.enter_context(nc.sbuf_tensor(name, shape, dt))
        pb = lambda name: ctx.enter_context(nc.psum_tensor(name, [P, 512], F32))
        sem = lambda name: ctx.enter_context(nc.semaphore(name))

        wcat = sb("wcat", [P, KC, C + 2 * GH])
        wnat = sb("wnat", [P, KC, C])
        ablk = sb("ablk", [P, KC, 2 * GH])
        wrT = sb("wrT", [P, KC, C])
        br = sb("br", [P, C])
        be = sb("be", [P, GH])
        xn = [sb(f"xn{b}", [P, C]) for b in range(2)]
        xnT = [sb(f"xnT{b}", [P, KC, P]) for b in range(2)]
        hs = [sb(f"hs{b}", [P, ROW + GH]) for b in range(2)]
        stats = sb("stats", [P, NT, 6])
        mean, diff, var, rstd = (sb(n, [P, NT]) for n in ("mean", "diff", "var", "rstd"))
        psT = pb("psT")
        psH, psR = ([pb(f"ps{n}{b}") for b in range(2)] for n in "HR")
        psW = pb("psW")[:, 0:KC * 2 * GH].rearrange("p (k n) -> p k n", k=KC)

        weights_in = sem("weights_in")
        small_in = sem("small_in")
        x_in = sem("x_in")
        table_out = [sem(f"table_out{b}") for b in range(2)]
        base_out = sem("base_out")
        fold_ps = sem("fold_ps")
        fold_sb = sem("fold_sb")
        varred = sem("varred")
        rooted = sem("rooted")
        xn_ready = sem("xn_ready")
        xnT_ps = sem("xnT_ps")
        xnT_ready = sem("xnT_ready")
        proj = sem("proj")
        hs_ready = sem("hs_ready")
        based = sem("based")
        step = sem("step")
        block = ctx.enter_context(nc.Block())

        @block.sync
        def _(sp):
            sp.dma_start(s.x1[:, 0:2, :], d.x[0:2 * P, :].rearrange("(t p) c -> p t c", p=P)).then_inc(x_in, 16)
            sp.dma_start(s.x1[:, 2:NT, :], d.x[2 * P:NP, :].rearrange("(t p) c -> p t c", p=P)).then_inc(x_in, 16)

            def store(i, b):
                sp.wait_ge(hs_ready, 2 * i + b + 1)
                sp.dma_start(d.table[bass.ds(i * (2 * P) + b * P, P), :], hs[b][:, 0:ROW]).then_inc(table_out[b], 16)
            tiles(sp, store)
            sp.wait_ge(based, NT)
            sp.dma_start(d.base[:, :].rearrange("(t p) c -> p t c", p=P), s.x1[:, :, :]).then_inc(base_out, 16)
            for b in range(2):
                sp.wait_ge(table_out[b], 16 * (NT // 2))
            sp.wait_ge(base_out, 16)

        @block.scalar
        def _(act):
            for dst, src in ((wnat, d.w), (wcat[:, :, 0:C], d.wT), (wrT, d.wrT)):
                act.dma_start(dst[:, :, :], src[:, :].rearrange("(k p) n -> p k n", p=P)).then_inc(weights_in, 16)
            act.dma_start(ablk[:, :, :], d.ablk[:, :].rearrange("(k p) n -> p k n", p=P)).then_inc(weights_in, 16)
            act.dma_start(s.ident[:, :], d.ident[:, :]).then_inc(weights_in, 16)
            act.dma_start(be[:, :], d.be[:, :]).then_inc(small_in, 16)
            act.dma_start(br[:, :], d.br[:, :]).then_inc(small_in, 16)
            act.wait_ge(fold_ps, 1)
            act.wait_ge(weights_in, 80)
            nc.scalar.activation(wcat[:, :, C:C + 2 * GH], psW[:, :, :], ACT.Copy).then_inc(fold_sb, 1)
            act.wait_ge(varred, 1)
            nc.scalar.activation(var[:, :], var[:, :], ACT.Sqrt).then_inc(rooted, 1)

            def copy_x(t, b):
                act.wait_ge(xnT_ps, t + 1)
                if not zero(t) and not (b == 1 and isinstance(t, int)):
                    act.wait_ge(proj, t - 1)
                nc.scalar.activation(xnT[b][:, :, :].rearrange("p k n -> p (k n)"), psT[:, 0:C], ACT.Copy).then_inc(xnT_ready, 1)

            def copy_h(i, b):
                act.wait_ge(proj, 2 * i + b + 1)
                if not zero(i):
                    act.wait_ge(table_out[b], 16 * i)
                    act.wait_ge(based, 2 * i + b - 1)
                nc.scalar.activation(hs[b][:, :], psH[b][:, 0:ROW + GH], ACT.Copy).then_inc(hs_ready, 1)

            copy_x(0, 0)
            copy_x(1, 1)
            copy_h(0, 0)

            def both(i):
                copy_x(2 * i, 0)
                copy_h(i - 1, 1)
                copy_x(2 * i + 1, 1)
                copy_h(i, 0)
            rounds(act, both)
            copy_h(NT // 2 - 1, 1)

        @block.tensor
        def _(pe):
            pe.wait_ge(weights_in, 80)
            for k in range(KC):
                for o in range(KC):
                    last = nc.tensor.matmul(psW[:, k, :], wnat[:, o, k * P:(k + 1) * P], ablk[:, o, :],
                                            start=(o == 0), stop=(o == KC - 1), skip_group_check=True)
            last.then_inc(fold_ps, 1)
            pe.wait_ge(fold_sb, 1)

            def turn(t, b):
                pe.wait_ge(xn_ready, t + 1)
                if not zero(t):
                    pe.wait_ge(xnT_ready, t)
                for k in range(KC):
                    last = nc.tensor.transpose(psT[:, k * P:(k + 1) * P], xn[b][:, k * P:(k + 1) * P], s.ident[:, :])
                last.then_inc(xnT_ps, 1)

            def project(i, b):
                t = 2 * i + b
                pe.wait_ge(xnT_ready, t + 1)
                if not zero(i):
                    pe.wait_ge(hs_ready, t - 1)
                    pe.wait_ge(based, t - 1)
                for ps, w in ((psH[b], wcat), (psR[b], wrT)):
                    n = w.shape[2]
                    for k in range(KC):
                        last = nc.tensor.matmul(ps[:, 0:n], xnT[b][:, k, :], w[:, k, :], start=(k == 0), stop=(k == KC - 1))
                last.then_inc(proj, 1)

            turn(0, 0)
            turn(1, 1)
            project(0, 0)

            def both(i):
                turn(2 * i, 0)
                project(i - 1, 1)
                turn(2 * i + 1, 1)
                project(i, 0)
            rounds(pe, both)
            project(NT // 2 - 1, 1)

        @block.vector
        def _(dve):
            at = [0]

            def link(ins):
                at[0] += 1
                ins.then_inc(step, 1)
                dve.wait_ge(step, at[0])

            dve.wait_ge(x_in, 32)
            with dve.Fori(0, NT // 2) as i:
                for b in range(2):
                    nc.vector.bn_stats(stats[:, 2 * i + b, :], s.x1[:, 2 * i + b, :]).then_inc(step, 1)
            at[0] += NT
            dve.wait_ge(step, at[0])
            spread(nc, link, stats, mean[:, :], diff[:, :], var[:, :], var[:, :], varred)
            dve.wait_ge(rooted, 1)
            link(nc.vector.reciprocal(rstd[:, :], var[:, :]))
            dve.wait_ge(small_in, 32)

            def norm(t, b):
                if not (isinstance(t, int) and t < 2):
                    dve.wait_ge(xnT_ps, t - 1)
                nc.vector.tensor_scalar(xn[b][:, :], s.x1[:, t, :], mean[:, bass.ds(t, 1)], rstd[:, bass.ds(t, 1)],
                                        ALU.subtract, ALU.mult).then_inc(xn_ready, 1)

            def base(t, b):
                dve.wait_ge(xn_ready, t + 1)
                nc.vector.tensor_tensor(s.x1[:, t, :], s.x1[:, t, :], br[:, :], ALU.add).then_inc(step, 1)
                dve.wait_ge(step, at[0] + t + 1)
                dve.wait_ge(hs_ready, t + 1)
                nc.vector.tensor_tensor(s.x1[:, t, :], s.x1[:, t, :], psR[b][:, 0:C], ALU.add)
                nc.vector.tensor_tensor(s.ssrc[:, t, :], hs[b][:, ROW:ROW + GH], be[:, :], ALU.add).then_inc(based, 1)

            norm(0, 0)
            norm(1, 1)
            with dve.Fori(0, NT // 2 - 1) as i:
                for b in range(2):
                    norm(2 * i + b + 2, b)
                    base(2 * i + b, b)
            for b in range(2):
                base(NT - 2 + b, b)


def build_crowded(s):
    def crowded(eng):
        return eng.value_load(s.crowded[0:1, 0:1], min_val=0, max_val=1)
    return crowded


def entries(nc, d, s):
    with ExitStack() as ctx:
        sb = lambda name, shape, dt=F32: ctx.enter_context(nc.sbuf_tensor(name, shape, dt))
        sem = lambda name: ctx.enter_context(nc.semaphore(name))
        iota = sb("iota", [P, CAND])
        qoff = sb("qoff", [P, CAND])
        adj = [sb(f"adj{b}", [P, NP]) for b in range(2)]
        cval = sb("cval", [P, CAND])
        cval2 = sb("cval2", [P, CAND])
        cidx = sb("cidx", [P, CAND], U32)
        cidf = sb("cidf", [P, CAND])
        pos = sb("pos", [P, SLOTS], U32)
        posf = sb("posf", [P, SLOTS])
        pick = sb("pick", [P, SLOTS, CAND])
        idf = sb("idf", [P, SLOTS])
        gone = sb("gone", [P, SLOTS])
        over = sb("over", [P, NT, Q4 + 1])
        overm = sb("overm", [P, 1])
        overall = sb("overall", [P, 1])
        best = [sb(f"best{b}", [P, SLOTS]) for b in range(2)]
        cols = [sb(f"cols{b}", [P, SLOTS], U32) for b in range(2)]
        rows = [sb(f"rows{b}", [P, SLOTS, ROW]) for b in range(2)]
        z = [sb(f"z{b}", [P, SLOTS, GH]) for b in range(2)]
        vw = sb("vw", [P, SLOTS, GH])
        low = sb("low", [P, SLOTS])
        top = sb("top", [P, GH])
        total = sb("total", [P, GH])
        psA = ctx.enter_context(nc.psum_tensor("psA", [P, 512], F32))
        consts_in = sem("econsts_in")
        adj_in = [sem(f"adj_in{b}") for b in range(2)]
        cleared = sem("cleared")
        searched = sem("searched")
        named = sem("named")
        turn = sem("turn")
        gathered = [sem(f"gathered{b}") for b in range(2)]
        scored = sem("scored")
        raised = sem("raised")
        weighted = sem("weighted")
        summed = sem("summed")
        added = sem("added1")
        search_step = sem("search_step")
        combine_step = sem("combine_step")
        tick = sem("search_tick")
        over_one = sem("over_one")
        over_all = sem("over_all")
        block = ctx.enter_context(nc.Block())

        @block.sync
        def _(sp):
            for b in range(2):
                sp.dma_start(adj[b][:, :], d.adj[b * P:(b + 1) * P, :]).then_inc(adj_in[b], 16)
            for dst, src in ((s.we, d.we), (iota, d.iota), (qoff, d.qoff)):
                sp.dma_start(dst[:, :], src[:, :]).then_inc(consts_in, 16)
            with sp.Fori(1, NT // 2) as i:
                for b in range(2):
                    sp.wait_ge(searched, 2 * i + b - 1)
                    sp.dma_start(adj[b][:, :], d.adj[bass.ds(i * (2 * P) + b * P, P), :]).then_inc(adj_in[b], 16)

        @block.gpsimd
        def _(pool):
            pool.wait_ge(cleared, 2)

            def gather(i, b):
                t = 2 * i + b
                if not zero(i):
                    pool.wait_ge(summed, t - 1)
                    pool.sem_inc(turn, 1)
                pool.wait_ge(named, t + 1)
                pool.sem_inc(turn, 1)
                for k in range(SLOTS):
                    pool.indirect_dma_start(rows[b][:, k, :], None, d.table[:, :],
                                            bass.IndirectOffsetOnAxis(cols[b][:, k:k + 1], 0),
                                            bounds_check=NP - 1, oob_is_err=False).then_inc(gathered[b], 16)
            tiles(pool, gather)
            pool.wait_ge(over_one, 1)
            nc.gpsimd.partition_all_reduce(overall[:, :], overm[:, :], P, bass.bass_isa.ReduceOp.max).then_inc(over_all, 1)

        @block.scalar
        def _(act):
            with act.Fori(0, NT // 2) as i:
                for b in range(2):
                    act.wait_ge(scored, 2 * i + b + 1)
                    nc.scalar.activation(z[b][:, :, :], z[b][:, :, :], ACT.Exp).then_inc(raised, 1)

        @block.tensor
        def _(pe):
            with pe.Fori(0, NT // 2) as i:
                for b in range(2):
                    pe.wait_ge(added, 2 * i + b + 1)
                    pe.wait_ge(weighted, 2 * i + b + 1)
                    for k in range(SLOTS):
                        last = nc.tensor.matmul(psA[:, 0:C], s.ident[:, :], rows[b][:, k, 0:C], start=(k == 0), stop=(k == SLOTS - 1))
                    last.then_inc(summed, 1)

        @block.vector
        def _(dve):
            for b in range(2):
                nc.vector.memset(rows[b][:, :, :], 0.0).then_inc(cleared, 1)
            dve.wait_ge(consts_in, 48)
            dve.wait_ge(cleared, 2)
            nc.vector.memset(gone[:, :], 0.0).then_inc(added, 1)
            dve.wait_ge(added, 1)
            SEARCH, COMBINE = 15, 9

            def chains(sem, per, t):
                now = [0]

                def chain(ins, wait=True):
                    now[0] += 1
                    assert now[0] <= per
                    ins.then_inc(sem, 1)
                    if wait:
                        dve.wait_ge(sem, per * t + now[0])
                return chain

            def search(i, b):
                t = 2 * i + b
                chain = chains(search_step, SEARCH, t)
                if not zero(t):
                    dve.wait_ge(named, t)
                if not zero(i):
                    dve.wait_ge(gathered[b], 16 * SLOTS * i)
                    dve.wait_ge(weighted, t - 1)
                dve.wait_ge(adj_in[b], 16 * (i + 1))
                dve.sem_inc(tick, 1)
                for q in range(Q4):
                    chain(nc.vector.max(cval[:, 8 * q:8 * q + 8], adj[b][:, q * QW:(q + 1) * QW]), q == Q4 - 1)
                nc.vector.tensor_copy(over[:, t, 0:Q4], cval[:, :].rearrange("p (q e) -> p q e", e=8)[:, :, 7])
                for q in range(Q4):
                    ins = nc.vector.max_index(cidx[:, 8 * q:8 * q + 8], cval[:, 8 * q:8 * q + 8], adj[b][:, q * QW:(q + 1) * QW])
                ins.then_inc(searched, 1)
                chain(nc.vector.max(best[b][:, 0:8], cval[:, :]))
                nc.vector.tensor_scalar(gone[:, 0:8], best[b][:, 0:8], 0.0, FAR, ALU.is_le, ALU.mult)
                chain(nc.vector.match_replace(cval2[:, :], best[b][:, 0:8], cval[:, :], -3e38), False)
                chain(nc.vector.max_index(pos[:, 0:8], best[b][:, 0:8], cval[:, :]))
                chain(nc.vector.tensor_copy(posf[:, 0:8], pos[:, 0:8]), False)
                chain(nc.vector.max(best[b][:, 8:16], cval2[:, :]))
                nc.vector.tensor_scalar(gone[:, 8:16], best[b][:, 8:16], 0.0, FAR, ALU.is_le, ALU.mult)
                chain(nc.vector.max_index(pos[:, 8:16], best[b][:, 8:16], cval2[:, :]))
                chain(nc.vector.tensor_copy(posf[:, 8:16], pos[:, 8:16]), False)
                chain(nc.vector.tensor_tensor(cidf[:, :], cidx[:, :], qoff[:, :], ALU.add))
                wide = [P, SLOTS, CAND]
                chain(nc.vector.tensor_tensor(pick[:, :, :], iota[:, :].unsqueeze(1).to_broadcast(wide),
                                              posf[:, :].unsqueeze(2).to_broadcast(wide), ALU.is_equal))
                chain(nc.vector.tensor_tensor(pick[:, :, :], pick[:, :, :], cidf[:, :].unsqueeze(1).to_broadcast(wide), ALU.mult))
                chain(nc.vector.tensor_reduce(idf[:, :], pick[:, :, :], AX_X, ALU.add))
                nc.vector.tensor_copy(over[:, t, Q4:Q4 + 1], best[b][:, SLOTS - 1:SLOTS])
                nc.vector.tensor_tensor(cols[b][:, :], idf[:, :], gone[:, :], ALU.add).then_inc(named, 1)

            def combine(i, b):
                t = 2 * i + b
                chain = chains(combine_step, COMBINE, t)
                h = rows[b][:, :, 0:C].rearrange("p s (h d) -> p s h d", d=GD)
                zb = z[b][:, :, :]
                zh = zb.rearrange("p s h -> p h s")
                each = lambda a: a.unsqueeze(1).to_broadcast([P, SLOTS, GH])
                slot = lambda a: a.unsqueeze(2).to_broadcast([P, SLOTS, GH])
                if not zero(t):
                    dve.wait_ge(weighted, t)
                nc.vector.tensor_scalar(low[:, :], best[b][:, :], 0.0, LOW, ALU.is_le, ALU.mult)
                chain(nc.vector.tensor_tensor(vw[:, :, :], slot(best[b][:, :]), each(s.we[:, :]), ALU.mult), False)
                dve.wait_ge(gathered[b], 16 * SLOTS * (i + 1))
                chain(nc.vector.tensor_tensor(zb, rows[b][:, :, C:ROW], each(s.ssrc[:, bass.ds(t, 1), :].rearrange("p a h -> p (a h)")), ALU.add))
                chain(nc.vector.tensor_tensor(zb, zb, vw[:, :, :], ALU.add))
                chain(nc.vector.scalar_tensor_tensor(zb, zb, 0.2, zb, ALU.mult, ALU.max))
                chain(nc.vector.tensor_tensor(zb, zb, slot(low[:, :]), ALU.add))
                chain(nc.vector.tensor_reduce(top[:, :], zh, AX_X, ALU.max))
                nc.vector.tensor_tensor(zb, zb, each(top[:, :]), ALU.subtract).then_inc(scored, 1)
                dve.wait_ge(raised, t + 1)
                chain(nc.vector.tensor_reduce(total[:, :], zh, AX_X, ALU.add))
                chain(nc.vector.reciprocal(total[:, :], total[:, :]))
                chain(nc.vector.tensor_tensor(zb, zb, each(total[:, :]), ALU.mult))
                nc.vector.tensor_tensor(h, h, zb.unsqueeze(3).to_broadcast([P, SLOTS, GH, GD]), ALU.mult).then_inc(weighted, 1)

            def add(t):
                dve.wait_ge(summed, t + 1)
                nc.vector.tensor_tensor(s.x1[:, t, :], s.x1[:, t, :], psA[:, 0:C], ALU.add).then_inc(added, 1)
                dve.wait_ge(added, t + 2)
                dve.sem_inc(tick, 1)
                nc.vector.bn_stats(s.stats[:, t, :], s.x1[:, t, :])

            search(0, 0)
            search(0, 1)
            combine(0, 0)
            with dve.Fori(1, NT // 2) as i:
                search(i, 0)
                add(2 * i - 2)
                combine(i - 1, 1)
                search(i, 1)
                add(2 * i - 1)
                combine(i, 0)
            add(NT - 2)
            combine(NT // 2 - 1, 1)
            nc.vector.tensor_reduce(overm[:, :], over[:, :, :].rearrange("p t q -> p (t q)"), AX_X, ALU.max).then_inc(over_one, 1)
            add(NT - 1)
            dve.wait_ge(over_all, 1)
            nc.vector.tensor_scalar(s.crowded[:, :], overall[:, :], 0.0, None, ALU.is_gt)


def general(nc, d, s):
    with ExitStack() as ctx:
        sb = lambda name, shape, dt=F32: ctx.enter_context(nc.sbuf_tensor(name, shape, dt))
        sem = lambda name: ctx.enter_context(nc.semaphore(name))
        row = sb("grow", [P, NP])
        rows = sb("grows", [P, 8, ROW])
        best = sb("gbest", [P, 8])
        found = sb("gfound", [P, 8], U32)
        foundf = sb("gfoundf", [P, 8])
        cols = sb("gcols", [P, 8], U32)
        low, there = sb("glow", [P, 8]), sb("gthere", [P, 8])
        z = sb("gz", [P, 9, GH])
        peak, newpeak, total, part = (sb(n, [P, GH]) for n in ("gpeak", "gnewpeak", "gtotal", "gpart"))
        acc, add = sb("gacc", [P, C]), sb("gadd", [P, C])
        row_in = sem("grow_in")
        base_in = sem("gbase_in")
        crowded = build_crowded(s)
        found_ready = sem("gfound_ready")
        tick = sem("gtick")
        ptick = sem("gptick")
        gathered = sem("ggathered")
        scored = sem("gscored")
        raised = sem("graised")
        tiled = sem("gtiled")
        step = sem("ggstep")
        block = ctx.enter_context(nc.Block())

        @block.sync
        def _(sp):
            with sp.If(crowded(sp) > 0):
                sp.dma_start(s.x1[:, :, :], d.base[:, :].rearrange("(t p) c -> p t c", p=P)).then_inc(base_in, 16)
                with sp.Fori(0, NT) as t:
                    sp.wait_ge(tiled, t + 1)
                    sp.dma_start(row[:, :], d.adj[bass.ds(t * P, P), :]).then_inc(row_in, 16)

        @block.gpsimd
        def _(pool):
            with pool.If(crowded(pool) > 0):
                with pool.Fori(0, NT * ROUNDS) as n:
                    pool.wait_ge(found_ready, n + 1)
                    pool.sem_inc(ptick, 1)
                    for k in range(8):
                        pool.indirect_dma_start(rows[:, k, :], None, d.table[:, :],
                                                bass.IndirectOffsetOnAxis(cols[:, k:k + 1], 0),
                                                bounds_check=NP - 1, oob_is_err=False).then_inc(gathered, 16)

        @block.scalar
        def _(act):
            with act.If(crowded(act) > 0):
                with act.Fori(0, NT * ROUNDS) as n:
                    act.wait_ge(scored, n + 1)
                    nc.scalar.activation(z[:, :, :], z[:, :, :], ACT.Exp).then_inc(raised, 1)

        @block.vector
        def _(dve):
            with dve.If(crowded(dve) > 0):
                nc.vector.memset(rows[:, :, :], 0.0).then_inc(tiled, 1)
                dve.wait_ge(base_in, 16)
                dve.sem_inc(tick, 1)
                PER, TILE = 24, 6
                with dve.Fori(0, NT) as t:
                    def link(k, ins):
                        ins.then_inc(step, 1)
                        dve.wait_ge(step, t * (PER * ROUNDS + TILE) + (PER * ROUNDS if k > 3 else 0) + k)

                    dve.wait_ge(tiled, t + 1)
                    link(1, nc.vector.memset(peak[:, :], LOW))
                    link(2, nc.vector.memset(total[:, :], 0.0))
                    link(3, nc.vector.memset(acc[:, :], 0.0))
                    dve.wait_ge(row_in, 16 * (t + 1))
                    dve.sem_inc(tick, 1)
                    with dve.Fori(0, ROUNDS) as r:
                        now = [0]

                        def chain(ins):
                            now[0] += 1
                            ins.then_inc(step, 1)
                            dve.wait_ge(step, t * (PER * ROUNDS + TILE) + 3 + PER * r + now[0])
                            dve.sem_inc(tick, 1)

                        n = t * ROUNDS + r
                        zs = z[:, 0:8, :]
                        zh = zs.rearrange("p s h -> p h s")
                        h = rows[:, :, 0:C]
                        each = lambda a: a.unsqueeze(1).to_broadcast([P, 8, GH])
                        slot = lambda a: a.unsqueeze(2).to_broadcast([P, 8, GH])
                        chain(nc.vector.max(best[:, :], row[:, :]))
                        chain(nc.vector.max_index(found[:, :], best[:, :], row[:, :]))
                        chain(nc.vector.match_replace(row[:, :], best[:, :], row[:, :], -3e38))
                        chain(nc.vector.tensor_scalar(low[:, :], best[:, :], 0.0, FAR, ALU.is_le, ALU.mult))
                        chain(nc.vector.tensor_copy(foundf[:, :], found[:, :]))
                        nc.vector.tensor_tensor(cols[:, :], foundf[:, :], low[:, :], ALU.add).then_inc(found_ready, 1)
                        dve.wait_ge(found_ready, n + 1)
                        chain(nc.vector.tensor_scalar(low[:, :], best[:, :], 0.0, LOW, ALU.is_le, ALU.mult))
                        chain(nc.vector.tensor_scalar(there[:, :], best[:, :], 0.0, None, ALU.is_gt))
                        chain(nc.vector.tensor_tensor(zs, slot(best[:, :]), each(s.we[:, :]), ALU.mult))
                        dve.wait_ge(gathered, 128 * (n + 1))
                        chain(nc.vector.tensor_tensor(rows[:, :, C:ROW], rows[:, :, C:ROW], each(s.ssrc[:, t, :]), ALU.add))
                        chain(nc.vector.tensor_tensor(zs, zs, rows[:, :, C:ROW], ALU.add))
                        chain(nc.vector.scalar_tensor_tensor(zs, zs, 0.2, zs, ALU.mult, ALU.max))
                        chain(nc.vector.tensor_tensor(zs, zs, slot(low[:, :]), ALU.add))
                        chain(nc.vector.tensor_reduce(newpeak[:, :], zh, AX_X, ALU.max))
                        chain(nc.vector.tensor_tensor(newpeak[:, :], newpeak[:, :], peak[:, :], ALU.max))
                        chain(nc.vector.tensor_tensor(zs, zs, each(newpeak[:, :]), ALU.subtract))
                        nc.vector.tensor_tensor(z[:, 8, :], peak[:, :], newpeak[:, :], ALU.subtract).then_inc(scored, 1)
                        dve.wait_ge(raised, n + 1)
                        chain(nc.vector.tensor_copy(peak[:, :], newpeak[:, :]))
                        chain(nc.vector.tensor_tensor(zs, zs, slot(there[:, :]), ALU.mult))
                        chain(nc.vector.tensor_reduce(part[:, :], zh, AX_X, ALU.add))
                        chain(nc.vector.tensor_tensor(total[:, :], total[:, :], z[:, 8, :], ALU.mult))
                        chain(nc.vector.tensor_tensor(total[:, :], total[:, :], part[:, :], ALU.add))
                        chain(nc.vector.tensor_tensor(h.rearrange("p s (h d) -> p s h d", d=GD), h.rearrange("p s (h d) -> p s h d", d=GD),
                                                      zs.unsqueeze(3).to_broadcast([P, 8, GH, GD]), ALU.mult))
                        ac = acc[:, :].rearrange("p (h d) -> p h d", d=GD)
                        chain(nc.vector.tensor_tensor(ac, ac, z[:, 8, :].unsqueeze(2).to_broadcast([P, GH, GD]), ALU.mult))
                        chain(nc.vector.tensor_reduce(add[:, :], h.rearrange("p s c -> p c s"), AX_X, ALU.add))
                        chain(nc.vector.tensor_tensor(acc[:, :], acc[:, :], add[:, :], ALU.add))
                        assert now[0] == PER, now
                    link(4, nc.vector.reciprocal(total[:, :], total[:, :]))
                    ac = acc[:, :].rearrange("p (h d) -> p h d", d=GD)
                    link(5, nc.vector.tensor_tensor(ac, ac, total[:, :].unsqueeze(2).to_broadcast([P, GH, GD]), ALU.mult))
                    link(6, nc.vector.tensor_tensor(s.x1[:, t, :], s.x1[:, t, :], acc[:, :], ALU.add))
                    dve.sem_inc(tick, 1)
                    nc.vector.bn_stats(s.stats[:, t, :], s.x1[:, t, :]).then_inc(tiled, 1)


def qkv(nc, d, s):
    with ExitStack() as ctx:
        sb = lambda name, shape, dt=F32: ctx.enter_context(nc.sbuf_tensor(name, shape, dt))
        pb = lambda name: ctx.enter_context(nc.psum_tensor(name, [P, 512], F32))
        sem = lambda name: ctx.enter_context(nc.semaphore(name))
        wqkvT = sb("wqkvT", [P, KC, QKV])
        ln1 = sb("ln1", [P, C])
        cos = sb("cos", [P, NT, HD])
        sin = sb("sin", [P, NT, HD])
        mean, diff, raw, var, rstd, rrms = (sb(n, [P, NT]) for n in ("qmean", "qdiff", "qraw", "qvar", "qrstd", "qrrms"))
        hn = [sb(f"hn{b}", [P, C]) for b in range(2)]
        hT = [sb(f"hT{b}", [P, KC, P]) for b in range(2)]
        qk = [sb(f"qk{b}", [P, QKV]) for b in range(2)]
        rot = [sb(f"rot{b}", [P, NQK, HD]) for b in range(2)]
        cross = sb("cross", [P, NQK, HD])
        kplain = sb("kplain", [P, P])
        psT, psQ, psK = pb("qpsT"), pb("qpsQ"), pb("qpsK")
        consts_in = sem("consts_in")
        varred = sem("qvarred")
        rooted = sem("qrooted")
        normed = sem("normed")
        meaned = sem("meaned")
        step = sem("qstep")
        hn_ready = sem("hn_ready")
        hT_ps = sem("hT_ps")
        hT_ready = sem("hT_ready")
        qkv_ps = sem("qkv_ps")
        qk_ready = sem("qk_ready")
        turned = sem("turned")
        qkT_ps = sem("qkT_ps")
        stored = sem("stored")
        k_split = sem("k_split")
        block = ctx.enter_context(nc.Block())

        def lagged(eng, one, two, three):
            def both(i):
                for b in range(2):
                    one(2 * i + b + 1, 1 - b)
                    two(2 * i + b, b)
                    three(2 * i + b - 1, 1 - b)

            one(0, 0)
            one(1, 1)
            two(0, 0)
            one(2, 0)
            two(1, 1)
            three(0, 0)
            both(1)
            with eng.Fori(2, NT // 2 - 1) as i:
                both(i)
            one(NT - 1, 1)
            two(NT - 2, 0)
            three(NT - 3, 1)
            two(NT - 1, 1)
            three(NT - 2, 0)
            three(NT - 1, 1)

        @block.gpsimd
        def _(pool):
            with pool.Fori(0, NT) as t:
                at = bass.ds(t * P, P)
                pool.wait_ge(stored, t + 1)
                pool.sem_inc(s.turn, 1)
                for x in range(2):
                    r = slice(64 * x, 64 * x + 64)
                    nc.gpsimd.tensor_copy(s.kT[x][r, at], kplain[r, :]).then_inc(k_split, 1)
                pool.wait_ge(k_split, 4 * t + 2)
                pool.sem_inc(s.turn, 1)
                for x in range(2):
                    r = slice(64 * x, 64 * x + 64)
                    nc.gpsimd.tensor_tensor(s.kT[x][64 - 64 * x:128 - 64 * x, at], kplain[r, :],
                                            s.kT[x][r, at].bitcast(F32), ALU.subtract).then_inc(k_split, 1)

        @block.sync
        def _(sp):
            sp.dma_start(wqkvT[:, :, :], d.wqkvT[:, :].rearrange("(k p) n -> p k n", p=P)).then_inc(consts_in, 16)
            sp.dma_start(ln1[:, :], d.ln1[:, :]).then_inc(consts_in, 16)
            sp.dma_start(cos[:, :, :], d.cos[:, :].rearrange("(t p) n -> p t n", p=P)).then_inc(consts_in, 16)
            sp.dma_start(sin[:, :, :], d.sin[:, :].rearrange("(t p) n -> p t n", p=P)).then_inc(consts_in, 16)

        @block.scalar
        def _(act):
            act.wait_ge(varred, 1)
            nc.scalar.activation(var[:, :], var[:, :], ACT.Sqrt).then_inc(rooted, 1)
            act.wait_ge(meaned, 1)
            nc.scalar.activation(rrms[:, :], rrms[:, :], ACT.Sqrt).then_inc(rooted, 1)

            def copy_x(t, b):
                act.wait_ge(hT_ps, t + 1)
                if not isinstance(t, int) or t >= 2:
                    act.wait_ge(qkv_ps, t - 1)
                nc.scalar.activation(hT[b][:, :, :].rearrange("p k n -> p (k n)"), psT[:, 0:C], ACT.Copy).then_inc(hT_ready, 1)

            def copy_qkv(t, b):
                act.wait_ge(qkv_ps, t + 1)
                if not isinstance(t, int) or t >= 2:
                    act.wait_ge(turned, t - 1)
                nc.scalar.activation(qk[b][:, :], psQ[:, :], ACT.Copy).then_inc(qk_ready, 1)

            def store(t, b):
                act.wait_ge(qkT_ps, t + 1)
                nc.scalar.activation(s.qT[:, :, bass.ds(t * P, P)], psK[:, 0:2 * P].rearrange("p (a n) -> p a n", a=2), ACT.Copy)
                if not zero(t):
                    act.wait_ge(k_split, 4 * t)
                nc.scalar.activation(kplain[:, :], psK[:, 2 * P:3 * P], ACT.Copy).then_inc(stored, 1)

            lagged(act, copy_x, copy_qkv, store)

        @block.tensor
        def _(pe):
            pe.wait_ge(consts_in, 64)

            def turn_x(t, b):
                pe.wait_ge(hn_ready, t + 1)
                if not zero(t):
                    pe.wait_ge(hT_ready, t)
                for k in range(KC):
                    last = nc.tensor.transpose(psT[:, k * P:(k + 1) * P], hn[b][:, k * P:(k + 1) * P], s.ident[:, :])
                last.then_inc(hT_ps, 1)

            def project(t, b):
                pe.wait_ge(hT_ready, t + 1)
                if not zero(t):
                    pe.wait_ge(qk_ready, t)
                for k in range(KC):
                    last = nc.tensor.matmul(psQ[:, :], hT[b][:, k, :], wqkvT[:, k, :], start=(k == 0), stop=(k == KC - 1))
                last.then_inc(qkv_ps, 1)

            def turn_qk(t, b):
                pe.wait_ge(turned, t + 1)
                if not zero(t):
                    pe.wait_ge(stored, t)
                for k in range(3):
                    last = nc.tensor.transpose(psK[:, k * P:(k + 1) * P],
                                               rot[b][:, 2 * k:2 * k + 2, :].rearrange("p a n -> p (a n)"), s.ident[:, :])
                last.then_inc(qkT_ps, 1)

            lagged(pe, turn_x, project, turn_qk)

        @block.vector
        def _(dve):
            at = [0]

            def link(ins):
                at[0] += 1
                ins.then_inc(step, 1)
                dve.wait_ge(step, at[0])

            nc.vector.memset(s.v[:, :, :, HD:HD + 1], 1.0)
            spread(nc, link, s.stats, mean[:, :], diff[:, :], raw[:, :], var[:, :], varred)
            dve.wait_ge(rooted, 1)
            link(nc.vector.reciprocal(rstd[:, :], var[:, :]))
            link(nc.vector.tensor_tensor(raw[:, :], raw[:, :], rstd[:, :], ALU.mult))
            link(nc.vector.tensor_tensor(raw[:, :], raw[:, :], rstd[:, :], ALU.mult))
            nc.vector.tensor_scalar(rrms[:, :], raw[:, :], EPS_RMS, None, ALU.add).then_inc(meaned, 1)
            dve.wait_ge(rooted, 2)
            link(nc.vector.reciprocal(rrms[:, :], rrms[:, :]))
            dve.wait_ge(consts_in, 64)
            base = at[0]
            PER = 3

            def scale(t, b):
                nc.vector.tensor_scalar(s.x2[:, t, :], s.x1[:, t, :], mean[:, bass.ds(t, 1)], rstd[:, bass.ds(t, 1)],
                                        ALU.subtract, ALU.mult).then_inc(normed, 1)
                dve.wait_ge(normed, t + 1)
                if not isinstance(t, int) or t >= 2:
                    dve.wait_ge(hT_ps, t - 1)
                nc.vector.scalar_tensor_tensor(hn[b][:, :], s.x2[:, t, :], rrms[:, bass.ds(t, 1)], ln1[:, :],
                                               ALU.mult, ALU.mult).then_inc(hn_ready, 1)

            def rope(i, b):
                t = 2 * i + b
                now = [0]

                def chain(ins, wait=True):
                    now[0] += 1
                    ins.then_inc(step, 1)
                    if wait:
                        dve.wait_ge(step, base + PER * t + now[0])

                dve.wait_ge(qk_ready, t + 1)
                if not (isinstance(i, int) and i == 0):
                    dve.wait_ge(qkT_ps, t - 1)
                src = qk[b][:, 0:NQK * HD].rearrange("p (a n) -> p a n", n=HD)
                half = HD // 2
                wide = lambda a, n: a.unsqueeze(1).to_broadcast([P, NQK, n])
                nc.vector.tensor_copy(s.v[:, t, :, 0:HD], qk[b][:, NQK * HD:QKV].rearrange("p (a n) -> p a n", n=HD))
                chain(nc.vector.tensor_tensor(rot[b][:, :, :], src, wide(cos[:, t, :], HD), ALU.mult), False)
                chain(nc.vector.tensor_tensor(cross[:, :, 0:half], src[:, :, half:HD], wide(sin[:, t, 0:half], half), ALU.mult), False)
                chain(nc.vector.tensor_tensor(cross[:, :, half:HD], src[:, :, 0:half], wide(sin[:, t, half:HD], half), ALU.mult))
                nc.vector.tensor_tensor(rot[b][:, :, :], rot[b][:, :, :], cross[:, :, :], ALU.add).then_inc(turned, 1)
                dve.wait_ge(turned, t + 1)
                assert now[0] == PER

            def both(i):
                for b in range(2):
                    scale(2 * i + b + 2, b)
                    rope(i, b)

            scale(0, 0)
            scale(1, 1)
            both(0)
            with dve.Fori(1, NT // 2 - 1) as i:
                both(i)
            for b in range(2):
                rope(NT // 2 - 1, b)


def attend(nc, d, s):
    with ExitStack() as ctx:
        sb = lambda name, shape, dt=F32: ctx.enter_context(nc.sbuf_tensor(name, shape, dt))
        pb = lambda name: ctx.enter_context(nc.psum_tensor(name, [P, 512], F32))
        sem = lambda name: ctx.enter_context(nc.semaphore(name))
        PAIRS = NT // 2
        W = 2 * P
        mask, maskT = sb("mask", [P, P]), sb("maskT", [P, P])
        maskR, maskTR = sb("maskR", [P, P], F32R), sb("maskTR", [P, P], F32R)
        identR, ones = sb("identR", [P, P], F32R), sb("ones", [P, P], F32R)
        woT = sb("woT", [P, KC, C])
        q = [[[sb(f"q{v}{x}{m}", [P, 2, W], F32R) for m in range(2)] for x in range(2)] for v in range(2)]
        kb = [sb(f"kblock{a}", [P, P], F32R) for a in range(4)]
        cand = [sb(f"cand{v}", [P, 2, 2, 2, PAIRS]) for v in range(2)]
        top = sb("atop", [P, 2, 4])
        diag = [sb(f"diag{x}", [P, 4, P], F32R) for x in range(2)]
        level = [sb(f"level{x}", [P, 2 * W]) for x in range(2)]
        pT = [sb(f"pT{a}", [P, 2, W]) for a in range(4)]
        part = sb("apart", [P, 2, 4])
        y = sb("y", [P, 2, C])
        yT = sb("yT", [P, 2, C])
        square = sb("square", [P, C])
        psM, psS, psO = ([pb(f"ps{n}{x}") for x in range(2)] for n in "MSO")
        psY, psZ = pb("psY"), pb("psZ")
        consts_in = sem("aconsts_in")
        rounded = sem("rounded")
        high_ready = sem("high_ready")
        q_ready = sem("q_ready")
        k_ready = [sem(f"k_ready{a}") for a in range(4)]
        m_ps = [sem(f"m_ps{x}") for x in range(2)]
        m_out = [sem(f"m_out{x}") for x in range(2)]
        topped = sem("topped")
        drawn = sem("drawn")
        level_ps = sem("level_ps")
        leveled = sem("leveled")
        s_ps = [sem(f"s_ps{a}") for a in range(4)]
        s_out = [sem(f"s_out{a}") for a in range(4)]
        p_ready = [sem(f"p_ready{a}") for a in range(4)]
        pv = [sem(f"pv{a}") for a in range(4)]
        inverted = sem("inverted")
        o_out = sem("o_out")
        yT_ps = sem("yT_ps")
        yT_ready = sem("yT_ready")
        z_ps = sem("z_ps")
        z_out = sem("z_out")
        squared = sem("squared")
        turn = sem("aturn")
        block = ctx.enter_context(nc.Block())

        def items(i, b):
            return (2 * i + 1) * (i + b)

        def after(i, b):
            return (i, 1) if b == 0 else (i + 1, 0)

        def whole(eng, body):
            body(0, 0)
            body(0, 1)
            with eng.Fori(1, PAIRS // 2 - 1) as i:
                for b in range(2):
                    body(i, b)
            body(PAIRS // 2 - 1, 0)
            body(PAIRS // 2 - 1, 1)
            body(PAIRS // 2, 0)

        def short(u, left):
            return isinstance(u, int) and PAIRS - 1 - u <= left

        def others(eng, u, item, first=None):
            if not zero(u):
                (first or item)(1, 0, u)
            if not short(u, PAIRS) or u >= 2:
                with eng.Fori(1, u) as j:
                    item(1 + j, j, j - 1)

        @block.sync
        def _(sp):
            sp.dma_start(mask[:, :], d.mask[:, :]).then_inc(consts_in, 16)
            sp.dma_start(maskT[:, :], d.maskT[:, :]).then_inc(consts_in, 16)
            sp.dma_start(woT[:, :, :], d.woT[:, :].rearrange("(k p) n -> p k n", p=P)).then_inc(consts_in, 16)

        @block.gpsimd
        def _(pool):
            def keys(n, pair):
                for a in range(4):
                    if not zero(n):
                        pool.wait_ge(s_ps[a], n)
                        pool.sem_inc(turn, 1)
                    nc.gpsimd.tensor_copy(kb[a][:, :], s.kT[a % 2][:, bass.ds(pair * W + a // 2 * P, P)]).then_inc(k_ready[a], 1)

            def queries(i, b):
                w = 2 * i + b
                for other, x in ((0, 0), (0, 1), (1, 0), (1, 1)):
                    if x == 0:
                        pool.wait_ge(high_ready, 4 * w + 2 * other + 2)
                        pool.sem_inc(turn, 1)
                    m = x ^ other
                    src = s.qT[64 * x:64 * x + 64, :, bass.ds(w * W, W)]
                    high = q[b][x][x][64 * x:64 * x + 64, :, :].bitcast(F32)
                    nc.gpsimd.tensor_tensor(q[b][x][m][64 - 64 * m:128 - 64 * m, :, :], src, high, ALU.subtract).then_inc(q_ready, 1)
                pool.wait_ge(q_ready, 4 * w + 4)
                pool.sem_inc(turn, 1)

            queries(0, 0)

            def pair_of_tiles(i, b):
                u, n = 2 * i + b, items(i, b)
                keys(n, u)
                if not short(u, 0):
                    for a in range(4):
                        pool.wait_ge(k_ready[a], n + 1)
                    pool.sem_inc(turn, 1)
                    queries(*after(i, b))
                others(pool, u, lambda k, pair, before: keys(n + k, pair))
            whole(pool, pair_of_tiles)

        @block.tensor
        def _(pe):
            pe.wait_ge(consts_in, 48)
            pe.wait_ge(rounded, 6)

            def measure(i, b, k, pair, own, t, x):
                n = 2 * items(i, b) + k
                if not zero(n):
                    pe.wait_ge(m_out[x], n)
                keys = P if own and t == 0 else W
                for h in range(2):
                    last = nc.tensor.matmul(psM[x][:, h * W:h * W + keys], q[b][x][x][:, h, t * P:(t + 1) * P],
                                            s.kT[x][:, bass.ds(pair * W, keys)], start=(h == 0), stop=not own, skip_group_check=True)
                if own:
                    for h in range(2):
                        last = nc.tensor.matmul(psM[x][:, h * W + keys - P:h * W + keys], identR[:, :], maskR[:, :],
                                                start=False, stop=True, skip_group_check=True)
                last.then_inc(m_ps[x], 1)

            def spread_level(u):
                for x in range(2):
                    pe.wait_ge(drawn, 2 * u + x + 1)
                    last = nc.tensor.matmul(psM[x][:, :], ones[:, :], diag[x][:, :, :].rearrange("p a n -> p (a n)"),
                                            start=True, stop=True)
                    last.then_inc(level_ps, 1)

            def scores(u, b, n, own, a):
                x = a % 2
                pe.wait_ge(k_ready[a], n + 1)
                if own and a == 0:
                    pe.wait_ge(q_ready, 4 * u + 4)
                if a >= 2:
                    pe.wait_ge(s_out[x], n + 1)
                elif not zero(n):
                    pe.wait_ge(s_out[2 + x], n)
                w = slice(P, W) if own and a >= 2 else slice(0, W)
                out = psS[x][:, :].rearrange("p (h n) -> p h n", h=2)[:, :, w]
                for m in range(2):
                    last = nc.tensor.matmul(out, kb[a][:, :], q[b][x][m][:, :, w],
                                            start=(m == 0), stop=(m == 1 and not own), skip_group_check=True)
                if own:
                    o = P if a < 2 else 0
                    for h in range(2):
                        last = nc.tensor.matmul(psS[x][:, h * W + w.start:h * W + w.start + P], identR[:, :], maskTR[:, :],
                                                start=False, stop=True, skip_group_check=True)
                last.then_inc(s_ps[a], 1)

            def clear_output(u):
                if not zero(u):
                    pe.wait_ge(o_out, u)
                for t in range(2):
                    nc.tensor.matmul(psO[t][:, 510:512], ones[:, :], ones[:, 0:2], start=True, stop=True)

            def times_v(n, pair, a):
                x = a % 2
                pe.wait_ge(p_ready[a], n + 1)
                for t in range(2):
                    for h in range(2):
                        o = (2 * h + x) * (HD + 1)
                        last = nc.tensor.matmul(psO[t][:, o:o + HD + 1], pT[a][:, h, t * P:(t + 1) * P],
                                                s.v[:, bass.ds(2 * pair + a // 2, 1), x, :].rearrange("p a n -> p (a n)"),
                                                start=False, stop=False, skip_group_check=True)
                last.then_inc(pv[a], 1)

            def turn_y(u):
                pe.wait_ge(o_out, u + 1)
                for t in range(2):
                    for k in range(KC):
                        last = nc.tensor.transpose(psY[:, (2 * t + k) * P:(2 * t + k + 1) * P], y[:, t, k * P:(k + 1) * P], s.ident[:, :])
                last.then_inc(yT_ps, 1)

            def times_wo(u):
                pe.wait_ge(yT_ready, u + 1)
                if not zero(u):
                    pe.wait_ge(z_out, u)
                for t in range(2):
                    for k in range(KC):
                        last = nc.tensor.matmul(psZ[:, t * C:(t + 1) * C], yT[:, t, k * P:(k + 1) * P], woT[:, k, :],
                                                start=(k == 0), stop=(k == KC - 1), skip_group_check=True)
                last.then_inc(z_ps, 1)

            def pair_of_tiles(i, b):
                u, n, w = 2 * i + b, items(i, b), after(i, b)
                more = not short(u, 0)
                for a in range(4):
                    t, x = a // 2, a % 2
                    scores(u, b, n, True, a)
                    if not zero(u):
                        times_v(n - 1, 0 if short(u, PAIRS) and u == 1 else u - 2, a)
                    if more:
                        if a == 0:
                            pe.wait_ge(leveled, 2 * (u + 1))
                            pe.wait_ge(q_ready, 4 * (u + 1) + 2)
                        measure(*w, a, u, False, t, x)
                        measure(*w, a, u + 1, True, t, 1 - x)

                def item(k, pair, before):
                    for a in range(4):
                        scores(u, b, n + k, False, a)
                        times_v(n + k - 1, before, a)
                        if more:
                            measure(*w, 2 * (k + 1) + a // 2, pair, False, a // 2, a % 2)

                def first(k, pair, before):
                    for x in range(2):
                        scores(u, b, n + k, False, x)
                    clear_output(u)
                    for x in range(2):
                        times_v(n + k - 1, before, x)
                        if more:
                            measure(*w, 2 * (k + 1), pair, False, 0, x)
                    turn_y(u - 1)
                    for x in range(2):
                        scores(u, b, n + k, False, 2 + x)
                        times_v(n + k - 1, before, 2 + x)
                        if more:
                            measure(*w, 2 * (k + 1) + 1, pair, False, 1, x)
                if zero(u):
                    clear_output(u)
                others(pe, u, item, first)
                if not zero(u):
                    times_wo(u - 1)
                if not short(u, 0):
                    spread_level(u + 1)

            pe.wait_ge(q_ready, 2)
            for t in range(2):
                for x in range(2):
                    measure(0, 0, t, 0, True, t, x)
            spread_level(0)
            whole(pe, pair_of_tiles)
            for a in range(4):
                times_v(items(PAIRS // 2, 1) - 1, PAIRS - 2, a)
            turn_y(PAIRS - 1)
            times_wo(PAIRS - 1)

        @block.scalar
        def _(act):
            def high(i, b):
                for other, x in ((0, 0), (0, 1), (1, 0), (1, 1)):
                    src = s.qT[64 * x:64 * x + 64, :, bass.ds((2 * i + b) * W, W)]
                    m = x ^ other
                    nc.scalar.activation(q[b][x][m][64 * m:64 * m + 64, :, :], src, ACT.Copy).then_inc(high_ready, 1)

            def level_all(u):
                for x in range(2):
                    act.wait_ge(level_ps, 2 * u + x + 1)
                    nc.scalar.activation(level[x][:, :], psM[x][:, :], ACT.Copy).then_inc(leveled, 1)

            def raise_(n, own):
                for a in range(4):
                    act.wait_ge(s_out[a], n + 1)
                    here = pT[a][:, :, P:W] if own and a >= 2 else pT[a][:, :, :]
                    nc.scalar.activation(here, here, ACT.Exp, scale=SCALE).then_inc(p_ready[a], 1)

            def squares(u):
                act.wait_ge(z_out, u + 1)
                for t in range(2):
                    nc.scalar.activation(square[:, :], s.x2[:, 2 * u + t, :], ACT.Square, accum_out=s.squares[:, bass.ds(2 * u + t, 1)]).then_inc(squared, 1)
                    act.wait_ge(squared, 2 * u + t + 1)

            def copy_y(u):
                act.wait_ge(yT_ps, u + 1)
                if not zero(u):
                    act.wait_ge(z_ps, u)
                nc.scalar.activation(yT[:, :, :].rearrange("p t n -> p (t n)"), psY[:, :], ACT.Copy).then_inc(yT_ready, 1)

            def pair_of_tiles(i, b):
                u, n = 2 * i + b, items(i, b)

                def first(k, pair, before):
                    copy_y(u - 1)
                    raise_(n + k, False)
                raise_(n, True)
                others(act, u, lambda k, pair, before: raise_(n + k, False), first)
                if not short(u, 1):
                    high(i + 1, b)
                if not short(u, 0):
                    level_all(u + 1)
                if not (isinstance(u, int) and u < 2):
                    squares(u - 2)

            high(0, 0)
            high(0, 1)
            level_all(0)
            whole(act, pair_of_tiles)
            squares(PAIRS - 2)
            copy_y(PAIRS - 1)
            squares(PAIRS - 1)

        @block.vector
        def _(dve):
            def largest(i, b, k, pair, own, t, x):
                dve.wait_ge(m_ps[x], 2 * items(i, b) + k + 1)
                nc.vector.tensor_reduce(cand[b][:, x, :, t, bass.ds(pair, 1)].rearrange("p h a -> p (h a)"),
                                        psM[x][:, :].rearrange("p (h n) -> p h n", h=2)[:, :, 0:P if own and t == 0 else W],
                                        AX_X, ALU.max).then_inc(m_out[x], 1)

            def lower(n, own, a):
                x = a % 2
                dve.wait_ge(s_ps[a], n + 1)
                if not zero(n):
                    dve.wait_ge(pv[a], n)
                w = slice(P, W) if own and a >= 2 else slice(0, W)
                if own and a >= 2:
                    nc.vector.memset(pT[a][:, :, 0:P], 0.0)
                part = lambda v: v.rearrange("p (h n) -> p h n", h=2)[:, :, w]
                nc.vector.tensor_tensor(pT[a][:, :, w], part(psS[x][:, :]), part(level[x][:, :]), ALU.subtract).then_inc(s_out[a], 1)

            def settle(i, b):
                u, n = 2 * i + b, items(i, b)
                for x in range(2):
                    dve.wait_ge(m_out[x], 2 * (n + u + 1))
                if not zero(u):
                    dve.wait_ge(drawn, 2 * u)
                nc.vector.tensor_reduce(top[:, :, :].rearrange("p x a -> p (x a)"), cand[b][:, :, :, :, :].rearrange("p x h t a -> p (x h t) a"), AX_X, ALU.max).then_inc(topped, 1)
                dve.wait_ge(topped, u + 1)
                for x in range(2):
                    if not zero(u):
                        dve.wait_ge(level_ps, 2 * u)
                    nc.vector.tensor_tensor(diag[x][:, :, :], s.ident[:, :].unsqueeze(1).to_broadcast([P, 4, P]),
                                            top[:, x, :].unsqueeze(2).to_broadcast([P, 4, P]), ALU.mult).then_inc(drawn, 1)

            def finish(u, n):
                for a in range(4):
                    dve.wait_ge(pv[a], n)
                if not zero(u):
                    dve.wait_ge(o_out, u)
                for t in range(2):
                    o = psO[t][:, 0:4 * (HD + 1)].rearrange("p (h n) -> p h n", n=HD + 1)
                    nc.vector.reciprocal(part[:, t, :], o[:, :, HD]).then_inc(inverted, 1)
                dve.wait_ge(inverted, 2 * (u + 1))
                if not zero(u):
                    dve.wait_ge(yT_ps, u)
                for t in range(2):
                    o = psO[t][:, 0:4 * (HD + 1)].rearrange("p (h n) -> p h n", n=HD + 1)
                    ins = nc.vector.tensor_tensor(y[:, t, :].rearrange("p (h n) -> p h n", n=HD), o[:, :, 0:HD],
                                                  part[:, t, :].unsqueeze(2).to_broadcast([P, 4, HD]), ALU.mult)
                ins.then_inc(o_out, 1)

            def add_z(u):
                dve.wait_ge(z_ps, u + 1)
                here = s.x2[:, bass.ds(2 * u, 2), :].rearrange("p t n -> p (t n)")
                nc.vector.tensor_tensor(here, here, psZ[:, :], ALU.add).then_inc(z_out, 1)

            for v in range(2):
                nc.vector.memset(cand[v][:, :, :, :, :].rearrange("p t x h a -> p (t x h a)"), LOW).then_inc(rounded, 1)
            dve.wait_ge(consts_in, 48)
            nc.vector.tensor_copy(identR[:, :], s.ident[:, :]).then_inc(rounded, 1)
            nc.vector.tensor_scalar(ones[:, :], s.ident[:, :], 0.0, 1.0, ALU.mult, ALU.add).then_inc(rounded, 1)
            nc.vector.tensor_copy(maskR[:, :], mask[:, :]).then_inc(rounded, 1)
            nc.vector.tensor_copy(maskTR[:, :], maskT[:, :]).then_inc(rounded, 1)
            dve.wait_ge(rounded, 6)
            for t in range(2):
                for x in range(2):
                    largest(0, 0, t, 0, True, t, x)
            settle(0, 0)

            def pair_of_tiles(i, b):
                u, n, w = 2 * i + b, items(i, b), after(i, b)
                dve.wait_ge(leveled, 2 * (u + 1))
                more = not short(u, 0)
                for a in range(4):
                    t, x = a // 2, a % 2
                    lower(n, True, a)
                    if more:
                        largest(*w, a, u, False, t, x)
                        largest(*w, a, u + 1, True, t, 1 - x)
                if not zero(u):
                    finish(u - 1, n)

                def item(k, pair, before):
                    for a in range(4):
                        lower(n + k, False, a)
                        if more:
                            largest(*w, 2 * (k + 1) + a // 2, pair, False, a // 2, a % 2)

                others(dve, u, item)
                if not short(u, 0):
                    settle(*w)
                if not zero(u):
                    add_z(u - 1)
            whole(dve, pair_of_tiles)
            finish(PAIRS - 1, items(PAIRS // 2, 1))
            add_z(PAIRS - 1)


def route(nc, d, s):
    with ExitStack() as ctx:
        sb = lambda name, shape, dt=F32: ctx.enter_context(nc.sbuf_tensor(name, shape, dt))
        pb = lambda name: ctx.enter_context(nc.psum_tensor(name, [P, 512], F32))
        sem = lambda name: ctx.enter_context(nc.semaphore(name))
        ln2 = sb("ln2", [P, C])
        routerT = sb("routerT", [P, KC, NE])
        before = sb("before", [P, P])
        all1 = sb("all1", [P, P])
        iota = sb("riota", [P, LIST])
        zeros = sb("zeros", [P, ZW])
        rrms = sb("rrms", [P, NT])
        flat = [sb(f"flat{b}", [P, C]) for b in range(2)]
        flatT = [sb(f"flatT{b}", [P, C]) for b in range(2)]
        grid = lambda name: sb(name, [P, NT, NE])
        logit, key, one1, one2, both, run, place = (grid(n) for n in ("logit", "key", "one1", "one2", "both", "run", "place"))
        lift = sb("lift", [P, NT, NE + 1])
        m1, m2, i12, den, psum1 = (sb(n, [P, NT]) for n in ("m1", "m2", "i12", "den", "psum1"))
        filled = sb("filled", [P, NE, NT])
        tiles, end, start = (sb(n, [P, NE]) for n in ("tiles", "end", "start"))
        owner = sb("owner", [P, LIST, NE])
        ownerf = sb("ownerf", [P, LIST])
        where = [sb(f"where{b}", [P, 2], U32) for b in range(2)]
        psT, psL = ([pb(f"r{n}{b}") for b in range(2)] for n in ("psT", "psL"))
        psR, psC = pb("rpsR"), pb("rpsC")
        consts_in = sem("rconsts_in")
        zeroed = sem("zeroed")
        blank = sem("blank")
        meaned = sem("rmeaned")
        rooted = sem("rrooted")
        flat_ready = sem("flat_ready")
        flatT_ps = sem("flatT_ps")
        flatT_ready = sem("flatT_ready")
        logit_ps = sem("logit_ps")
        logit_ready = sem("logit_ready")
        lifted = sem("lifted")
        raised = sem("rraised")
        chosen = sem("chosen")
        counted = sem("counted")
        placed = sem("placed")
        again = sem("again")
        turn = sem("rturn")
        sent = [sem(f"sent{b}") for b in range(2)]
        step = sem("rstep")
        block = ctx.enter_context(nc.Block())

        def lagged(eng, one, two):
            def both(i):
                for b in range(2):
                    one(2 * i + b + 1, 1 - b)
                    two(2 * i + b, b)

            one(0, 0)
            both(0)
            with eng.Fori(1, NT // 2 - 1) as i:
                both(i)
            one(NT - 1, 1)
            for b in range(2):
                two(NT - 2 + b, b)

        @block.sync
        def _(sp):
            for dst, src in ((ln2[:, :], d.ln2[:, :]), (routerT[:, :, :], d.routerT[:, :].rearrange("(k p) n -> p k n", p=P)),
                             (before[:, :], d.before[:, :]), (iota[:, :], d.list[:, :])):
                sp.dma_start(dst, src).then_inc(consts_in, 16)
            sp.wait_ge(zeroed, 1)
            flatlist = d.list_x[:, :].rearrange("(p a) c -> p (a c)", p=P)
            for k in range(LIST * C // ZW):
                sp.dma_start(flatlist[:, k * ZW:(k + 1) * ZW], zeros[:, :]).then_inc(blank, 16)
            for e in range(NE):
                sp.dma_start(s.w13[:, e, :, :], d.w13[e, :, :].rearrange("(k p) n -> p k n", p=P)).then_inc(s.weights_in, 16)
                sp.dma_start(s.w2[:, e, :, :], d.w2[e, :, :].rearrange("(k p) n -> p k n", p=P)).then_inc(s.weights_in, 16)

        @block.gpsimd
        def _(pool):
            nc.gpsimd.memset(zeros[:, :], 0.0).then_inc(zeroed, 1)
            pool.wait_ge(blank, 16 * (LIST * C // ZW))
            pool.wait_ge(placed, 1)

            def body(i, b):
                t = 2 * i + b
                pool.wait_ge(again, t + 1)
                pool.sem_inc(turn, 1)
                for k in range(2):
                    pool.indirect_dma_start(d.list_x[:, :], bass.IndirectOffsetOnAxis(where[b][:, k:k + 1], 0),
                                            flat[b][:, :], None, bounds_check=LIST * P - 1, oob_is_err=False).then_inc(sent[b], 16)

            for b in range(2):
                body(0, b)
            with pool.Fori(1, NT // 2) as i:
                for b in range(2):
                    body(i, b)
            for b in range(2):
                pool.wait_ge(sent[b], 32 * (NT // 2))

        @block.scalar
        def _(act):
            act.wait_ge(meaned, 1)
            nc.scalar.activation(rrms[:, :], rrms[:, :], ACT.Sqrt).then_inc(rooted, 1)

            def copy_x(t, b):
                act.wait_ge(flatT_ps, t + 1)
                if not isinstance(t, int) or t >= 2:
                    act.wait_ge(logit_ps, t - 1)
                nc.scalar.activation(flatT[b][:, :], psT[b][:, 0:C], ACT.Copy).then_inc(flatT_ready, 1)

            def copy_logit(t, b):
                act.wait_ge(logit_ps, t + 1)
                nc.scalar.activation(logit[:, t, :], psL[b][:, 0:NE], ACT.Copy).then_inc(logit_ready, 1)

            lagged(act, copy_x, copy_logit)
            act.wait_ge(lifted, 1)
            nc.scalar.activation(lift[:, :, :], lift[:, :, :], ACT.Exp).then_inc(raised, 1)

        @block.tensor
        def _(pe):
            pe.wait_ge(consts_in, 64)

            def turn_x(t, b):
                pe.wait_ge(flat_ready, t + 1)
                if not isinstance(t, int) or t >= 2:
                    pe.wait_ge(flatT_ready, t - 1)
                for k in range(KC):
                    last = nc.tensor.transpose(psT[b][:, k * P:(k + 1) * P], flat[b][:, k * P:(k + 1) * P], s.ident[:, :])
                last.then_inc(flatT_ps, 1)

            def logits(t, b):
                pe.wait_ge(flatT_ready, t + 1)
                if not isinstance(t, int) or t >= 2:
                    pe.wait_ge(logit_ready, t - 1)
                for k in range(KC):
                    last = nc.tensor.matmul(psL[b][:, 0:NE], flatT[b][:, k * P:(k + 1) * P], routerT[:, k, :], start=(k == 0), stop=(k == KC - 1))
                last.then_inc(logit_ps, 1)

            lagged(pe, turn_x, logits)
            pe.wait_ge(chosen, 1)
            m = both[:, :, :].rearrange("p t e -> p (t e)")
            nc.tensor.matmul(psR[:, 0:NT * NE], before[:, :], m, start=True, stop=True)
            nc.tensor.matmul(psC[:, 0:NT * NE], all1[:, :], m, start=True, stop=True).then_inc(counted, 1)

        @block.vector
        def _(dve):
            at = [0]

            def link(ins):
                at[0] += 1
                ins.then_inc(step, 1)
                dve.wait_ge(step, at[0])

            tt = lambda out, a, b, op: link(nc.vector.tensor_tensor(out, a, b, op))
            nc.vector.memset(all1[:, :], 1.0)
            nc.vector.tensor_scalar(rrms[:, :], s.squares[:, :], 1.0 / C, EPS_RMS, ALU.mult, ALU.add).then_inc(meaned, 1)
            dve.wait_ge(rooted, 1)
            link(nc.vector.reciprocal(rrms[:, :], rrms[:, :]))
            dve.wait_ge(consts_in, 64)

            def normal(t, b, done):
                if done is flat_ready:
                    nc.vector.tensor_tensor(s.x1[:, t, :], s.x1[:, t, :], s.x2[:, t, :], ALU.add)
                else:
                    nc.vector.tensor_copy(where[b][:, :], s.where[:, t, :])
                nc.vector.scalar_tensor_tensor(flat[b][:, :], s.x2[:, t, :], rrms[:, bass.ds(t, 1)], ln2[:, :],
                                               ALU.mult, ALU.mult).then_inc(done, 1)

            for b in range(2):
                normal(b, b, flat_ready)
            with dve.Fori(1, NT // 2) as i:
                for b in range(2):
                    dve.wait_ge(flatT_ps, 2 * i + b - 1)
                    normal(2 * i + b, b, flat_ready)
            dve.wait_ge(logit_ready, NT)

            each = lambda a: a.unsqueeze(2).to_broadcast([P, NT, NE])
            number = iota[:, 0:NE].unsqueeze(1).to_broadcast([P, NT, NE])

            def choose(one, m, logits):
                link(nc.vector.tensor_reduce(m[:, :], logits, AX_X, ALU.max))
                tt(key[:, :, :], logits, each(m[:, :]), ALU.is_lt)
                link(nc.vector.scalar_tensor_tensor(key[:, :, :], key[:, :, :], float(NE), number, ALU.mult, ALU.add))
                link(nc.vector.tensor_reduce(i12[:, :], key[:, :, :], AX_X, ALU.min))
                tt(one, number, each(i12[:, :]), ALU.is_equal)

            choose(one1[:, :, :], m1, logit[:, :, :])
            link(nc.vector.scalar_tensor_tensor(run[:, :, :], one1[:, :, :], LOW, logit[:, :, :], ALU.mult, ALU.add))
            choose(one2[:, :, :], m2, run[:, :, :])
            tt(lift[:, :, 0:NE], logit[:, :, :], each(m1[:, :]), ALU.subtract)
            nc.vector.tensor_tensor(lift[:, :, NE], m2[:, :], m1[:, :], ALU.subtract).then_inc(lifted, 1)
            nc.vector.tensor_tensor(both[:, :, :], one1[:, :, :], one2[:, :, :], ALU.add).then_inc(chosen, 1)
            dve.wait_ge(raised, 1)
            link(nc.vector.tensor_reduce(psum1[:, :], lift[:, :, 0:NE], AX_X, ALU.add))
            link(nc.vector.reciprocal(psum1[:, :], psum1[:, :]))
            tt(m2[:, :], lift[:, :, NE], psum1[:, :], ALU.mult)
            tt(den[:, :], psum1[:, :], m2[:, :], ALU.add)
            link(nc.vector.tensor_scalar(den[:, :], den[:, :], 1e-9, None, ALU.add))
            link(nc.vector.reciprocal(den[:, :], den[:, :]))
            tt(s.share[:, :, 0], psum1[:, :], den[:, :], ALU.mult)
            tt(s.share[:, :, 1], m2[:, :], den[:, :], ALU.mult)
            dve.wait_ge(counted, 1)
            count = psC[:, 0:NT * NE].rearrange("p (t e) -> p t e", e=NE)
            link(nc.vector.tensor_copy(key[:, :, :], count))
            for e in range(NE):
                link(nc.vector.tensor_tensor_scan(run[:, :, e], key[:, :, e], key[:, :, e], 0.0, ALU.add, ALU.max))
            link(nc.vector.tensor_scalar(m1[:, :], iota[:, 0:NT], float(P), None, ALU.mult))
            tt(filled[:, :, :], run[:, NT - 1, :].unsqueeze(2).to_broadcast([P, NE, NT]),
               m1[:, :].unsqueeze(1).to_broadcast([P, NE, NT]), ALU.is_gt)
            link(nc.vector.tensor_reduce(tiles[:, :], filled[:, :, :], AX_X, ALU.add))
            link(nc.vector.tensor_tensor_scan(end[:, :], tiles[:, :], tiles[:, :], 0.0, ALU.add, ALU.max))
            tt(start[:, :], end[:, :], tiles[:, :], ALU.subtract)
            link(nc.vector.tensor_scalar(start[:, :], start[:, :], float(P), None, ALU.mult))
            tt(place[:, :, :], run[:, :, :], key[:, :, :], ALU.subtract)
            tt(place[:, :, :], place[:, :, :], start[:, :].unsqueeze(1).to_broadcast([P, NT, NE]), ALU.add)
            tt(place[:, :, :], place[:, :, :], psR[:, 0:NT * NE].rearrange("p (t e) -> p t e", e=NE), ALU.add)
            for n, one in enumerate((one1, one2)):
                tt(one[:, :, :], one[:, :, :], place[:, :, :], ALU.mult)
                link(nc.vector.tensor_reduce(i12[:, :], one[:, :, :], AX_X, ALU.add))
                link(nc.vector.tensor_copy(s.where[:, :, n], i12[:, :]))
            dve.sem_inc(placed, 1)
            tt(owner[:, :, :], iota[:, :].unsqueeze(2).to_broadcast([P, LIST, NE]),
               end[:, :].unsqueeze(1).to_broadcast([P, LIST, NE]), ALU.is_ge)
            link(nc.vector.tensor_reduce(ownerf[:, :], owner[:, :, :], AX_X, ALU.add))
            link(nc.vector.tensor_scalar(s.owner[:, :], ownerf[:, :], float(NE - 1), None, ALU.min))
            for b in range(2):
                normal(b, b, again)
            with dve.Fori(1, NT // 2) as i:
                for b in range(2):
                    dve.wait_ge(sent[b], 32 * i)
                    normal(2 * i + b, b, again)


def experts(nc, d, s):
    with ExitStack() as ctx:
        sb = lambda name, shape, dt=F32: ctx.enter_context(nc.sbuf_tensor(name, shape, dt))
        pb = lambda name: ctx.enter_context(nc.psum_tensor(name, [P, 512], F32))
        sem = lambda name: ctx.enter_context(nc.semaphore(name))
        xs = [sb(f"xs{b}", [P, C]) for b in range(2)]
        xT = sb("exT", [P, C])
        gate = [sb(f"gate{z}", [P, HH]) for z in range(2)]
        h = sb("h", [P, KH * P])
        hT = sb("hidT", [P, KH * P])
        ys = [sb(f"ys{b}", [P, C]) for b in range(2)]
        psA = [pb(f"epsA{z}") for z in range(2)]
        psB = [pb(f"epsB{z}") for z in range(2)]
        psT, psY = pb("epsT"), pb("epsY")
        psH = [pb(f"epsH{z}") for z in range(2)]
        x_in = [sem(f"ex_in{b}") for b in range(2)]
        x_ps = sem("ex_ps")
        x_ready = sem("ex_ready")
        up = [sem(f"up{z}") for z in range(2)]
        gated = [sem(f"gated{z}") for z in range(2)]
        h_ready = [sem(f"h_ready{z}") for z in range(2)]
        h_ps = [sem(f"h_ps{z}") for z in range(2)]
        hT_ready = [sem(f"ehT{z}") for z in range(2)]
        y_ps = sem("ey_ps")
        y_ready = sem("ey_ready")
        y_out = [sem(f"ey_out{b}") for b in range(2)]
        block = ctx.enter_context(nc.Block())
        T3 = KH // 2 * P

        def pairs(eng, body):
            for b in range(2):
                body(b, b)
            with eng.Fori(1, LIST // 2) as i:
                for b in range(2):
                    body(2 * i + b, b)

        @block.sync
        def _(sp):
            for b in range(2):
                sp.dma_start(xs[b][:, :], d.list_x[b * P:(b + 1) * P, :]).then_inc(x_in[b], 16)
            with sp.Fori(1, LIST // 2) as i:
                for b in range(2):
                    sp.wait_ge(x_ps, 2 * i + b - 1)
                    sp.dma_start(xs[b][:, :], d.list_x[bass.ds(i * (2 * P) + b * P, P), :]).then_inc(x_in[b], 16)

        @block.gpsimd
        def _(pool):
            def body(n, b):
                pool.wait_ge(y_ready, n + 1)
                pool.sem_inc(s.turn, 1)
                pool.dma_start(d.list_y[bass.ds(n * P, P), :], ys[b][:, :]).then_inc(y_out[b], 16)
            pairs(pool, body)
            for b in range(2):
                pool.wait_ge(y_out[b], 16 * (LIST // 2))

        @block.tensor
        def _(pe):
            pe.wait_ge(s.weights_in, 32 * NE)

            def turn_x(n, b, i):
                pe.wait_ge(x_in[b], 16 * (i + 1))
                for k in range(KC):
                    last = nc.tensor.transpose(psT[:, k * P:(k + 1) * P], xs[b][:, k * P:(k + 1) * P], s.ident[:, :])
                last.then_inc(x_ps, 1)

            def turn_h(n):
                for z in range(2):
                    for w in range(2):
                        pe.wait_ge(h_ready[w], n + 1)
                    if not zero(n):
                        pe.wait_ge(hT_ready[z], n)
                    for k in range(KH // 2):
                        o = z * T3 + k * P
                        last = nc.tensor.transpose(psH[z][:, k * P:(k + 1) * P], h[:, o:o + P], s.ident[:, :])
                    last.then_inc(h_ps[z], 1)

            def ups(n, e):
                pe.wait_ge(x_ready, n + 1)
                for z in range(2):
                    if not zero(n):
                        pe.wait_ge(h_ready[z], n)
                    for ps, off in ((psA[z], 0), (psB[z], HID)):
                        for k in range(KC):
                            last = nc.tensor.matmul(ps[:, 0:HH], xT[:, k * P:(k + 1) * P],
                                                    s.w13[:, bass.ds(e, 1), k, off + z * HH:off + (z + 1) * HH].rearrange("p a n -> p (a n)"),
                                                    start=(k == 0), stop=(k == KC - 1))
                    last.then_inc(up[z], 1)

            def down(n, e):
                if not zero(n):
                    pe.wait_ge(y_ready, n)
                for k in range(KH):
                    if k % (KH // 2) == 0:
                        pe.wait_ge(hT_ready[k // (KH // 2)], n + 1)
                    last = nc.tensor.matmul(psY[:, 0:C], hT[:, k * P:(k + 1) * P],
                                            s.w2[:, bass.ds(e, 1), k, :].rearrange("p a n -> p (a n)"),
                                            start=(k == 0), stop=(k == KH - 1))
                last.then_inc(y_ps, 1)

            def expert(n):
                return pe.value_load(s.owner[0:1, bass.ds(n, 1)], min_val=0, max_val=NE - 1)

            turn_x(0, 0, 0)
            ups(0, expert(0))
            turn_x(1, 1, 0)
            turn_h(0)
            ups(1, expert(1))
            down(0, expert(0))
            with pe.Fori(1, LIST // 2) as i:
                for b in range(2):
                    n = 2 * i + b
                    turn_x(n, b, i)
                    turn_h(n - 1)
                    ups(n, expert(n))
                    down(n - 1, expert(n - 1))
            turn_h(LIST - 1)
            down(LIST - 1, expert(LIST - 1))

        @block.scalar
        def _(act):
            def body(n, b):
                act.wait_ge(x_ps, n + 1)
                if not zero(n):
                    act.wait_ge(up[1], n)
                nc.scalar.activation(xT[:, :], psT[:, 0:C], ACT.Copy).then_inc(x_ready, 1)
                if not zero(n):
                    copy_h(n - 1)
                for z in range(2):
                    act.wait_ge(up[z], n + 1)
                    if not zero(n):
                        act.wait_ge(h_ready[z], n)
                    nc.scalar.activation(gate[z][:, :], psA[z][:, 0:HH], ACT.Silu).then_inc(gated[z], 1)

            def copy_h(n):
                act.wait_ge(h_ps[0], n + 1)
                if not zero(n):
                    act.wait_ge(y_ps, n)
                nc.scalar.activation(hT[:, 0:T3], psH[0][:, 0:T3], ACT.Copy).then_inc(hT_ready[0], 1)

            pairs(act, body)
            copy_h(LIST - 1)

        @block.vector
        def _(dve):
            nc.vector.memset(h[:, HID:KH * P], 0.0)

            def copy_h(n):
                dve.wait_ge(h_ps[1], n + 1)
                if not zero(n):
                    dve.wait_ge(y_ps, n)
                nc.vector.tensor_copy(hT[:, T3:2 * T3], psH[1][:, 0:T3]).then_inc(hT_ready[1], 1)

            def copy_y(n, b, i):
                dve.wait_ge(y_ps, n + 1)
                if not zero(i):
                    dve.wait_ge(y_out[b], 16 * i)
                nc.vector.tensor_copy(ys[b][:, :], psY[:, 0:C]).then_inc(y_ready, 1)

            def hidden(n):
                for z in range(2):
                    dve.wait_ge(gated[z], n + 1)
                    if not zero(n):
                        dve.wait_ge(h_ps[1], n)
                    nc.vector.tensor_tensor(h[:, z * HH:(z + 1) * HH], gate[z][:, :], psB[z][:, 0:HH], ALU.mult).then_inc(h_ready[z], 1)

            hidden(0)
            copy_h(0)
            hidden(1)
            copy_y(0, 0, 0)

            def both(i):
                copy_h(2 * i - 1)
                hidden(2 * i)
                copy_y(2 * i - 1, 1, i - 1)
                copy_h(2 * i)
                hidden(2 * i + 1)
                copy_y(2 * i, 0, i)
            rounds(dve, both, LIST // 2)
            copy_h(LIST - 1)
            copy_y(LIST - 1, 1, LIST // 2 - 1)


def finish(nc, d, s):
    with ExitStack() as ctx:
        sb = lambda name, shape, dt=F32: ctx.enter_context(nc.sbuf_tensor(name, shape, dt))
        sem = lambda name: ctx.enter_context(nc.semaphore(name))
        got = [[sb(f"got{b}{k}", [P, C]) for k in range(2)] for b in range(2)]
        where = [sb(f"fwhere{b}", [P, 2], U32) for b in range(2)]
        out = [sb(f"out{b}", [P, C]) for b in range(2)]
        named = sem("fnamed")
        turn = sem("fturn")
        fetched = [sem(f"fetched{b}") for b in range(2)]
        added = sem("added")
        ready = sem("fready")
        out_sent = [sem(f"out_sent{b}") for b in range(2)]
        block = ctx.enter_context(nc.Block())
        @block.gpsimd
        def _(pool):
            def body(i, b):
                t = 2 * i + b
                if not zero(i):
                    pool.wait_ge(ready, t - 1)
                    pool.sem_inc(turn, 1)
                pool.wait_ge(named, t + 1)
                pool.sem_inc(turn, 1)
                for k in range(2):
                    pool.indirect_dma_start(got[b][k][:, :], None, d.list_y[:, :],
                                            bass.IndirectOffsetOnAxis(where[b][:, k:k + 1], 0),
                                            bounds_check=LIST * P - 1, oob_is_err=False).then_inc(fetched[b], 16)
            tiles(pool, body)

        @block.scalar
        def _(act):
            def body(i, b):
                if not zero(i):
                    act.wait_ge(fetched[b], 32 * i)
                nc.scalar.activation(where[b][:, :], s.where[:, 2 * i + b, :], ACT.Copy).then_inc(named, 1)
            tiles(act, body)

        @block.vector
        def _(dve):
            def body(i, b):
                t = 2 * i + b
                dve.wait_ge(fetched[b], 32 * (i + 1))
                if not zero(i):
                    dve.wait_ge(out_sent[b], 16 * i)
                nc.vector.scalar_tensor_tensor(got[b][0][:, :], got[b][0][:, :], s.share[:, t, 0:1], s.x1[:, t, :],
                                               ALU.mult, ALU.add).then_inc(added, 1)
                dve.wait_ge(added, t + 1)
                nc.vector.scalar_tensor_tensor(out[b][:, :], got[b][1][:, :], s.share[:, t, 1:2], got[b][0][:, :],
                                               ALU.mult, ALU.add).then_inc(ready, 1)
            tiles(dve, body)

        @block.sync
        def _(sp):
            def body(i, b):
                t = 2 * i + b
                sp.wait_ge(ready, t + 1)
                sp.dma_start(d.out[bass.ds(i * (2 * P) + b * P, P), :], out[b][:, :]).then_inc(out_sent[b], 16)
            tiles(sp, body)
            for b in range(2):
                sp.wait_ge(out_sent[b], 16 * (NT // 2))


class Named:
    pass


def build(nc, d):
    with ExitStack() as ctx:
        sb = lambda name, shape, dt=F32: ctx.enter_context(nc.sbuf_tensor(name, shape, dt))
        s = Named()
        s.ident = sb("ident", [P, P])
        s.x1 = sb("x1", [P, NT, C])
        s.stats = sb("rowstats", [P, NT, 6])
        s.squares = sb("squares", [P, NT])
        s.where = sb("where", [P, NT, 2], U32)
        s.share = sb("share", [P, NT, 2])
        s.owner = sb("owners", [P, LIST], I32)
        s.weights_in = ctx.enter_context(nc.semaphore("expert_weights_in"))
        s.turn = ctx.enter_context(nc.semaphore("store_turn"))
        s.crowded = sb("crowded", [P, 1], I32)
        with ExitStack() as inner:
            sbi = lambda name, shape, dt=F32: inner.enter_context(nc.sbuf_tensor(name, shape, dt))
            s.ssrc = sbi("ssrc", [P, NT, GH])
            s.we = sbi("we", [P, GH])
            table(nc, d, s)
            entries(nc, d, s)
            general(nc, d, s)
        s.x2 = sb("x2", [P, NT, C])
        with ExitStack() as inner:
            sbi = lambda name, shape, dt=F32: inner.enter_context(nc.sbuf_tensor(name, shape, dt))
            s.qT = sbi("qT", [P, 2, NP])
            s.kT = [sbi(f"kT{x}", [P, NP], F32R) for x in range(2)]
            s.v = sbi("v", [P, NT, 2, HD + 1])
            qkv(nc, d, s)
            attend(nc, d, s)
        s.w13 = sb("w13", [P, NE, KC, 2 * HID])
        s.w2 = sb("w2", [P, NE, KH, C])
        route(nc, d, s)
        experts(nc, d, s)
        finish(nc, d, s)


def kernel(x, adj, **w):
    import concourse.bacc as bacc
    from concourse.bass_utils import run_bass_kernel_spmd

    w = {k[3:]: np.asarray(v) for k, v in w.items()}
    x, adj = np.asarray(x), np.asarray(adj)

    xp = np.zeros((NP, C), np.float32)
    xp[:N] = x
    ap = np.zeros((NP, NP), np.float32)
    ap[:N, :N] = adj
    ap[np.arange(N, NP), np.arange(N, NP)] = 1.0
    ablk = np.zeros((C, 2 * GH), np.float32)
    for h in range(GH):
        ablk[h * GD:(h + 1) * GD, h] = w["gnn_a_dst"][h]
        ablk[h * GD:(h + 1) * GD, GH + h] = w["gnn_a_src"][h]
    wide = lambda v: np.ascontiguousarray(np.broadcast_to(v.reshape(1, -1), (P, v.size)))
    arrays = {
        "x": xp, "adj": ap, "w": w["gnn_W"], "wT": w["gnn_W"].T, "wrT": w["gnn_Wr"].T, "ablk": ablk,
        "br": wide(w["gnn_br"]), "be": wide(w["gnn_be"]), "we": wide(w["gnn_We"]),
        "ident": np.eye(P, dtype=np.float32),
        "iota": wide(np.arange(CAND, dtype=np.float32)),
        "qoff": wide((np.arange(CAND) // 8 * QW).astype(np.float32)),
    }
    order = (0, 2, 1, 3)
    wq = w["ffn_wq"].reshape(4, HD, C)[list(order)].reshape(C, C)
    arrays["wqkvT"] = np.concatenate([wq, w["ffn_wk"], w["ffn_wv"]]).T
    arrays["woT"] = w["ffn_wo"].reshape(C, 4, HD)[:, list(order)].reshape(C, C).T
    arrays["ln1"] = wide(w["ffn_ln1_w"])
    freq = np.outer(np.arange(NP, dtype=np.float32), 1.0 / 10000.0 ** (np.arange(0, HD, 2, dtype=np.float32) / HD))
    emb = np.concatenate([freq, freq], axis=-1)
    arrays["cos"] = np.cos(emb).astype(np.float32)
    arrays["sin"] = (np.sin(emb) * np.where(np.arange(HD) < HD // 2, -1, 1)).astype(np.float32)
    causal = np.where(np.arange(P)[None, :] <= np.arange(P)[:, None], 0.0, LOW).astype(np.float32)
    arrays["mask"], arrays["maskT"] = causal, causal.T
    arrays["ln2"] = wide(w["ffn_ln2_w"])
    arrays["routerT"] = w["ffn_router_w"].T
    arrays["before"] = np.triu(np.ones((P, P), np.float32), 1)
    arrays["list"] = wide(np.arange(LIST, dtype=np.float32))
    arrays["w13"] = np.concatenate([w["ffn_w1"], w["ffn_w3"]], axis=1).transpose(0, 2, 1)
    arrays["w2"] = np.zeros((NE, KH * P, C), np.float32)
    arrays["w2"][:, :HID] = w["ffn_w2"].transpose(0, 2, 1)
    arrays = {k: np.ascontiguousarray(v) for k, v in arrays.items()}
    nc = bacc.Bacc("TRN2", target_bir_lowering=False, num_devices=1)
    d = Named()
    for name, a in arrays.items():
        setattr(d, name, nc.dram_tensor(f"in_{name}", a.shape, mybir.dt.from_np(a.dtype), kind="ExternalInput").ap())
    d.table = nc.dram_tensor("table", (NP, ROW), F32, kind="Internal").ap()
    d.base = nc.dram_tensor("base", (NP, C), F32, kind="Internal").ap()
    d.list_x = nc.dram_tensor("list_x", (LIST * P, C), F32, kind="Internal").ap()
    d.list_y = nc.dram_tensor("list_y", (LIST * P, C), F32, kind="Internal").ap()
    d.out = nc.dram_tensor("out", (NP, C), F32, kind="ExternalOutput").ap()
    build(nc, d)
    r = run_bass_kernel_spmd(nc, [{f"in_{k}": v for k, v in arrays.items()}], core_ids=[0])
    return r.results[0]["out"][:N]
```

```python
from contextlib import ExitStack

import numpy as np

import concourse.bass as bass
from concourse import mybir

F32 = mybir.dt.float32
F32R = mybir.dt.float32r
U32 = mybir.dt.uint32
I32 = mybir.dt.int32
ALU = mybir.AluOpType
ACT = mybir.ActivationFunctionType
AX_X = mybir.AxisListType.X

P = 128
N = 3327
NT = -(-N // P)
NP = NT * P
C = 256
KC = C // P
GH, GD = 8, 32
ROW = C + GH
Q4 = 4
QW = NP // Q4
SLOTS = 16
CAND = Q4 * 8
EPS = 1e-5
ROUNDS = NP // 8
FAR = float(2 ** 20)
LOW = -1e30
HD = 64
NQK = 6
QKV = (NQK + 2) * HD
SCALE = HD ** -0.5
EPS_RMS = 1e-6
NE = 8
HID = 682
HH = HID // 2
KH = -(-HID // P)
LIST = (2 * NP + NE * (P - 1)) // P + (2 * NP + NE * (P - 1)) // P % 2
ZW = LIST * C // 16


def zero(v):
    return isinstance(v, int) and v == 0


def tiles(eng, body):
    for b in range(2):
        body(0, b)
    with eng.Fori(1, NT // 2) as i:
        for b in range(2):
            body(i, b)


def fours(eng, body):
    for b in range(4):
        body(0, b)
    with eng.Fori(1, NT // 4) as i:
        for b in range(4):
            body(i, b)
    for b in range(NT % 4):
        body(NT // 4, b)


def rounds(eng, body, last=NT // 2):
    body(1)
    with eng.Fori(2, last) as i:
        body(i)


def spread(nc, link, stats, mean, diff, raw, var, done):
    m0, v0, m1, v1 = (stats[:, :, k] for k in (1, 2, 4, 5))
    link(nc.vector.tensor_tensor(mean, m0, m1, ALU.add))
    link(nc.vector.tensor_scalar(mean, mean, 0.5, None, ALU.mult))
    link(nc.vector.tensor_tensor(diff, m0, m1, ALU.subtract))
    link(nc.vector.scalar_tensor_tensor(diff, diff, 0.25, diff, ALU.mult, ALU.mult))
    link(nc.vector.tensor_tensor(raw, v0, v1, ALU.add))
    link(nc.vector.scalar_tensor_tensor(raw, raw, 1.0 / C, diff, ALU.mult, ALU.add))
    nc.vector.tensor_scalar(var, raw, EPS, None, ALU.add).then_inc(done, 1)


def table(nc, d, s):
    with ExitStack() as ctx:
        sb = lambda name, shape, dt=F32: ctx.enter_context(nc.sbuf_tensor(name, shape, dt))
        pb = lambda name: ctx.enter_context(nc.psum_tensor(name, [P, 512], F32))
        sem = lambda name: ctx.enter_context(nc.semaphore(name))

        wcat = sb("wcat", [P, KC, C + 2 * GH])
        wnat = sb("wnat", [P, KC, C])
        ablk = sb("ablk", [P, KC, 2 * GH])
        wrT = sb("wrT", [P, KC, C])
        br = sb("br", [P, C])
        be = sb("be", [P, GH])
        xn = [sb(f"xn{b}", [P, C]) for b in range(2)]
        xnT = [sb(f"xnT{b}", [P, KC, P]) for b in range(2)]
        hs = [sb(f"hs{b}", [P, ROW + GH]) for b in range(2)]
        stats = sb("stats", [P, NT, 6])
        mean, diff, var, rstd = (sb(n, [P, NT]) for n in ("mean", "diff", "var", "rstd"))
        psT = pb("psT")
        psH, psR = ([pb(f"ps{n}{b}") for b in range(2)] for n in "HR")
        psW = pb("psW")[:, 0:KC * 2 * GH].rearrange("p (k n) -> p k n", k=KC)

        weights_in = sem("weights_in")
        small_in = sem("small_in")
        x_in = [sem(f"x_in{half}") for half in range(2)]
        table_out = [sem(f"table_out{b}") for b in range(2)]
        fold_ps = sem("fold_ps")
        fold_sb = sem("fold_sb")
        varred = sem("varred")
        rooted = sem("rooted")
        xn_ready = sem("xn_ready")
        xnT_ps = sem("xnT_ps")
        xnT_ready = sem("xnT_ready")
        proj = sem("proj")
        hs_ready = sem("hs_ready")
        based = sem("based")
        step = sem("step")
        block = ctx.enter_context(nc.Block())

        @block.sync
        def _(sp):
            for half in range(2):
                t = half * NT // 2
                sp.dma_start(s.x1[:, t:t + NT // 2, :], d.x[t * P:(t + NT // 2) * P, :].rearrange("(t p) c -> p t c", p=P)).then_inc(x_in[half], 16)
            for half in range(2):
                sp.wait_ge(x_in[half], 16)
            for b in range(3):
                sp.dma_start(s.adj[b][:, :], d.adj[b * P:(b + 1) * P, :]).then_inc(s.adj_in[b], 16)

            def store(i, b):
                sp.wait_ge(hs_ready, 2 * i + b + 1)
                sp.dma_start(d.table[bass.ds(i * (2 * P) + b * P, P), :], hs[b][:, 0:ROW]).then_inc(table_out[b], 16)
            tiles(sp, store)
            sp.wait_ge(based, NT)
            sp.dma_start(d.base[:, :].rearrange("(t p) c -> p t c", p=P), s.x1[:, :, :]).then_inc(s.base_out, 16)
            for b in range(2):
                sp.wait_ge(table_out[b], 16 * (NT // 2))

        @block.gpsimd
        def _(pool):
            for b in range(3):
                nc.gpsimd.memset(s.rows[b][:, :, :], 0.0)

        @block.scalar
        def _(act):
            for dst, src in ((wnat, d.w), (wcat[:, :, 0:C], d.wT), (wrT, d.wrT)):
                act.dma_start(dst[:, :, :], src[:, :].rearrange("(k p) n -> p k n", p=P)).then_inc(weights_in, 16)
            act.dma_start(ablk[:, :, :], d.ablk[:, :].rearrange("(k p) n -> p k n", p=P)).then_inc(weights_in, 16)
            act.dma_start(s.ident[:, :], d.ident[:, :]).then_inc(weights_in, 16)
            act.dma_start(be[:, :], d.be[:, :]).then_inc(small_in, 16)
            act.dma_start(br[:, :], d.br[:, :]).then_inc(small_in, 16)
            act.wait_ge(fold_ps, 1)
            act.wait_ge(weights_in, 80)
            nc.scalar.activation(wcat[:, :, C:C + 2 * GH], psW[:, :, :], ACT.Copy).then_inc(fold_sb, 1)
            act.wait_ge(varred, 1)
            nc.scalar.activation(var[:, :], var[:, :], ACT.Sqrt).then_inc(rooted, 1)

            def copy_x(t, b):
                act.wait_ge(xnT_ps, t + 1)
                if not zero(t) and not (b == 1 and isinstance(t, int)):
                    act.wait_ge(proj, t - 1)
                nc.scalar.activation(xnT[b][:, :, :].rearrange("p k n -> p (k n)"), psT[:, 0:C], ACT.Copy).then_inc(xnT_ready, 1)

            def copy_h(i, b):
                act.wait_ge(proj, 2 * i + b + 1)
                if not zero(i):
                    act.wait_ge(table_out[b], 16 * i)
                    act.wait_ge(based, 2 * i + b - 1)
                nc.scalar.activation(hs[b][:, :], psH[b][:, 0:ROW + GH], ACT.Copy).then_inc(hs_ready, 1)

            copy_x(0, 0)
            copy_x(1, 1)
            copy_h(0, 0)

            def both(i):
                copy_x(2 * i, 0)
                copy_h(i - 1, 1)
                copy_x(2 * i + 1, 1)
                copy_h(i, 0)
            rounds(act, both)
            copy_h(NT // 2 - 1, 1)

        @block.tensor
        def _(pe):
            pe.wait_ge(weights_in, 80)
            for k in range(KC):
                for o in range(KC):
                    last = nc.tensor.matmul(psW[:, k, :], wnat[:, o, k * P:(k + 1) * P], ablk[:, o, :],
                                            start=(o == 0), stop=(o == KC - 1), skip_group_check=True)
            last.then_inc(fold_ps, 1)
            pe.wait_ge(fold_sb, 1)

            def turn(t, b):
                pe.wait_ge(xn_ready, t + 1)
                if not zero(t):
                    pe.wait_ge(xnT_ready, t)
                for k in range(KC):
                    last = nc.tensor.transpose(psT[:, k * P:(k + 1) * P], xn[b][:, k * P:(k + 1) * P], s.ident[:, :])
                last.then_inc(xnT_ps, 1)

            def project(i, b):
                t = 2 * i + b
                pe.wait_ge(xnT_ready, t + 1)
                if not zero(i):
                    pe.wait_ge(hs_ready, t - 1)
                    pe.wait_ge(based, t - 1)
                for ps, w in ((psH[b], wcat), (psR[b], wrT)):
                    n = w.shape[2]
                    for k in range(KC):
                        last = nc.tensor.matmul(ps[:, 0:n], xnT[b][:, k, :], w[:, k, :], start=(k == 0), stop=(k == KC - 1))
                last.then_inc(proj, 1)

            turn(0, 0)
            turn(1, 1)
            project(0, 0)

            def both(i):
                turn(2 * i, 0)
                project(i - 1, 1)
                turn(2 * i + 1, 1)
                project(i, 0)
            rounds(pe, both)
            project(NT // 2 - 1, 1)

        @block.vector
        def _(dve):
            at = [0]

            def link(ins):
                at[0] += 1
                ins.then_inc(step, 1)
                dve.wait_ge(step, at[0])

            for half in range(2):
                dve.wait_ge(x_in[half], 16)
                for t in range(half * NT // 2, (half + 1) * NT // 2):
                    nc.vector.bn_stats(stats[:, t, :], s.x1[:, t, :]).then_inc(step, 1)
            at[0] += NT
            dve.wait_ge(step, at[0])
            spread(nc, link, stats, mean[:, :], diff[:, :], var[:, :], var[:, :], varred)
            dve.wait_ge(rooted, 1)
            link(nc.vector.reciprocal(rstd[:, :], var[:, :]))
            dve.wait_ge(small_in, 32)

            def norm(t, b):
                if not (isinstance(t, int) and t < 2):
                    dve.wait_ge(xnT_ps, t - 1)
                nc.vector.tensor_scalar(xn[b][:, :], s.x1[:, t, :], mean[:, bass.ds(t, 1)], rstd[:, bass.ds(t, 1)],
                                        ALU.subtract, ALU.mult).then_inc(xn_ready, 1)

            def base(t, b):
                dve.wait_ge(xn_ready, t + 1)
                nc.vector.tensor_tensor(s.x1[:, t, :], s.x1[:, t, :], br[:, :], ALU.add).then_inc(step, 1)
                dve.wait_ge(step, at[0] + t + 1)
                dve.wait_ge(hs_ready, t + 1)
                nc.vector.tensor_tensor(s.x1[:, t, :], s.x1[:, t, :], psR[b][:, 0:C], ALU.add)
                nc.vector.tensor_tensor(s.ssrc[:, t, :], hs[b][:, ROW:ROW + GH], be[:, :], ALU.add).then_inc(based, 1)

            norm(0, 0)
            norm(1, 1)
            with dve.Fori(0, NT // 2 - 1) as i:
                for b in range(2):
                    norm(2 * i + b + 2, b)
                    base(2 * i + b, b)
            for b in range(2):
                base(NT - 2 + b, b)


def build_crowded(s):
    def crowded(eng):
        return eng.value_load(s.crowded[0:1, 0:1], min_val=0, max_val=1)
    return crowded


def entries(nc, d, s):
    with ExitStack() as ctx:
        sb = lambda name, shape, dt=F32: ctx.enter_context(nc.sbuf_tensor(name, shape, dt))
        sem = lambda name: ctx.enter_context(nc.semaphore(name))
        iota = sb("iota", [P, CAND])
        qoff = sb("qoff", [P, CAND])
        cval = sb("cval", [P, CAND])
        cval2 = sb("cval2", [P, CAND])
        cidx = sb("cidx", [P, CAND], U32)
        cidf = sb("cidf", [P, CAND])
        pos = sb("pos", [P, SLOTS], U32)
        posf = sb("posf", [P, SLOTS])
        pick = sb("pick", [P, SLOTS, CAND])
        idf = sb("idf", [P, SLOTS])
        gone = sb("gone", [P, SLOTS])
        over = sb("over", [P, NT, Q4 + 1])
        overm = sb("overm", [P, 1])
        overall = sb("overall", [P, 1])
        best = [sb(f"best{b}", [P, SLOTS]) for b in range(3)]
        cols = [sb(f"cols{b}", [P, SLOTS], U32) for b in range(3)]
        z = [sb(f"z{b}", [P, SLOTS, GH]) for b in range(3)]
        vw = sb("vw", [P, SLOTS, GH])
        low = sb("low", [P, SLOTS])
        top = sb("top", [P, GH])
        total = sb("total", [P, GH])
        psA = ctx.enter_context(nc.psum_tensor("psA", [P, 512], F32))
        consts_in = sem("econsts_in")
        searched = sem("searched")
        named = sem("named")
        turn = sem("turn")
        gathered = [sem(f"gathered{b}") for b in range(3)]
        scored = sem("scored")
        raised = sem("raised")
        weighted = sem("weighted")
        summed = sem("summed")
        added = sem("added1")
        search_step = sem("search_step")
        weigh_step = sem("weigh_step")
        tick = sem("search_tick")
        over_one = sem("over_one")
        over_all = sem("over_all")
        block = ctx.enter_context(nc.Block())

        def threes(eng, body):
            for b in range(3):
                body(0, b)
            with eng.Fori(1, NT // 3) as i:
                for b in range(3):
                    body(i, b)
            for b in range(NT % 3):
                body(NT // 3, b)

        @block.sync
        def _(sp):
            for dst, src in ((s.we, d.we), (iota, d.iota), (qoff, d.qoff)):
                sp.dma_start(dst[:, :], src[:, :]).then_inc(consts_in, 16)

            def load(i, b):
                sp.wait_ge(searched, 3 * i + b - 2)
                sp.dma_start(s.adj[b][:, :], d.adj[bass.ds(i * (3 * P) + b * P, P), :]).then_inc(s.adj_in[b], 16)
            with sp.Fori(1, NT // 3) as i:
                for b in range(3):
                    load(i, b)
            for b in range(NT % 3):
                load(NT // 3, b)

        @block.gpsimd
        def _(pool):
            def gather(i, b):
                t = 3 * i + b
                if not zero(i):
                    pool.wait_ge(summed, t - 2)
                    pool.sem_inc(turn, 1)
                pool.wait_ge(named, t + 1)
                pool.sem_inc(turn, 1)
                for k in range(SLOTS):
                    pool.indirect_dma_start(s.rows[b][:, k, :], None, d.table[:, :],
                                            bass.IndirectOffsetOnAxis(cols[b][:, k:k + 1], 0),
                                            bounds_check=NP - 1, oob_is_err=False).then_inc(gathered[b], 16)
            threes(pool, gather)
            pool.wait_ge(over_one, 1)
            nc.gpsimd.partition_all_reduce(overall[:, :], overm[:, :], P, bass.bass_isa.ReduceOp.max).then_inc(over_all, 1)

        @block.scalar
        def _(act):
            def raise_(i, b):
                act.wait_ge(scored, 3 * i + b + 1)
                nc.scalar.activation(z[b][:, :, :], z[b][:, :, :], ACT.Exp).then_inc(raised, 1)
            threes(act, raise_)

        @block.tensor
        def _(pe):
            def add_up(i, b):
                pe.wait_ge(added, 3 * i + b + 1)
                pe.wait_ge(weighted, 3 * i + b + 1)
                for k in range(SLOTS):
                    last = nc.tensor.matmul(psA[:, 0:C], s.ident[:, :], s.rows[b][:, k, 0:C], start=(k == 0), stop=(k == SLOTS - 1))
                last.then_inc(summed, 1)
            threes(pe, add_up)

        @block.vector
        def _(dve):
            nc.vector.memset(gone[:, :], 0.0).then_inc(added, 1)
            dve.wait_ge(added, 1)
            SEARCH, WEIGH = 15, 9

            def step(i, b, search=True, weigh=True):
                t = 3 * i + b
                o, ob, oi = t - 2, (b + 1) % 3, i if b == 2 else i - 1
                values, older = best[b], best[ob]

                def found(k):
                    dve.wait_ge(search_step, SEARCH * t + k)

                def weighed(k):
                    dve.wait_ge(weigh_step, WEIGH * o + k)

                if search:
                    if not zero(t):
                        dve.wait_ge(named, t)
                    if not zero(i):
                        dve.wait_ge(gathered[b], 16 * SLOTS * i)
                        dve.wait_ge(weighted, t - 2)
                    dve.wait_ge(s.adj_in[b], 16 * (i + 1))
                    dve.sem_inc(tick, 1)
                    for q in range(Q4):
                        nc.vector.max(cval[:, 8 * q:8 * q + 8], s.adj[b][:, q * QW:(q + 1) * QW]).then_inc(search_step, 1)
                    found(4)
                    nc.vector.tensor_copy(over[:, t, 0:Q4], cval[:, :].rearrange("p (q e) -> p q e", e=8)[:, :, 7])
                    for q in range(Q4):
                        ins = nc.vector.max_index(cidx[:, 8 * q:8 * q + 8], cval[:, 8 * q:8 * q + 8], s.adj[b][:, q * QW:(q + 1) * QW])
                    ins.then_inc(searched, 1)
                    nc.vector.max(values[:, 0:8], cval[:, :]).then_inc(search_step, 1)
                if weigh:
                    zb = z[ob][:, :, :]
                    zh = zb.rearrange("p s h -> p h s")
                    each = lambda a: a.unsqueeze(1).to_broadcast([P, SLOTS, GH])
                    slot = lambda a: a.unsqueeze(2).to_broadcast([P, SLOTS, GH])
                    if not zero(o):
                        dve.wait_ge(weighted, o)
                    nc.vector.tensor_scalar(low[:, :], older[:, :], 0.0, LOW, ALU.is_le, ALU.mult)
                    nc.vector.tensor_tensor(vw[:, :, :], slot(older[:, :]), each(s.we[:, :]), ALU.mult).then_inc(weigh_step, 1)
                if search:
                    found(5)
                    nc.vector.tensor_scalar(gone[:, 0:8], values[:, 0:8], 0.0, FAR, ALU.is_le, ALU.mult)
                    nc.vector.match_replace(cval2[:, :], values[:, 0:8], cval[:, :], -3e38).then_inc(search_step, 1)
                    nc.vector.max_index(pos[:, 0:8], values[:, 0:8], cval[:, :]).then_inc(search_step, 1)
                if weigh:
                    dve.wait_ge(gathered[ob], 16 * SLOTS * (oi + 1))
                    nc.vector.tensor_tensor(zb, s.rows[ob][:, :, C:ROW], each(s.ssrc[:, bass.ds(o, 1), :].rearrange("p a h -> p (a h)")), ALU.add).then_inc(weigh_step, 1)
                if search:
                    found(7)
                    nc.vector.tensor_copy(posf[:, 0:8], pos[:, 0:8]).then_inc(search_step, 1)
                    nc.vector.max(values[:, 8:16], cval2[:, :]).then_inc(search_step, 1)
                if weigh:
                    weighed(2)
                    nc.vector.tensor_tensor(zb, zb, vw[:, :, :], ALU.add).then_inc(weigh_step, 1)
                if search:
                    found(9)
                    nc.vector.tensor_scalar(gone[:, 8:16], values[:, 8:16], 0.0, FAR, ALU.is_le, ALU.mult)
                    nc.vector.max_index(pos[:, 8:16], values[:, 8:16], cval2[:, :]).then_inc(search_step, 1)
                if weigh:
                    weighed(3)
                    nc.vector.scalar_tensor_tensor(zb, zb, 0.2, zb, ALU.mult, ALU.max).then_inc(weigh_step, 1)
                if search:
                    if zero(t):
                        dve.wait_ge(consts_in, 48)
                    found(10)
                    nc.vector.tensor_copy(posf[:, 8:16], pos[:, 8:16]).then_inc(search_step, 1)
                    nc.vector.tensor_tensor(cidf[:, :], cidx[:, :], qoff[:, :], ALU.add).then_inc(search_step, 1)
                if weigh:
                    weighed(4)
                    nc.vector.tensor_tensor(zb, zb, slot(low[:, :]), ALU.add).then_inc(weigh_step, 1)
                if search:
                    wide = [P, SLOTS, CAND]
                    found(12)
                    nc.vector.tensor_tensor(pick[:, :, :], iota[:, :].unsqueeze(1).to_broadcast(wide),
                                            posf[:, :].unsqueeze(2).to_broadcast(wide), ALU.is_equal).then_inc(search_step, 1)
                if weigh:
                    weighed(5)
                    nc.vector.tensor_reduce(top[:, :], zh, AX_X, ALU.max).then_inc(weigh_step, 1)
                if search:
                    found(13)
                    nc.vector.tensor_tensor(pick[:, :, :], pick[:, :, :], cidf[:, :].unsqueeze(1).to_broadcast(wide), ALU.mult).then_inc(search_step, 1)
                if weigh:
                    weighed(6)
                    nc.vector.tensor_tensor(zb, zb, each(top[:, :]), ALU.subtract).then_inc(scored, 1)
                if search:
                    found(14)
                    nc.vector.tensor_reduce(idf[:, :], pick[:, :, :], AX_X, ALU.add).then_inc(search_step, 1)
                if weigh:
                    dve.wait_ge(raised, o + 1)
                    nc.vector.tensor_reduce(total[:, :], zh, AX_X, ALU.add).then_inc(weigh_step, 1)
                if search:
                    found(15)
                    nc.vector.tensor_tensor(cols[b][:, :], idf[:, :], gone[:, :], ALU.add).then_inc(named, 1)
                    nc.vector.tensor_copy(over[:, t, Q4:Q4 + 1], values[:, SLOTS - 1:SLOTS])
                if weigh:
                    weighed(7)
                    nc.vector.reciprocal(total[:, :], total[:, :]).then_inc(weigh_step, 1)
                    weighed(8)
                    nc.vector.tensor_tensor(zb, zb, each(total[:, :]), ALU.mult).then_inc(weigh_step, 1)
                    h = s.rows[ob][:, :, 0:C].rearrange("p s (h d) -> p s h d", d=GD)
                    weighed(9)
                    nc.vector.tensor_tensor(h, h, zb.unsqueeze(3).to_broadcast([P, SLOTS, GH, GD]), ALU.mult).then_inc(weighted, 1)

            def add(t):
                dve.wait_ge(summed, t + 1)
                nc.vector.tensor_tensor(s.x1[:, t, :], s.x1[:, t, :], psA[:, 0:C], ALU.add).then_inc(added, 1)
                dve.wait_ge(added, t + 2)
                dve.sem_inc(tick, 1)
                nc.vector.bn_stats(s.stats[:, t, :], s.x1[:, t, :])

            step(0, 0, weigh=False)
            step(0, 1, weigh=False)
            step(0, 2)
            step(1, 0)
            dve.wait_ge(s.base_out, 16)
            dve.sem_inc(tick, 1)
            add(0)
            step(1, 1)
            add(1)
            step(1, 2)
            add(2)
            with dve.Fori(2, NT // 3) as i:
                for b in range(3):
                    step(i, b)
                    add(3 * i + b - 3)
            for t in range(NT // 3 * 3, NT + 2):
                step(t // 3, t % 3, search=t < NT)
                add(t - 3)
            nc.vector.tensor_reduce(overm[:, :], over[:, :, :].rearrange("p t q -> p (t q)"), AX_X, ALU.max).then_inc(over_one, 1)
            add(NT - 1)
            dve.wait_ge(over_all, 1)
            nc.vector.tensor_scalar(s.crowded[:, :], overall[:, :], 0.0, None, ALU.is_gt)


def general(nc, d, s):
    with ExitStack() as ctx:
        sb = lambda name, shape, dt=F32: ctx.enter_context(nc.sbuf_tensor(name, shape, dt))
        sem = lambda name: ctx.enter_context(nc.semaphore(name))
        row = sb("grow", [P, NP])
        rows = sb("grows", [P, 8, ROW])
        best = sb("gbest", [P, 8])
        found = sb("gfound", [P, 8], U32)
        foundf = sb("gfoundf", [P, 8])
        cols = sb("gcols", [P, 8], U32)
        low, there = sb("glow", [P, 8]), sb("gthere", [P, 8])
        z = sb("gz", [P, 9, GH])
        peak, newpeak, total, part = (sb(n, [P, GH]) for n in ("gpeak", "gnewpeak", "gtotal", "gpart"))
        acc, add = sb("gacc", [P, C]), sb("gadd", [P, C])
        row_in = sem("grow_in")
        base_in = sem("gbase_in")
        crowded = build_crowded(s)
        found_ready = sem("gfound_ready")
        tick = sem("gtick")
        ptick = sem("gptick")
        gathered = sem("ggathered")
        scored = sem("gscored")
        raised = sem("graised")
        tiled = sem("gtiled")
        step = sem("ggstep")
        block = ctx.enter_context(nc.Block())

        @block.sync
        def _(sp):
            with sp.If(crowded(sp) > 0):
                sp.dma_start(s.x1[:, :, :], d.base[:, :].rearrange("(t p) c -> p t c", p=P)).then_inc(base_in, 16)
                with sp.Fori(0, NT) as t:
                    sp.wait_ge(tiled, t + 1)
                    sp.dma_start(row[:, :], d.adj[bass.ds(t * P, P), :]).then_inc(row_in, 16)

        @block.gpsimd
        def _(pool):
            with pool.If(crowded(pool) > 0):
                with pool.Fori(0, NT * ROUNDS) as n:
                    pool.wait_ge(found_ready, n + 1)
                    pool.sem_inc(ptick, 1)
                    for k in range(8):
                        pool.indirect_dma_start(rows[:, k, :], None, d.table[:, :],
                                                bass.IndirectOffsetOnAxis(cols[:, k:k + 1], 0),
                                                bounds_check=NP - 1, oob_is_err=False).then_inc(gathered, 16)

        @block.scalar
        def _(act):
            with act.If(crowded(act) > 0):
                with act.Fori(0, NT * ROUNDS) as n:
                    act.wait_ge(scored, n + 1)
                    nc.scalar.activation(z[:, :, :], z[:, :, :], ACT.Exp).then_inc(raised, 1)

        @block.vector
        def _(dve):
            with dve.If(crowded(dve) > 0):
                nc.vector.memset(rows[:, :, :], 0.0).then_inc(tiled, 1)
                dve.wait_ge(base_in, 16)
                dve.sem_inc(tick, 1)
                PER, TILE = 24, 6
                with dve.Fori(0, NT) as t:
                    def link(k, ins):
                        ins.then_inc(step, 1)
                        dve.wait_ge(step, t * (PER * ROUNDS + TILE) + (PER * ROUNDS if k > 3 else 0) + k)

                    dve.wait_ge(tiled, t + 1)
                    link(1, nc.vector.memset(peak[:, :], LOW))
                    link(2, nc.vector.memset(total[:, :], 0.0))
                    link(3, nc.vector.memset(acc[:, :], 0.0))
                    dve.wait_ge(row_in, 16 * (t + 1))
                    dve.sem_inc(tick, 1)
                    with dve.Fori(0, ROUNDS) as r:
                        now = [0]

                        def chain(ins):
                            now[0] += 1
                            ins.then_inc(step, 1)
                            dve.wait_ge(step, t * (PER * ROUNDS + TILE) + 3 + PER * r + now[0])
                            dve.sem_inc(tick, 1)

                        n = t * ROUNDS + r
                        zs = z[:, 0:8, :]
                        zh = zs.rearrange("p s h -> p h s")
                        h = rows[:, :, 0:C]
                        each = lambda a: a.unsqueeze(1).to_broadcast([P, 8, GH])
                        slot = lambda a: a.unsqueeze(2).to_broadcast([P, 8, GH])
                        chain(nc.vector.max(best[:, :], row[:, :]))
                        chain(nc.vector.max_index(found[:, :], best[:, :], row[:, :]))
                        chain(nc.vector.match_replace(row[:, :], best[:, :], row[:, :], -3e38))
                        chain(nc.vector.tensor_scalar(low[:, :], best[:, :], 0.0, FAR, ALU.is_le, ALU.mult))
                        chain(nc.vector.tensor_copy(foundf[:, :], found[:, :]))
                        nc.vector.tensor_tensor(cols[:, :], foundf[:, :], low[:, :], ALU.add).then_inc(found_ready, 1)
                        dve.wait_ge(found_ready, n + 1)
                        chain(nc.vector.tensor_scalar(low[:, :], best[:, :], 0.0, LOW, ALU.is_le, ALU.mult))
                        chain(nc.vector.tensor_scalar(there[:, :], best[:, :], 0.0, None, ALU.is_gt))
                        chain(nc.vector.tensor_tensor(zs, slot(best[:, :]), each(s.we[:, :]), ALU.mult))
                        dve.wait_ge(gathered, 128 * (n + 1))
                        chain(nc.vector.tensor_tensor(rows[:, :, C:ROW], rows[:, :, C:ROW], each(s.ssrc[:, t, :]), ALU.add))
                        chain(nc.vector.tensor_tensor(zs, zs, rows[:, :, C:ROW], ALU.add))
                        chain(nc.vector.scalar_tensor_tensor(zs, zs, 0.2, zs, ALU.mult, ALU.max))
                        chain(nc.vector.tensor_tensor(zs, zs, slot(low[:, :]), ALU.add))
                        chain(nc.vector.tensor_reduce(newpeak[:, :], zh, AX_X, ALU.max))
                        chain(nc.vector.tensor_tensor(newpeak[:, :], newpeak[:, :], peak[:, :], ALU.max))
                        chain(nc.vector.tensor_tensor(zs, zs, each(newpeak[:, :]), ALU.subtract))
                        nc.vector.tensor_tensor(z[:, 8, :], peak[:, :], newpeak[:, :], ALU.subtract).then_inc(scored, 1)
                        dve.wait_ge(raised, n + 1)
                        chain(nc.vector.tensor_copy(peak[:, :], newpeak[:, :]))
                        chain(nc.vector.tensor_tensor(zs, zs, slot(there[:, :]), ALU.mult))
                        chain(nc.vector.tensor_reduce(part[:, :], zh, AX_X, ALU.add))
                        chain(nc.vector.tensor_tensor(total[:, :], total[:, :], z[:, 8, :], ALU.mult))
                        chain(nc.vector.tensor_tensor(total[:, :], total[:, :], part[:, :], ALU.add))
                        chain(nc.vector.tensor_tensor(h.rearrange("p s (h d) -> p s h d", d=GD), h.rearrange("p s (h d) -> p s h d", d=GD),
                                                      zs.unsqueeze(3).to_broadcast([P, 8, GH, GD]), ALU.mult))
                        ac = acc[:, :].rearrange("p (h d) -> p h d", d=GD)
                        chain(nc.vector.tensor_tensor(ac, ac, z[:, 8, :].unsqueeze(2).to_broadcast([P, GH, GD]), ALU.mult))
                        chain(nc.vector.tensor_reduce(add[:, :], h.rearrange("p s c -> p c s"), AX_X, ALU.add))
                        chain(nc.vector.tensor_tensor(acc[:, :], acc[:, :], add[:, :], ALU.add))
                        assert now[0] == PER, now
                    link(4, nc.vector.reciprocal(total[:, :], total[:, :]))
                    ac = acc[:, :].rearrange("p (h d) -> p h d", d=GD)
                    link(5, nc.vector.tensor_tensor(ac, ac, total[:, :].unsqueeze(2).to_broadcast([P, GH, GD]), ALU.mult))
                    link(6, nc.vector.tensor_tensor(s.x1[:, t, :], s.x1[:, t, :], acc[:, :], ALU.add))
                    dve.sem_inc(tick, 1)
                    nc.vector.bn_stats(s.stats[:, t, :], s.x1[:, t, :]).then_inc(tiled, 1)


def qkv(nc, d, s):
    with ExitStack() as ctx:
        sb = lambda name, shape, dt=F32: ctx.enter_context(nc.sbuf_tensor(name, shape, dt))
        pb = lambda name: ctx.enter_context(nc.psum_tensor(name, [P, 512], F32))
        sem = lambda name: ctx.enter_context(nc.semaphore(name))
        wqkvT = sb("wqkvT", [P, KC, QKV])
        ln1 = sb("ln1", [P, C])
        cos = sb("cos", [P, NT, HD])
        sin = sb("sin", [P, NT, HD])
        mean, diff, raw, var, rstd, rrms = (sb(n, [P, NT]) for n in ("qmean", "qdiff", "qraw", "qvar", "qrstd", "qrrms"))
        hn = [sb(f"hn{b}", [P, C]) for b in range(2)]
        hT = [sb(f"hT{b}", [P, KC, P]) for b in range(2)]
        qk = [sb(f"qk{b}", [P, QKV]) for b in range(2)]
        rot = [sb(f"rot{b}", [P, NQK, HD]) for b in range(2)]
        cross = sb("cross", [P, NQK, HD])
        kplain = sb("kplain", [P, P])
        psT, psQ, psK = pb("qpsT"), pb("qpsQ"), pb("qpsK")
        consts_in = sem("consts_in")
        varred = sem("qvarred")
        rooted = sem("qrooted")
        normed = sem("normed")
        meaned = sem("meaned")
        step = sem("qstep")
        hn_ready = sem("hn_ready")
        hT_ps = sem("hT_ps")
        hT_ready = sem("hT_ready")
        qkv_ps = sem("qkv_ps")
        qk_ready = sem("qk_ready")
        turned = sem("turned")
        qkT_ps = sem("qkT_ps")
        stored = sem("stored")
        k_split = sem("k_split")
        block = ctx.enter_context(nc.Block())

        def lagged(eng, one, two, three):
            def both(i):
                for b in range(2):
                    one(2 * i + b + 1, 1 - b)
                    two(2 * i + b, b)
                    three(2 * i + b - 1, 1 - b)

            one(0, 0)
            one(1, 1)
            two(0, 0)
            one(2, 0)
            two(1, 1)
            three(0, 0)
            both(1)
            with eng.Fori(2, NT // 2 - 1) as i:
                both(i)
            one(NT - 1, 1)
            two(NT - 2, 0)
            three(NT - 3, 1)
            two(NT - 1, 1)
            three(NT - 2, 0)
            three(NT - 1, 1)

        @block.gpsimd
        def _(pool):
            with pool.Fori(0, NT) as t:
                at = bass.ds(t * P, P)
                pool.wait_ge(stored, t + 1)
                pool.sem_inc(s.turn, 1)
                for x in range(2):
                    r = slice(64 * x, 64 * x + 64)
                    nc.gpsimd.tensor_copy(s.kT[x][r, at], kplain[r, :]).then_inc(k_split, 1)
                pool.wait_ge(k_split, 4 * t + 2)
                pool.sem_inc(s.turn, 1)
                for x in range(2):
                    r = slice(64 * x, 64 * x + 64)
                    nc.gpsimd.tensor_tensor(s.kT[x][64 - 64 * x:128 - 64 * x, at], kplain[r, :],
                                            s.kT[x][r, at].bitcast(F32), ALU.subtract).then_inc(k_split, 1)

        @block.sync
        def _(sp):
            sp.dma_start(wqkvT[:, :, :], d.wqkvT[:, :].rearrange("(k p) n -> p k n", p=P)).then_inc(consts_in, 16)
            sp.dma_start(ln1[:, :], d.ln1[:, :]).then_inc(consts_in, 16)
            sp.dma_start(cos[:, :, :], d.cos[:, :].rearrange("(t p) n -> p t n", p=P)).then_inc(consts_in, 16)
            sp.dma_start(sin[:, :, :], d.sin[:, :].rearrange("(t p) n -> p t n", p=P)).then_inc(consts_in, 16)

        @block.scalar
        def _(act):
            act.wait_ge(varred, 1)
            nc.scalar.activation(var[:, :], var[:, :], ACT.Sqrt).then_inc(rooted, 1)
            act.wait_ge(meaned, 1)
            nc.scalar.activation(rrms[:, :], rrms[:, :], ACT.Sqrt).then_inc(rooted, 1)

            def copy_x(t, b):
                act.wait_ge(hT_ps, t + 1)
                if not isinstance(t, int) or t >= 2:
                    act.wait_ge(qkv_ps, t - 1)
                nc.scalar.activation(hT[b][:, :, :].rearrange("p k n -> p (k n)"), psT[:, 0:C], ACT.Copy).then_inc(hT_ready, 1)

            def copy_qkv(t, b):
                act.wait_ge(qkv_ps, t + 1)
                if not isinstance(t, int) or t >= 2:
                    act.wait_ge(turned, t - 1)
                nc.scalar.activation(qk[b][:, :], psQ[:, :], ACT.Copy).then_inc(qk_ready, 1)

            def store(t, b):
                act.wait_ge(qkT_ps, t + 1)
                nc.scalar.activation(s.qT[:, :, bass.ds(t * P, P)], psK[:, 0:2 * P].rearrange("p (a n) -> p a n", a=2), ACT.Copy)
                if not zero(t):
                    act.wait_ge(k_split, 4 * t)
                nc.scalar.activation(kplain[:, :], psK[:, 2 * P:3 * P], ACT.Copy).then_inc(stored, 1)

            lagged(act, copy_x, copy_qkv, store)

        @block.tensor
        def _(pe):
            pe.wait_ge(consts_in, 64)

            def turn_x(t, b):
                pe.wait_ge(hn_ready, t + 1)
                if not zero(t):
                    pe.wait_ge(hT_ready, t)
                for k in range(KC):
                    last = nc.tensor.transpose(psT[:, k * P:(k + 1) * P], hn[b][:, k * P:(k + 1) * P], s.ident[:, :])
                last.then_inc(hT_ps, 1)

            def project(t, b):
                pe.wait_ge(hT_ready, t + 1)
                if not zero(t):
                    pe.wait_ge(qk_ready, t)
                for k in range(KC):
                    last = nc.tensor.matmul(psQ[:, :], hT[b][:, k, :], wqkvT[:, k, :], start=(k == 0), stop=(k == KC - 1))
                last.then_inc(qkv_ps, 1)

            def turn_qk(t, b):
                pe.wait_ge(turned, t + 1)
                if not zero(t):
                    pe.wait_ge(stored, t)
                for k in range(3):
                    last = nc.tensor.transpose(psK[:, k * P:(k + 1) * P],
                                               rot[b][:, 2 * k:2 * k + 2, :].rearrange("p a n -> p (a n)"), s.ident[:, :])
                last.then_inc(qkT_ps, 1)

            lagged(pe, turn_x, project, turn_qk)

        @block.vector
        def _(dve):
            at = [0]

            def link(ins):
                at[0] += 1
                ins.then_inc(step, 1)
                dve.wait_ge(step, at[0])

            nc.vector.memset(s.v[:, :, :, HD:HD + 1], 1.0)
            spread(nc, link, s.stats, mean[:, :], diff[:, :], raw[:, :], var[:, :], varred)
            dve.wait_ge(rooted, 1)
            link(nc.vector.reciprocal(rstd[:, :], var[:, :]))
            link(nc.vector.tensor_tensor(raw[:, :], raw[:, :], rstd[:, :], ALU.mult))
            link(nc.vector.tensor_tensor(raw[:, :], raw[:, :], rstd[:, :], ALU.mult))
            nc.vector.tensor_scalar(rrms[:, :], raw[:, :], EPS_RMS, None, ALU.add).then_inc(meaned, 1)
            dve.wait_ge(rooted, 2)
            link(nc.vector.reciprocal(rrms[:, :], rrms[:, :]))
            dve.wait_ge(consts_in, 64)
            base = at[0]
            PER = 3

            def scale(t, b):
                nc.vector.tensor_scalar(s.x2[:, t, :], s.x1[:, t, :], mean[:, bass.ds(t, 1)], rstd[:, bass.ds(t, 1)],
                                        ALU.subtract, ALU.mult).then_inc(normed, 1)
                dve.wait_ge(normed, t + 1)
                if not isinstance(t, int) or t >= 2:
                    dve.wait_ge(hT_ps, t - 1)
                nc.vector.scalar_tensor_tensor(hn[b][:, :], s.x2[:, t, :], rrms[:, bass.ds(t, 1)], ln1[:, :],
                                               ALU.mult, ALU.mult).then_inc(hn_ready, 1)

            def rope(i, b):
                t = 2 * i + b
                now = [0]

                def chain(ins, wait=True):
                    now[0] += 1
                    ins.then_inc(step, 1)
                    if wait:
                        dve.wait_ge(step, base + PER * t + now[0])

                dve.wait_ge(qk_ready, t + 1)
                if not (isinstance(i, int) and i == 0):
                    dve.wait_ge(qkT_ps, t - 1)
                src = qk[b][:, 0:NQK * HD].rearrange("p (a n) -> p a n", n=HD)
                half = HD // 2
                wide = lambda a, n: a.unsqueeze(1).to_broadcast([P, NQK, n])
                nc.vector.tensor_copy(s.v[:, t, :, 0:HD], qk[b][:, NQK * HD:QKV].rearrange("p (a n) -> p a n", n=HD))
                chain(nc.vector.tensor_tensor(rot[b][:, :, :], src, wide(cos[:, t, :], HD), ALU.mult), False)
                chain(nc.vector.tensor_tensor(cross[:, :, 0:half], src[:, :, half:HD], wide(sin[:, t, 0:half], half), ALU.mult), False)
                chain(nc.vector.tensor_tensor(cross[:, :, half:HD], src[:, :, 0:half], wide(sin[:, t, half:HD], half), ALU.mult))
                nc.vector.tensor_tensor(rot[b][:, :, :], rot[b][:, :, :], cross[:, :, :], ALU.add).then_inc(turned, 1)
                dve.wait_ge(turned, t + 1)
                assert now[0] == PER

            def both(i):
                for b in range(2):
                    scale(2 * i + b + 2, b)
                    rope(i, b)

            scale(0, 0)
            scale(1, 1)
            both(0)
            with dve.Fori(1, NT // 2 - 1) as i:
                both(i)
            for b in range(2):
                rope(NT // 2 - 1, b)


def attend(nc, d, s):
    with ExitStack() as ctx:
        sb = lambda name, shape, dt=F32: ctx.enter_context(nc.sbuf_tensor(name, shape, dt))
        pb = lambda name: ctx.enter_context(nc.psum_tensor(name, [P, 512], F32))
        sem = lambda name: ctx.enter_context(nc.semaphore(name))
        PAIRS = NT // 2
        W = 2 * P
        mask, maskT = sb("mask", [P, P]), sb("maskT", [P, P])
        maskR, maskTR = sb("maskR", [P, P], F32R), sb("maskTR", [P, P], F32R)
        identR, ones = sb("identR", [P, P], F32R), sb("ones", [P, P], F32R)
        woT = sb("woT", [P, KC, C])
        q = [[[sb(f"q{v}{x}{m}", [P, 2, W], F32R) for m in range(2)] for x in range(2)] for v in range(2)]
        kb = [sb(f"kblock{a}", [P, P], F32R) for a in range(4)]
        cand = [sb(f"cand{v}", [P, 2, 2, 2, PAIRS]) for v in range(2)]
        top = sb("atop", [P, 2, 4])
        diag = [sb(f"diag{x}", [P, 4, P], F32R) for x in range(2)]
        level = [sb(f"level{x}", [P, 2 * W]) for x in range(2)]
        pT = [sb(f"pT{a}", [P, 2, W]) for a in range(4)]
        part = sb("apart", [P, 2, 4])
        y = sb("y", [P, 2, C])
        yT = sb("yT", [P, 2, C])
        square = sb("square", [P, C])
        zeros = sb("zeros", [P, ZW])
        psM, psS, psO = ([pb(f"ps{n}{x}") for x in range(2)] for n in "MSO")
        psY, psZ = pb("psY"), pb("psZ")
        consts_in = sem("aconsts_in")
        rounded = sem("rounded")
        high_ready = sem("high_ready")
        q_ready = sem("q_ready")
        k_ready = [sem(f"k_ready{a}") for a in range(4)]
        m_ps = [sem(f"m_ps{x}") for x in range(2)]
        m_out = [sem(f"m_out{x}") for x in range(2)]
        topped = sem("topped")
        drawn = sem("drawn")
        level_ps = sem("level_ps")
        leveled = sem("leveled")
        s_ps = [sem(f"s_ps{a}") for a in range(4)]
        s_out = [sem(f"s_out{a}") for a in range(4)]
        p_ready = [sem(f"p_ready{a}") for a in range(4)]
        pv = [sem(f"pv{a}") for a in range(4)]
        inverted = sem("inverted")
        o_out = sem("o_out")
        yT_ps = sem("yT_ps")
        yT_ready = sem("yT_ready")
        z_ps = sem("z_ps")
        z_out = sem("z_out")
        squared = sem("squared")
        zeroed = sem("zeroed")
        blank = sem("blank")
        turn = sem("aturn")
        block = ctx.enter_context(nc.Block())

        def items(i, b):
            return (2 * i + 1) * (i + b)

        def after(i, b):
            return (i, 1) if b == 0 else (i + 1, 0)

        def whole(eng, body):
            body(0, 0)
            body(0, 1)
            with eng.Fori(1, PAIRS // 2 - 1) as i:
                for b in range(2):
                    body(i, b)
            body(PAIRS // 2 - 1, 0)
            body(PAIRS // 2 - 1, 1)
            body(PAIRS // 2, 0)

        def short(u, left):
            return isinstance(u, int) and PAIRS - 1 - u <= left

        def others(eng, u, item, first=None):
            if not zero(u):
                (first or item)(1, 0, u)
            if not isinstance(u, int) or u >= 2:
                with eng.Fori(1, u) as j:
                    item(1 + j, j, j - 1)

        @block.sync
        def _(sp):
            sp.dma_start(mask[:, :], d.mask[:, :]).then_inc(consts_in, 16)
            sp.dma_start(maskT[:, :], d.maskT[:, :]).then_inc(consts_in, 16)
            sp.dma_start(woT[:, :, :], d.woT[:, :].rearrange("(k p) n -> p k n", p=P)).then_inc(consts_in, 16)
            sp.wait_ge(zeroed, 1)
            flatlist = d.list_x[:, :].rearrange("(p a) c -> p (a c)", p=P)
            for k in range(LIST * C // ZW):
                sp.dma_start(flatlist[:, k * ZW:(k + 1) * ZW], zeros[:, :]).then_inc(blank, 16)
            sp.wait_ge(blank, 16 * (LIST * C // ZW))

        @block.gpsimd
        def _(pool):
            def keys(n, pair):
                for a in range(4):
                    if not zero(n):
                        pool.wait_ge(s_ps[a], n)
                        pool.sem_inc(turn, 1)
                    nc.gpsimd.tensor_copy(kb[a][:, :], s.kT[a % 2][:, bass.ds(pair * W + a // 2 * P, P)]).then_inc(k_ready[a], 1)

            def queries(i, b):
                w = 2 * i + b
                for other, x in ((0, 0), (0, 1), (1, 0), (1, 1)):
                    if x == 0:
                        pool.wait_ge(high_ready, 4 * w + 2 * other + 2)
                        pool.sem_inc(turn, 1)
                    m = x ^ other
                    src = s.qT[64 * x:64 * x + 64, :, bass.ds(w * W, W)]
                    high = q[b][x][x][64 * x:64 * x + 64, :, :].bitcast(F32)
                    nc.gpsimd.tensor_tensor(q[b][x][m][64 - 64 * m:128 - 64 * m, :, :], src, high, ALU.subtract).then_inc(q_ready, 1)
                pool.wait_ge(q_ready, 4 * w + 4)
                pool.sem_inc(turn, 1)

            nc.gpsimd.memset(zeros[:, :], 0.0).then_inc(zeroed, 1)
            pool.wait_ge(zeroed, 1)
            queries(0, 0)

            def pair_of_tiles(i, b):
                u, n = 2 * i + b, items(i, b)
                keys(n, u)
                if not short(u, 0):
                    for a in range(4):
                        pool.wait_ge(k_ready[a], n + 1)
                    pool.sem_inc(turn, 1)
                    queries(*after(i, b))
                others(pool, u, lambda k, pair, before: keys(n + k, pair))
            whole(pool, pair_of_tiles)

        @block.tensor
        def _(pe):
            pe.wait_ge(consts_in, 48)
            pe.wait_ge(rounded, 6)

            def measure(i, b, k, pair, own, t, x):
                n = 2 * items(i, b) + k
                if not zero(n):
                    pe.wait_ge(m_out[x], n)
                keys = P if own and t == 0 else W
                for h in range(2):
                    last = nc.tensor.matmul(psM[x][:, h * W:h * W + keys], q[b][x][x][:, h, t * P:(t + 1) * P],
                                            s.kT[x][:, bass.ds(pair * W, keys)], start=(h == 0), stop=not own, skip_group_check=True)
                if own:
                    for h in range(2):
                        last = nc.tensor.matmul(psM[x][:, h * W + keys - P:h * W + keys], identR[:, :], maskR[:, :],
                                                start=False, stop=True, skip_group_check=True)
                last.then_inc(m_ps[x], 1)

            def spread_level(u):
                for x in range(2):
                    pe.wait_ge(drawn, 2 * u + x + 1)
                    last = nc.tensor.matmul(psM[x][:, :], ones[:, :], diag[x][:, :, :].rearrange("p a n -> p (a n)"),
                                            start=True, stop=True)
                    last.then_inc(level_ps, 1)

            def scores(u, b, n, own, a):
                x = a % 2
                pe.wait_ge(k_ready[a], n + 1)
                if own and a == 0:
                    pe.wait_ge(q_ready, 4 * u + 4)
                if a >= 2:
                    pe.wait_ge(s_out[x], n + 1)
                elif not zero(n):
                    pe.wait_ge(s_out[2 + x], n)
                w = slice(P, W) if own and a >= 2 else slice(0, W)
                out = psS[x][:, :].rearrange("p (h n) -> p h n", h=2)[:, :, w]
                for m in range(2):
                    last = nc.tensor.matmul(out, kb[a][:, :], q[b][x][m][:, :, w],
                                            start=(m == 0), stop=(m == 1 and not own), skip_group_check=True)
                if own:
                    o = P if a < 2 else 0
                    for h in range(2):
                        last = nc.tensor.matmul(psS[x][:, h * W + w.start:h * W + w.start + P], identR[:, :], maskTR[:, :],
                                                start=False, stop=True, skip_group_check=True)
                last.then_inc(s_ps[a], 1)

            def clear_output(u):
                if not zero(u):
                    pe.wait_ge(o_out, u)
                for t in range(2):
                    nc.tensor.matmul(psO[t][:, 510:512], ones[:, :], ones[:, 0:2], start=True, stop=True)

            def times_v(n, pair, a):
                x = a % 2
                pe.wait_ge(p_ready[a], n + 1)
                for t in range(2):
                    for h in range(2):
                        o = (2 * h + x) * (HD + 1)
                        last = nc.tensor.matmul(psO[t][:, o:o + HD + 1], pT[a][:, h, t * P:(t + 1) * P],
                                                s.v[:, bass.ds(2 * pair + a // 2, 1), x, :].rearrange("p a n -> p (a n)"),
                                                start=False, stop=False, skip_group_check=True)
                last.then_inc(pv[a], 1)

            def turn_y(u):
                pe.wait_ge(o_out, u + 1)
                for t in range(2):
                    for k in range(KC):
                        last = nc.tensor.transpose(psY[:, (2 * t + k) * P:(2 * t + k + 1) * P], y[:, t, k * P:(k + 1) * P], s.ident[:, :])
                last.then_inc(yT_ps, 1)

            def times_wo(u):
                pe.wait_ge(yT_ready, u + 1)
                if not zero(u):
                    pe.wait_ge(z_out, u)
                for t in range(2):
                    for k in range(KC):
                        last = nc.tensor.matmul(psZ[:, t * C:(t + 1) * C], yT[:, t, k * P:(k + 1) * P], woT[:, k, :],
                                                start=(k == 0), stop=(k == KC - 1), skip_group_check=True)
                last.then_inc(z_ps, 1)

            def pair_of_tiles(i, b):
                u, n, w = 2 * i + b, items(i, b), after(i, b)
                more = not short(u, 0)
                for a in range(4):
                    t, x = a // 2, a % 2
                    scores(u, b, n, True, a)
                    if not zero(u):
                        times_v(n - 1, 0 if isinstance(u, int) and u == 1 else u - 2, a)
                    if more:
                        if a == 0:
                            pe.wait_ge(leveled, 2 * (u + 1))
                            pe.wait_ge(q_ready, 4 * (u + 1) + 2)
                        measure(*w, a, u, False, t, x)
                        measure(*w, a, u + 1, True, t, 1 - x)

                def item(k, pair, before):
                    for a in range(4):
                        scores(u, b, n + k, False, a)
                        times_v(n + k - 1, before, a)
                        if more:
                            measure(*w, 2 * (k + 1) + a // 2, pair, False, a // 2, a % 2)

                def first(k, pair, before):
                    for x in range(2):
                        scores(u, b, n + k, False, x)
                    clear_output(u)
                    for x in range(2):
                        times_v(n + k - 1, before, x)
                        if more:
                            measure(*w, 2 * (k + 1), pair, False, 0, x)
                    turn_y(u - 1)
                    for x in range(2):
                        scores(u, b, n + k, False, 2 + x)
                        times_v(n + k - 1, before, 2 + x)
                        if more:
                            measure(*w, 2 * (k + 1) + 1, pair, False, 1, x)
                if zero(u):
                    clear_output(u)
                others(pe, u, item, first)
                if not zero(u):
                    times_wo(u - 1)
                if not short(u, 0):
                    spread_level(u + 1)

            pe.wait_ge(q_ready, 2)
            for t in range(2):
                for x in range(2):
                    measure(0, 0, t, 0, True, t, x)
            spread_level(0)
            whole(pe, pair_of_tiles)
            for a in range(4):
                times_v(items(PAIRS // 2, 1) - 1, PAIRS - 2, a)
            turn_y(PAIRS - 1)
            times_wo(PAIRS - 1)

        @block.scalar
        def _(act):
            def high(i, b):
                for other, x in ((0, 0), (0, 1), (1, 0), (1, 1)):
                    src = s.qT[64 * x:64 * x + 64, :, bass.ds((2 * i + b) * W, W)]
                    m = x ^ other
                    nc.scalar.activation(q[b][x][m][64 * m:64 * m + 64, :, :], src, ACT.Copy).then_inc(high_ready, 1)

            def level_all(u):
                for x in range(2):
                    act.wait_ge(level_ps, 2 * u + x + 1)
                    nc.scalar.activation(level[x][:, :], psM[x][:, :], ACT.Copy).then_inc(leveled, 1)

            def raise_(n, own):
                for a in range(4):
                    act.wait_ge(s_out[a], n + 1)
                    here = pT[a][:, :, P:W] if own and a >= 2 else pT[a][:, :, :]
                    nc.scalar.activation(here, here, ACT.Exp, scale=SCALE).then_inc(p_ready[a], 1)

            def squares(u):
                act.wait_ge(z_out, u + 1)
                for t in range(2):
                    nc.scalar.activation(square[:, :], s.x2[:, 2 * u + t, :], ACT.Square, accum_out=s.squares[:, bass.ds(2 * u + t, 1)]).then_inc(squared, 1)
                    act.wait_ge(squared, 2 * u + t + 1)

            def copy_y(u):
                act.wait_ge(yT_ps, u + 1)
                if not zero(u):
                    act.wait_ge(z_ps, u)
                nc.scalar.activation(yT[:, :, :].rearrange("p t n -> p (t n)"), psY[:, :], ACT.Copy).then_inc(yT_ready, 1)

            def pair_of_tiles(i, b):
                u, n = 2 * i + b, items(i, b)

                def first(k, pair, before):
                    copy_y(u - 1)
                    raise_(n + k, False)
                raise_(n, True)
                others(act, u, lambda k, pair, before: raise_(n + k, False), first)
                if not short(u, 1):
                    high(i + 1, b)
                if not short(u, 0):
                    level_all(u + 1)
                if not (isinstance(u, int) and u < 2):
                    squares(u - 2)

            high(0, 0)
            high(0, 1)
            level_all(0)
            whole(act, pair_of_tiles)
            squares(PAIRS - 2)
            copy_y(PAIRS - 1)
            squares(PAIRS - 1)

        @block.vector
        def _(dve):
            def largest(i, b, k, pair, own, t, x):
                dve.wait_ge(m_ps[x], 2 * items(i, b) + k + 1)
                nc.vector.tensor_reduce(cand[b][:, x, :, t, bass.ds(pair, 1)].rearrange("p h a -> p (h a)"),
                                        psM[x][:, :].rearrange("p (h n) -> p h n", h=2)[:, :, 0:P if own and t == 0 else W],
                                        AX_X, ALU.max).then_inc(m_out[x], 1)

            def lower(n, own, a):
                x = a % 2
                dve.wait_ge(s_ps[a], n + 1)
                if not zero(n):
                    dve.wait_ge(pv[a], n)
                w = slice(P, W) if own and a >= 2 else slice(0, W)
                if own and a >= 2:
                    nc.vector.memset(pT[a][:, :, 0:P], 0.0)
                part = lambda v: v.rearrange("p (h n) -> p h n", h=2)[:, :, w]
                nc.vector.tensor_tensor(pT[a][:, :, w], part(psS[x][:, :]), part(level[x][:, :]), ALU.subtract).then_inc(s_out[a], 1)

            def settle(i, b):
                u, n = 2 * i + b, items(i, b)
                for x in range(2):
                    dve.wait_ge(m_out[x], 2 * (n + u + 1))
                if not zero(u):
                    dve.wait_ge(drawn, 2 * u)
                nc.vector.tensor_reduce(top[:, :, :].rearrange("p x a -> p (x a)"), cand[b][:, :, :, :, :].rearrange("p x h t a -> p (x h t) a"), AX_X, ALU.max).then_inc(topped, 1)
                dve.wait_ge(topped, u + 1)
                for x in range(2):
                    if not zero(u):
                        dve.wait_ge(level_ps, 2 * u)
                    nc.vector.tensor_tensor(diag[x][:, :, :], s.ident[:, :].unsqueeze(1).to_broadcast([P, 4, P]),
                                            top[:, x, :].unsqueeze(2).to_broadcast([P, 4, P]), ALU.mult).then_inc(drawn, 1)

            def finish(u, n):
                for a in range(4):
                    dve.wait_ge(pv[a], n)
                if not zero(u):
                    dve.wait_ge(o_out, u)
                for t in range(2):
                    o = psO[t][:, 0:4 * (HD + 1)].rearrange("p (h n) -> p h n", n=HD + 1)
                    nc.vector.reciprocal(part[:, t, :], o[:, :, HD]).then_inc(inverted, 1)
                dve.wait_ge(inverted, 2 * (u + 1))
                if not zero(u):
                    dve.wait_ge(yT_ps, u)
                for t in range(2):
                    o = psO[t][:, 0:4 * (HD + 1)].rearrange("p (h n) -> p h n", n=HD + 1)
                    ins = nc.vector.tensor_tensor(y[:, t, :].rearrange("p (h n) -> p h n", n=HD), o[:, :, 0:HD],
                                                  part[:, t, :].unsqueeze(2).to_broadcast([P, 4, HD]), ALU.mult)
                ins.then_inc(o_out, 1)

            def add_z(u):
                dve.wait_ge(z_ps, u + 1)
                here = s.x2[:, bass.ds(2 * u, 2), :].rearrange("p t n -> p (t n)")
                nc.vector.tensor_tensor(here, here, psZ[:, :], ALU.add).then_inc(z_out, 1)

            for v in range(2):
                nc.vector.memset(cand[v][:, :, :, :, :].rearrange("p t x h a -> p (t x h a)"), LOW).then_inc(rounded, 1)
            dve.wait_ge(consts_in, 48)
            nc.vector.tensor_copy(identR[:, :], s.ident[:, :]).then_inc(rounded, 1)
            nc.vector.tensor_scalar(ones[:, :], s.ident[:, :], 0.0, 1.0, ALU.mult, ALU.add).then_inc(rounded, 1)
            nc.vector.tensor_copy(maskR[:, :], mask[:, :]).then_inc(rounded, 1)
            nc.vector.tensor_copy(maskTR[:, :], maskT[:, :]).then_inc(rounded, 1)
            dve.wait_ge(rounded, 6)
            for t in range(2):
                for x in range(2):
                    largest(0, 0, t, 0, True, t, x)
            settle(0, 0)

            def pair_of_tiles(i, b):
                u, n, w = 2 * i + b, items(i, b), after(i, b)
                dve.wait_ge(leveled, 2 * (u + 1))
                more = not short(u, 0)
                for a in range(4):
                    t, x = a // 2, a % 2
                    lower(n, True, a)
                    if more:
                        largest(*w, a, u, False, t, x)
                        largest(*w, a, u + 1, True, t, 1 - x)
                if not zero(u):
                    finish(u - 1, n)

                def item(k, pair, before):
                    for a in range(4):
                        lower(n + k, False, a)
                        if more:
                            largest(*w, 2 * (k + 1) + a // 2, pair, False, a // 2, a % 2)

                others(dve, u, item)
                if not short(u, 0):
                    settle(*w)
                if not zero(u):
                    add_z(u - 1)
            whole(dve, pair_of_tiles)
            finish(PAIRS - 1, items(PAIRS // 2, 1))
            add_z(PAIRS - 1)


def route(nc, d, s):
    with ExitStack() as ctx:
        sb = lambda name, shape, dt=F32: ctx.enter_context(nc.sbuf_tensor(name, shape, dt))
        pb = lambda name: ctx.enter_context(nc.psum_tensor(name, [P, 512], F32))
        sem = lambda name: ctx.enter_context(nc.semaphore(name))
        ln2 = sb("ln2", [P, C])
        routerT = sb("routerT", [P, KC, NE])
        before = sb("before", [P, P])
        all1 = sb("all1", [P, P])
        iota = sb("riota", [P, LIST])
        rrms = sb("rrms", [P, NT])
        flat = [sb(f"flat{b}", [P, C]) for b in range(4)]
        flatT = [sb(f"flatT{b}", [P, C]) for b in range(2)]
        grid = lambda name: sb(name, [P, NT, NE])
        logit, key, one1, one2, both, run, place = (grid(n) for n in ("logit", "key", "one1", "one2", "both", "run", "place"))
        lift = sb("lift", [P, NT, NE + 1])
        m1, m2, i12, den, psum1 = (sb(n, [P, NT]) for n in ("m1", "m2", "i12", "den", "psum1"))
        filled = sb("filled", [P, NE, NT])
        tiles, end, start = (sb(n, [P, NE]) for n in ("tiles", "end", "start"))
        owner = sb("owner", [P, LIST, NE])
        ownerf = sb("ownerf", [P, LIST])
        where = [sb(f"where{b}", [P, 2], U32) for b in range(4)]
        psT, psL = ([pb(f"r{n}{b}") for b in range(2)] for n in ("psT", "psL"))
        psR, psC = pb("rpsR"), pb("rpsC")
        consts_in = sem("rconsts_in")
        meaned = sem("rmeaned")
        rooted = sem("rrooted")
        flat_ready = sem("flat_ready")
        flatT_ps = sem("flatT_ps")
        flatT_ready = sem("flatT_ready")
        logit_ps = sem("logit_ps")
        logit_ready = sem("logit_ready")
        lifted = sem("lifted")
        raised = sem("rraised")
        chosen = sem("chosen")
        counted = sem("counted")
        placed = sem("placed")
        again = sem("again")
        turn = sem("rturn")
        sent = [sem(f"sent{b}") for b in range(4)]
        step = sem("rstep")
        block = ctx.enter_context(nc.Block())

        def lagged(eng, one, two):
            def both(i):
                for b in range(2):
                    one(2 * i + b + 1, 1 - b)
                    two(2 * i + b, b)

            one(0, 0)
            both(0)
            with eng.Fori(1, NT // 2 - 1) as i:
                both(i)
            one(NT - 1, 1)
            for b in range(2):
                two(NT - 2 + b, b)

        @block.sync
        def _(sp):
            for dst, src in ((ln2[:, :], d.ln2[:, :]), (routerT[:, :, :], d.routerT[:, :].rearrange("(k p) n -> p k n", p=P)),
                             (before[:, :], d.before[:, :]), (iota[:, :], d.list[:, :])):
                sp.dma_start(dst, src).then_inc(consts_in, 16)
            for e in range(NE):
                sp.dma_start(s.w13[:, e, :, :], d.w13[e, :, :].rearrange("(k p) n -> p k n", p=P)).then_inc(s.weights_in, 16)
                sp.dma_start(s.w2[:, e, :, :], d.w2[e, :, :].rearrange("(k p) n -> p k n", p=P)).then_inc(s.weights_in, 16)

        @block.gpsimd
        def _(pool):
            pool.wait_ge(placed, 1)

            def body(i, b):
                t = 4 * i + b
                pool.wait_ge(again, t + 1)
                pool.sem_inc(turn, 1)
                for k in range(2):
                    pool.indirect_dma_start(d.list_x[:, :], bass.IndirectOffsetOnAxis(where[b][:, k:k + 1], 0),
                                            flat[b][:, :], None, bounds_check=LIST * P - 1, oob_is_err=False).then_inc(sent[b], 16)

            fours(pool, body)
            for b in range(4):
                pool.wait_ge(sent[b], 32 * (NT // 4 + (b < NT % 4)))

        @block.scalar
        def _(act):
            act.wait_ge(meaned, 1)
            nc.scalar.activation(rrms[:, :], rrms[:, :], ACT.Sqrt).then_inc(rooted, 1)

            def copy_x(t, b):
                act.wait_ge(flatT_ps, t + 1)
                if not isinstance(t, int) or t >= 2:
                    act.wait_ge(logit_ps, t - 1)
                nc.scalar.activation(flatT[b][:, :], psT[b][:, 0:C], ACT.Copy).then_inc(flatT_ready, 1)

            def copy_logit(t, b):
                act.wait_ge(logit_ps, t + 1)
                nc.scalar.activation(logit[:, t, :], psL[b][:, 0:NE], ACT.Copy).then_inc(logit_ready, 1)

            lagged(act, copy_x, copy_logit)
            act.wait_ge(lifted, 1)
            nc.scalar.activation(lift[:, :, :], lift[:, :, :], ACT.Exp).then_inc(raised, 1)

        @block.tensor
        def _(pe):
            pe.wait_ge(consts_in, 64)

            def turn_x(t, b):
                pe.wait_ge(flat_ready, t + 1)
                if not isinstance(t, int) or t >= 2:
                    pe.wait_ge(flatT_ready, t - 1)
                for k in range(KC):
                    last = nc.tensor.transpose(psT[b][:, k * P:(k + 1) * P], flat[b][:, k * P:(k + 1) * P], s.ident[:, :])
                last.then_inc(flatT_ps, 1)

            def logits(t, b):
                pe.wait_ge(flatT_ready, t + 1)
                if not isinstance(t, int) or t >= 2:
                    pe.wait_ge(logit_ready, t - 1)
                for k in range(KC):
                    last = nc.tensor.matmul(psL[b][:, 0:NE], flatT[b][:, k * P:(k + 1) * P], routerT[:, k, :], start=(k == 0), stop=(k == KC - 1))
                last.then_inc(logit_ps, 1)

            lagged(pe, turn_x, logits)
            pe.wait_ge(chosen, 1)
            m = both[:, :, :].rearrange("p t e -> p (t e)")
            nc.tensor.matmul(psR[:, 0:NT * NE], before[:, :], m, start=True, stop=True)
            nc.tensor.matmul(psC[:, 0:NT * NE], all1[:, :], m, start=True, stop=True).then_inc(counted, 1)

        @block.vector
        def _(dve):
            at = [0]

            def link(ins):
                at[0] += 1
                ins.then_inc(step, 1)
                dve.wait_ge(step, at[0])

            tt = lambda out, a, b, op: link(nc.vector.tensor_tensor(out, a, b, op))
            nc.vector.memset(all1[:, :], 1.0)
            nc.vector.tensor_scalar(rrms[:, :], s.squares[:, :], 1.0 / C, EPS_RMS, ALU.mult, ALU.add).then_inc(meaned, 1)
            dve.wait_ge(rooted, 1)
            link(nc.vector.reciprocal(rrms[:, :], rrms[:, :]))
            dve.wait_ge(consts_in, 64)

            def normal(t, b, done):
                if done is flat_ready:
                    nc.vector.tensor_tensor(s.x1[:, t, :], s.x1[:, t, :], s.x2[:, t, :], ALU.add)
                else:
                    nc.vector.tensor_copy(where[b][:, :], s.where[:, t, :])
                nc.vector.scalar_tensor_tensor(flat[b][:, :], s.x2[:, t, :], rrms[:, bass.ds(t, 1)], ln2[:, :],
                                               ALU.mult, ALU.mult).then_inc(done, 1)

            for b in range(2):
                normal(b, b, flat_ready)
            with dve.Fori(1, NT // 2) as i:
                for b in range(2):
                    dve.wait_ge(flatT_ps, 2 * i + b - 1)
                    normal(2 * i + b, b, flat_ready)
            dve.wait_ge(logit_ready, NT)

            each = lambda a: a.unsqueeze(2).to_broadcast([P, NT, NE])
            number = iota[:, 0:NE].unsqueeze(1).to_broadcast([P, NT, NE])

            def choose(one, m, logits):
                link(nc.vector.tensor_reduce(m[:, :], logits, AX_X, ALU.max))
                tt(key[:, :, :], logits, each(m[:, :]), ALU.is_lt)
                link(nc.vector.scalar_tensor_tensor(key[:, :, :], key[:, :, :], float(NE), number, ALU.mult, ALU.add))
                link(nc.vector.tensor_reduce(i12[:, :], key[:, :, :], AX_X, ALU.min))
                tt(one, number, each(i12[:, :]), ALU.is_equal)

            choose(one1[:, :, :], m1, logit[:, :, :])
            link(nc.vector.scalar_tensor_tensor(run[:, :, :], one1[:, :, :], LOW, logit[:, :, :], ALU.mult, ALU.add))
            choose(one2[:, :, :], m2, run[:, :, :])
            tt(lift[:, :, 0:NE], logit[:, :, :], each(m1[:, :]), ALU.subtract)
            nc.vector.tensor_tensor(lift[:, :, NE], m2[:, :], m1[:, :], ALU.subtract).then_inc(lifted, 1)
            nc.vector.tensor_tensor(both[:, :, :], one1[:, :, :], one2[:, :, :], ALU.add).then_inc(chosen, 1)
            dve.wait_ge(raised, 1)
            link(nc.vector.tensor_reduce(psum1[:, :], lift[:, :, 0:NE], AX_X, ALU.add))
            link(nc.vector.reciprocal(psum1[:, :], psum1[:, :]))
            tt(m2[:, :], lift[:, :, NE], psum1[:, :], ALU.mult)
            tt(den[:, :], psum1[:, :], m2[:, :], ALU.add)
            link(nc.vector.tensor_scalar(den[:, :], den[:, :], 1e-9, None, ALU.add))
            link(nc.vector.reciprocal(den[:, :], den[:, :]))
            tt(s.share[:, :, 0], psum1[:, :], den[:, :], ALU.mult)
            tt(s.share[:, :, 1], m2[:, :], den[:, :], ALU.mult)
            dve.wait_ge(counted, 1)
            count = psC[:, 0:NT * NE].rearrange("p (t e) -> p t e", e=NE)
            link(nc.vector.tensor_copy(key[:, :, :], count))
            for e in range(NE):
                link(nc.vector.tensor_tensor_scan(run[:, :, e], key[:, :, e], key[:, :, e], 0.0, ALU.add, ALU.max))
            link(nc.vector.tensor_scalar(m1[:, :], iota[:, 0:NT], float(P), None, ALU.mult))
            tt(filled[:, :, :], run[:, NT - 1, :].unsqueeze(2).to_broadcast([P, NE, NT]),
               m1[:, :].unsqueeze(1).to_broadcast([P, NE, NT]), ALU.is_gt)
            link(nc.vector.tensor_reduce(tiles[:, :], filled[:, :, :], AX_X, ALU.add))
            link(nc.vector.tensor_tensor_scan(end[:, :], tiles[:, :], tiles[:, :], 0.0, ALU.add, ALU.max))
            tt(start[:, :], end[:, :], tiles[:, :], ALU.subtract)
            link(nc.vector.tensor_scalar(start[:, :], start[:, :], float(P), None, ALU.mult))
            tt(place[:, :, :], run[:, :, :], key[:, :, :], ALU.subtract)
            tt(place[:, :, :], place[:, :, :], start[:, :].unsqueeze(1).to_broadcast([P, NT, NE]), ALU.add)
            tt(place[:, :, :], place[:, :, :], psR[:, 0:NT * NE].rearrange("p (t e) -> p t e", e=NE), ALU.add)
            for n, one in enumerate((one1, one2)):
                tt(one[:, :, :], one[:, :, :], place[:, :, :], ALU.mult)
                link(nc.vector.tensor_reduce(i12[:, :], one[:, :, :], AX_X, ALU.add))
                link(nc.vector.tensor_copy(s.where[:, :, n], i12[:, :]))
            dve.sem_inc(placed, 1)
            tt(owner[:, :, :], iota[:, :].unsqueeze(2).to_broadcast([P, LIST, NE]),
               end[:, :].unsqueeze(1).to_broadcast([P, LIST, NE]), ALU.is_ge)
            link(nc.vector.tensor_reduce(ownerf[:, :], owner[:, :, :], AX_X, ALU.add))
            link(nc.vector.tensor_scalar(s.owner[:, :], ownerf[:, :], float(NE - 1), None, ALU.min))

            def once_more(i, b):
                if not zero(i):
                    dve.wait_ge(sent[b], 32 * i)
                normal(4 * i + b, b, again)
            fours(dve, once_more)


def experts(nc, d, s):
    with ExitStack() as ctx:
        sb = lambda name, shape, dt=F32: ctx.enter_context(nc.sbuf_tensor(name, shape, dt))
        pb = lambda name: ctx.enter_context(nc.psum_tensor(name, [P, 512], F32))
        sem = lambda name: ctx.enter_context(nc.semaphore(name))
        xs = [sb(f"xs{b}", [P, C]) for b in range(2)]
        xT = sb("exT", [P, C])
        gate = [sb(f"gate{z}", [P, HH]) for z in range(2)]
        h = sb("h", [P, KH * P])
        hT = sb("hidT", [P, KH * P])
        ys = [sb(f"ys{b}", [P, C]) for b in range(2)]
        psA = [pb(f"epsA{z}") for z in range(2)]
        psB = [pb(f"epsB{z}") for z in range(2)]
        psT, psY = pb("epsT"), pb("epsY")
        psH = [pb(f"epsH{z}") for z in range(2)]
        x_in = [sem(f"ex_in{b}") for b in range(2)]
        x_ps = sem("ex_ps")
        x_ready = sem("ex_ready")
        up = [sem(f"up{z}") for z in range(2)]
        gated = [sem(f"gated{z}") for z in range(2)]
        h_ready = [sem(f"h_ready{z}") for z in range(2)]
        h_ps = [sem(f"h_ps{z}") for z in range(2)]
        hT_ready = [sem(f"ehT{z}") for z in range(2)]
        y_ps = sem("ey_ps")
        y_ready = sem("ey_ready")
        y_out = [sem(f"ey_out{b}") for b in range(2)]
        block = ctx.enter_context(nc.Block())
        T3 = KH // 2 * P

        def pairs(eng, body):
            for b in range(2):
                body(b, b)
            with eng.Fori(1, LIST // 2) as i:
                for b in range(2):
                    body(2 * i + b, b)

        @block.sync
        def _(sp):
            for b in range(2):
                sp.dma_start(xs[b][:, :], d.list_x[b * P:(b + 1) * P, :]).then_inc(x_in[b], 16)
            with sp.Fori(1, LIST // 2) as i:
                for b in range(2):
                    sp.wait_ge(x_ps, 2 * i + b - 1)
                    sp.dma_start(xs[b][:, :], d.list_x[bass.ds(i * (2 * P) + b * P, P), :]).then_inc(x_in[b], 16)

        @block.gpsimd
        def _(pool):
            def body(n, b):
                pool.wait_ge(y_ready, n + 1)
                pool.sem_inc(s.turn, 1)
                pool.dma_start(d.list_y[bass.ds(n * P, P), :], ys[b][:, :]).then_inc(y_out[b], 16)
            pairs(pool, body)
            for b in range(2):
                pool.wait_ge(y_out[b], 16 * (LIST // 2))

        @block.tensor
        def _(pe):
            pe.wait_ge(s.weights_in, 32 * NE)

            def turn_x(n, b, i):
                pe.wait_ge(x_in[b], 16 * (i + 1))
                for k in range(KC):
                    last = nc.tensor.transpose(psT[:, k * P:(k + 1) * P], xs[b][:, k * P:(k + 1) * P], s.ident[:, :])
                last.then_inc(x_ps, 1)

            def turn_h(n):
                for z in range(2):
                    for w in range(2):
                        pe.wait_ge(h_ready[w], n + 1)
                    if not zero(n):
                        pe.wait_ge(hT_ready[z], n)
                    for k in range(KH // 2):
                        o = z * T3 + k * P
                        last = nc.tensor.transpose(psH[z][:, k * P:(k + 1) * P], h[:, o:o + P], s.ident[:, :])
                    last.then_inc(h_ps[z], 1)

            def ups(n, e):
                pe.wait_ge(x_ready, n + 1)
                for z in range(2):
                    if not zero(n):
                        pe.wait_ge(h_ready[z], n)
                    for ps, off in ((psA[z], 0), (psB[z], HID)):
                        for k in range(KC):
                            last = nc.tensor.matmul(ps[:, 0:HH], xT[:, k * P:(k + 1) * P],
                                                    s.w13[:, bass.ds(e, 1), k, off + z * HH:off + (z + 1) * HH].rearrange("p a n -> p (a n)"),
                                                    start=(k == 0), stop=(k == KC - 1))
                    last.then_inc(up[z], 1)

            def down(n, e):
                if not zero(n):
                    pe.wait_ge(y_ready, n)
                for k in range(KH):
                    if k % (KH // 2) == 0:
                        pe.wait_ge(hT_ready[k // (KH // 2)], n + 1)
                    last = nc.tensor.matmul(psY[:, 0:C], hT[:, k * P:(k + 1) * P],
                                            s.w2[:, bass.ds(e, 1), k, :].rearrange("p a n -> p (a n)"),
                                            start=(k == 0), stop=(k == KH - 1))
                last.then_inc(y_ps, 1)

            def expert(n):
                return pe.value_load(s.owner[0:1, bass.ds(n, 1)], min_val=0, max_val=NE - 1)

            turn_x(0, 0, 0)
            ups(0, expert(0))
            turn_x(1, 1, 0)
            turn_h(0)
            ups(1, expert(1))
            down(0, expert(0))
            with pe.Fori(1, LIST // 2) as i:
                for b in range(2):
                    n = 2 * i + b
                    turn_x(n, b, i)
                    turn_h(n - 1)
                    ups(n, expert(n))
                    down(n - 1, expert(n - 1))
            turn_h(LIST - 1)
            down(LIST - 1, expert(LIST - 1))

        @block.scalar
        def _(act):
            def body(n, b):
                act.wait_ge(x_ps, n + 1)
                if not zero(n):
                    act.wait_ge(up[1], n)
                nc.scalar.activation(xT[:, :], psT[:, 0:C], ACT.Copy).then_inc(x_ready, 1)
                if not zero(n):
                    copy_h(n - 1)
                for z in range(2):
                    act.wait_ge(up[z], n + 1)
                    if not zero(n):
                        act.wait_ge(h_ready[z], n)
                    nc.scalar.activation(gate[z][:, :], psA[z][:, 0:HH], ACT.Silu).then_inc(gated[z], 1)

            def copy_h(n):
                act.wait_ge(h_ps[0], n + 1)
                if not zero(n):
                    act.wait_ge(y_ps, n)
                nc.scalar.activation(hT[:, 0:T3], psH[0][:, 0:T3], ACT.Copy).then_inc(hT_ready[0], 1)

            pairs(act, body)
            copy_h(LIST - 1)

        @block.vector
        def _(dve):
            nc.vector.memset(h[:, HID:KH * P], 0.0)

            def copy_h(n):
                dve.wait_ge(h_ps[1], n + 1)
                if not zero(n):
                    dve.wait_ge(y_ps, n)
                nc.vector.tensor_copy(hT[:, T3:2 * T3], psH[1][:, 0:T3]).then_inc(hT_ready[1], 1)

            def copy_y(n, b, i):
                dve.wait_ge(y_ps, n + 1)
                if not zero(i):
                    dve.wait_ge(y_out[b], 16 * i)
                nc.vector.tensor_copy(ys[b][:, :], psY[:, 0:C]).then_inc(y_ready, 1)

            def hidden(n):
                for z in range(2):
                    dve.wait_ge(gated[z], n + 1)
                    if not zero(n):
                        dve.wait_ge(h_ps[1], n)
                    nc.vector.tensor_tensor(h[:, z * HH:(z + 1) * HH], gate[z][:, :], psB[z][:, 0:HH], ALU.mult).then_inc(h_ready[z], 1)

            hidden(0)
            copy_h(0)
            hidden(1)
            copy_y(0, 0, 0)

            def both(i):
                copy_h(2 * i - 1)
                hidden(2 * i)
                copy_y(2 * i - 1, 1, i - 1)
                copy_h(2 * i)
                hidden(2 * i + 1)
                copy_y(2 * i, 0, i)
            rounds(dve, both, LIST // 2)
            copy_h(LIST - 1)
            copy_y(LIST - 1, 1, LIST // 2 - 1)


def finish(nc, d, s):
    with ExitStack() as ctx:
        sb = lambda name, shape, dt=F32: ctx.enter_context(nc.sbuf_tensor(name, shape, dt))
        sem = lambda name: ctx.enter_context(nc.semaphore(name))
        got = [[sb(f"got{b}{k}", [P, C]) for k in range(2)] for b in range(4)]
        where = [sb(f"fwhere{b}", [P, 2], U32) for b in range(4)]
        out = [sb(f"out{b}", [P, C]) for b in range(4)]
        named = sem("fnamed")
        fetched = [sem(f"fetched{b}") for b in range(4)]
        added = sem("added")
        ready = sem("fready")
        out_sent = [sem(f"out_sent{b}") for b in range(4)]
        block = ctx.enter_context(nc.Block())
        @block.gpsimd
        def _(pool):
            def body(i, b):
                t = 4 * i + b
                if not zero(i):
                    pool.wait_ge(ready, t - 3)
                    pool.sem_inc(s.turn, 1)
                pool.wait_ge(named, t + 1)
                pool.sem_inc(s.turn, 1)
                for k in range(2):
                    pool.indirect_dma_start(got[b][k][:, :], None, d.list_y[:, :],
                                            bass.IndirectOffsetOnAxis(where[b][:, k:k + 1], 0),
                                            bounds_check=LIST * P - 1, oob_is_err=False).then_inc(fetched[b], 16)
            fours(pool, body)

        @block.scalar
        def _(act):
            def body(i, b):
                if not zero(i):
                    act.wait_ge(fetched[b], 32 * i)
                nc.scalar.activation(where[b][:, :], s.where[:, 4 * i + b, :], ACT.Copy).then_inc(named, 1)
            fours(act, body)

        @block.vector
        def _(dve):
            def body(i, b):
                t = 4 * i + b
                dve.wait_ge(fetched[b], 32 * (i + 1))
                if not zero(i):
                    dve.wait_ge(out_sent[b], 16 * i)
                nc.vector.scalar_tensor_tensor(got[b][0][:, :], got[b][0][:, :], s.share[:, t, 0:1], s.x1[:, t, :],
                                               ALU.mult, ALU.add).then_inc(added, 1)
                dve.wait_ge(added, t + 1)
                nc.vector.scalar_tensor_tensor(out[b][:, :], got[b][1][:, :], s.share[:, t, 1:2], got[b][0][:, :],
                                               ALU.mult, ALU.add).then_inc(ready, 1)
            fours(dve, body)

        @block.sync
        def _(sp):
            def body(i, b):
                t = 4 * i + b
                sp.wait_ge(ready, t + 1)
                sp.dma_start(d.out[bass.ds(i * (4 * P) + b * P, P), :], out[b][:, :]).then_inc(out_sent[b], 16)
            fours(sp, body)
            for b in range(4):
                sp.wait_ge(out_sent[b], 16 * (NT // 4 + (b < NT % 4)))


class Named:
    pass


def build(nc, d):
    with ExitStack() as ctx:
        sb = lambda name, shape, dt=F32: ctx.enter_context(nc.sbuf_tensor(name, shape, dt))
        s = Named()
        s.ident = sb("ident", [P, P])
        s.x1 = sb("x1", [P, NT, C])
        s.stats = sb("rowstats", [P, NT, 6])
        s.squares = sb("squares", [P, NT])
        s.where = sb("where", [P, NT, 2], U32)
        s.share = sb("share", [P, NT, 2])
        s.owner = sb("owners", [P, LIST], I32)
        s.weights_in = ctx.enter_context(nc.semaphore("expert_weights_in"))
        s.turn = ctx.enter_context(nc.semaphore("store_turn"))
        s.crowded = sb("crowded", [P, 1], I32)
        with ExitStack() as inner:
            sbi = lambda name, shape, dt=F32: inner.enter_context(nc.sbuf_tensor(name, shape, dt))
            s.rows = [sbi(f"rows{b}", [P, SLOTS, ROW]) for b in range(3)]
            s.base_out = ctx.enter_context(nc.semaphore("base_out"))
            s.adj = [sbi(f"adj{b}", [P, NP]) for b in range(3)]
            s.adj_in = [ctx.enter_context(nc.semaphore(f"adj_in{b}")) for b in range(3)]
            s.ssrc = sbi("ssrc", [P, NT, GH])
            s.we = sbi("we", [P, GH])
            table(nc, d, s)
            entries(nc, d, s)
            general(nc, d, s)
        s.x2 = sb("x2", [P, NT, C])
        with ExitStack() as inner:
            sbi = lambda name, shape, dt=F32: inner.enter_context(nc.sbuf_tensor(name, shape, dt))
            s.qT = sbi("qT", [P, 2, NP])
            s.kT = [sbi(f"kT{x}", [P, NP], F32R) for x in range(2)]
            s.v = sbi("v", [P, NT, 2, HD + 1])
            qkv(nc, d, s)
            attend(nc, d, s)
        s.w13 = sb("w13", [P, NE, KC, 2 * HID])
        s.w2 = sb("w2", [P, NE, KH, C])
        route(nc, d, s)
        experts(nc, d, s)
        finish(nc, d, s)


def kernel(x, adj, **w):
    import concourse.bacc as bacc
    from concourse.bass_utils import run_bass_kernel_spmd

    w = {k[3:]: np.asarray(v) for k, v in w.items()}
    x, adj = np.asarray(x), np.asarray(adj)

    xp = np.zeros((NP, C), np.float32)
    xp[:N] = x
    ap = np.zeros((NP, NP), np.float32)
    ap[:N, :N] = adj
    ap[np.arange(N, NP), np.arange(N, NP)] = 1.0
    ablk = np.zeros((C, 2 * GH), np.float32)
    for h in range(GH):
        ablk[h * GD:(h + 1) * GD, h] = w["gnn_a_dst"][h]
        ablk[h * GD:(h + 1) * GD, GH + h] = w["gnn_a_src"][h]
    wide = lambda v: np.ascontiguousarray(np.broadcast_to(v.reshape(1, -1), (P, v.size)))
    arrays = {
        "x": xp, "adj": ap, "w": w["gnn_W"], "wT": w["gnn_W"].T, "wrT": w["gnn_Wr"].T, "ablk": ablk,
        "br": wide(w["gnn_br"]), "be": wide(w["gnn_be"]), "we": wide(w["gnn_We"]),
        "ident": np.eye(P, dtype=np.float32),
        "iota": wide(np.arange(CAND, dtype=np.float32)),
        "qoff": wide((np.arange(CAND) // 8 * QW).astype(np.float32)),
    }
    order = (0, 2, 1, 3)
    wq = w["ffn_wq"].reshape(4, HD, C)[list(order)].reshape(C, C)
    arrays["wqkvT"] = np.concatenate([wq, w["ffn_wk"], w["ffn_wv"]]).T
    arrays["woT"] = w["ffn_wo"].reshape(C, 4, HD)[:, list(order)].reshape(C, C).T
    arrays["ln1"] = wide(w["ffn_ln1_w"])
    freq = np.outer(np.arange(NP, dtype=np.float32), 1.0 / 10000.0 ** (np.arange(0, HD, 2, dtype=np.float32) / HD))
    emb = np.concatenate([freq, freq], axis=-1)
    arrays["cos"] = np.cos(emb).astype(np.float32)
    arrays["sin"] = (np.sin(emb) * np.where(np.arange(HD) < HD // 2, -1, 1)).astype(np.float32)
    causal = np.where(np.arange(P)[None, :] <= np.arange(P)[:, None], 0.0, LOW).astype(np.float32)
    arrays["mask"], arrays["maskT"] = causal, causal.T
    arrays["ln2"] = wide(w["ffn_ln2_w"])
    arrays["routerT"] = w["ffn_router_w"].T
    arrays["before"] = np.triu(np.ones((P, P), np.float32), 1)
    arrays["list"] = wide(np.arange(LIST, dtype=np.float32))
    arrays["w13"] = np.concatenate([w["ffn_w1"], w["ffn_w3"]], axis=1).transpose(0, 2, 1)
    arrays["w2"] = np.zeros((NE, KH * P, C), np.float32)
    arrays["w2"][:, :HID] = w["ffn_w2"].transpose(0, 2, 1)
    arrays = {k: np.ascontiguousarray(v) for k, v in arrays.items()}
    nc = bacc.Bacc("TRN2", target_bir_lowering=False, num_devices=1)
    d = Named()
    for name, a in arrays.items():
        setattr(d, name, nc.dram_tensor(f"in_{name}", a.shape, mybir.dt.from_np(a.dtype), kind="ExternalInput").ap())
    d.table = nc.dram_tensor("table", (NP, ROW), F32, kind="Internal").ap()
    d.base = nc.dram_tensor("base", (NP, C), F32, kind="Internal").ap()
    d.list_x = nc.dram_tensor("list_x", (LIST * P, C), F32, kind="Internal").ap()
    d.list_y = nc.dram_tensor("list_y", (LIST * P, C), F32, kind="Internal").ap()
    d.out = nc.dram_tensor("out", (NP, C), F32, kind="ExternalOutput").ap()
    build(nc, d)
    r = run_bass_kernel_spmd(nc, [{f"in_{k}": v for k, v in arrays.items()}], core_ids=[0])
    return r.results[0]["out"][:N]
```
